# Optimizing a Trainium2 kernel written in Bass

```python
import numpy as np
import jax
import jax.numpy as jnp

def _softmax(x, axis=-1):
    return jax.nn.softmax(x, axis=axis)

def _gelu(x):
    return jax.nn.gelu(x, approximate=True)

def _silu(x):
    return jax.nn.silu(x)

def _sigmoid(x):
    return jax.nn.sigmoid(x)

def _layernorm(x, axis=-1, eps=1e-05):
    m = jnp.mean(x, axis=axis, keepdims=True)
    v = jnp.var(x, axis=axis, keepdims=True)
    return (x - m) / jnp.sqrt(v + eps)

def _scatter_add(tgt, idx, src, axis=0):
    return tgt.at[idx].add(src)

def _segment_sum(src, seg, n):
    return jax.ops.segment_sum(src, seg, n)
kernel_name = 'mk_flamingo_gated_d2_seqx_r8_eec3c5'

def setup_inputs(seed: int=0):
    np.random.seed(seed)
    _w = jnp.asarray

    def _rec_inputs():
        import jax
        import jax.numpy as jnp
        _rk = jax.random.key(seed)
        x = -0.0005207 + 1.001 * jax.random.normal(jax.random.fold_in(_rk, 1), (64, 64, 256), jnp.float32)
        _lenS = 64 - jax.random.randint(jax.random.fold_in(_rk, 7), (64,), 0, max(1, 64 // 4) + 1, jnp.int32)
        _lenS2 = 64 - jax.random.randint(jax.random.fold_in(_rk, 8), (64,), 0, max(1, 64 // 4) + 1, jnp.int32)
        _ctx_2048P = jax.random.normal(jax.random.fold_in(_rk, 12), (64, 16, 256), jnp.float32)
        _ctx_2048c = jax.random.dirichlet(jax.random.fold_in(_rk, 512), 0.3 * jnp.ones((16,), jnp.float32), (64, 64))
        _ctx_2048t = jnp.einsum('bsk,bkd->bsd', _ctx_2048c, _ctx_2048P)
        _ctx_2048t = _ctx_2048t * jax.lax.rsqrt(jnp.mean(jnp.square(_ctx_2048t)) + 1e-12) * 0.953939
        ctx_2048 = -5.72187e-05 + 0.999849 * (_ctx_2048t + 0.3 * jax.random.normal(jax.random.fold_in(_rk, 612), (64, 64, 256), jnp.float32))
        _validS = jnp.arange(64)[None, :] < _lenS[:, None]
        _validS2 = jnp.arange(64)[None, :] < _lenS2[:, None]
        _causal = jnp.tril(jnp.ones((64, 64), dtype=bool))
        mask_BxSx4224_bf0 = jnp.logical_not(jnp.ones((64, 64, 528), dtype=bool))
        _g = jax.random.normal(jax.random.fold_in(_rk, 9001), (2, 2), jnp.float32)
        _g = jnp.sign(_g) * jnp.maximum(jnp.abs(_g), 1.0) + (_g == 0) * 1.0
        g_xattn = _g[0]
        g_ffn = _g[1]
        return (x, ctx_2048, mask_BxSx4224_bf0, g_xattn, g_ffn)
    x, ctx_2048, mask_BxSx4224_bf0, g_xattn, g_ffn = _rec_inputs()

    def _L0_xattn_setup():
        import jax, jax.numpy as jnp
        import numpy as np
        import math
        DIM = 256
        B, Q_LEN, KV_LEN = (8, 128, 512)
        key = jax.random.key(seed)
        ks = jax.random.split(key, 8)
        x = jax.random.normal(ks[0], (B, Q_LEN, DIM), dtype=jnp.float32)
        mask = jnp.zeros((B, Q_LEN, KV_LEN + Q_LEN), dtype=bool)
        k_cache = jax.random.normal(ks[1], (B, KV_LEN, DIM), dtype=jnp.float32)
        v_cache = jax.random.normal(ks[2], (B, KV_LEN, DIM), dtype=jnp.float32)
        scale = 1.0 / math.sqrt(DIM)
        wq = jax.random.normal(ks[3], (DIM, DIM), dtype=jnp.float32) * scale
        wk = jax.random.normal(ks[4], (DIM, DIM), dtype=jnp.float32) * scale
        wv = jax.random.normal(ks[5], (DIM, DIM), dtype=jnp.float32) * scale
        wo = jax.random.normal(ks[6], (DIM, DIM), dtype=jnp.float32) * scale
        return {'x': x, 'mask': mask, 'k_cache': k_cache, 'v_cache': v_cache, 'wq': wq, 'wk': wk, 'wv': wv, 'wo': wo}
    _L0_xattn_all = _L0_xattn_setup()
    _L0_xattn_in = {k: v for k, v in _L0_xattn_all.items() if k in ('wq', 'wk', 'wv', 'wo')}
    del _L0_xattn_all

    def _L0_ffn_setup():
        import jax, jax.numpy as jnp
        import numpy as np
        D_MODEL = 256
        HIDDEN = int(2 * D_MODEL * 4 / 3)

        def ternary_quant(w):
            s = jnp.mean(jnp.abs(w))
            q = jnp.clip(jnp.round(w / s), -1.0, 1.0) * s
            return w + jax.lax.stop_gradient(q - w)
        key = jax.random.key(seed)
        k0, k1, k2, k3 = jax.random.split(key, 4)
        x = jax.random.normal(k0, (4, 512, D_MODEL), dtype=jnp.float32)
        std_in = 1.0 / np.sqrt(D_MODEL)
        std_h = 1.0 / np.sqrt(HIDDEN)
        w1 = jax.random.uniform(k1, (HIDDEN, D_MODEL), jnp.float32, -std_in, std_in)
        w3 = jax.random.uniform(k2, (HIDDEN, D_MODEL), jnp.float32, -std_in, std_in)
        w2 = jax.random.uniform(k3, (D_MODEL, HIDDEN), jnp.float32, -std_h, std_h)
        return {'x': x, 'w1': w1, 'w3': w3, 'w2': w2}
    _L0_ffn_all = _L0_ffn_setup()
    _L0_ffn_in = {k: v for k, v in _L0_ffn_all.items() if k in ('w1', 'w3', 'w2')}
    del _L0_ffn_all

    def _L1_xattn_setup():
        import jax, jax.numpy as jnp
        import numpy as np
        B_DIM, T_DIM, C_DIM = (16, 128, 256)

        def _wkv(w, u, k, v):
            Bn, Tn, Cn = k.shape
            NEG_INF = jnp.float32(-1e+38)

            def step(carry, kv_t):
                p, q, o = carry
                kt, vt = kv_t
                no = jnp.maximum(o, u + kt)
                A = jnp.exp(o - no)
                E = jnp.exp(u + kt - no)
                y = (A * p + E * vt) / (A * q + E)
                no2 = jnp.maximum(w + o, kt)
                A2 = jnp.exp(w + o - no2)
                E2 = jnp.exp(kt - no2)
                return ((A2 * p + E2 * vt, A2 * q + E2, no2), y)
            init = (jnp.zeros((Bn, Cn), k.dtype), jnp.zeros((Bn, Cn), k.dtype), jnp.full((Bn, Cn), NEG_INF, k.dtype))
            kT = jnp.moveaxis(k, 1, 0)
            vT = jnp.moveaxis(v, 1, 0)
            _, yT = jax.lax.scan(step, init, (kT, vT))
            return jnp.moveaxis(yT, 0, 1)
        key = jax.random.key(seed)
        k1, k2, k3, k4 = jax.random.split(key, 4)
        w = -jnp.exp(jax.random.normal(k1, (C_DIM,), jnp.float32))
        u = jax.random.normal(k2, (C_DIM,), jnp.float32)
        k = jax.random.normal(k3, (B_DIM, T_DIM, C_DIM), jnp.float32)
        v = jax.random.normal(k4, (B_DIM, T_DIM, C_DIM), jnp.float32)
        return {'B': B_DIM, 'T': T_DIM, 'C': C_DIM, 'w': w, 'u': u, 'k': k, 'v': v}
    _L1_xattn_all = _L1_xattn_setup()
    _L1_xattn_in = {k: v for k, v in _L1_xattn_all.items() if k in ('w', 'u')}
    del _L1_xattn_all

    def _L1_ffn_setup():
        import jax, jax.numpy as jnp
        import numpy as np
        E = 8
        TOP_K = 2
        D = 256
        F = 128
        FS = 256
        B, T = (2, 128)
        key = jax.random.key(seed)
        ks = jax.random.split(key, 8)
        s = 0.02
        return {'x': jax.random.normal(ks[0], (B, T, D), dtype=jnp.float32), 'router_w': jax.random.normal(ks[1], (D, E), dtype=jnp.float32) * s, 'shared_gate': jax.random.normal(ks[2], (D, FS), dtype=jnp.float32) * s, 'shared_up': jax.random.normal(ks[3], (D, FS), dtype=jnp.float32) * s, 'shared_down': jax.random.normal(ks[4], (FS, D), dtype=jnp.float32) * s, 'w_gate': jax.random.normal(ks[5], (E, D, F), dtype=jnp.float32) * s, 'w_up': jax.random.normal(ks[6], (E, D, F), dtype=jnp.float32) * s, 'w_down': jax.random.normal(ks[7], (E, F, D), dtype=jnp.float32) * s}
    _L1_ffn_all = _L1_ffn_setup()
    _L1_ffn_in = {k: v for k, v in _L1_ffn_all.items() if k in ('router_w', 'shared_gate', 'shared_up', 'shared_down', 'w_gate', 'w_up', 'w_down')}
    del _L1_ffn_all
    return {'x': x, 'ctx_2048': ctx_2048, 'mask_BxSx4224_bf0': mask_BxSx4224_bf0, 'g_xattn': g_xattn, 'g_ffn': g_ffn, 'L0_xattn_wq': _L0_xattn_in['wq'], 'L0_xattn_wk': _L0_xattn_in['wk'], 'L0_xattn_wv': _L0_xattn_in['wv'], 'L0_xattn_wo': _L0_xattn_in['wo'], 'L0_ffn_w1': _L0_ffn_in['w1'], 'L0_ffn_w3': _L0_ffn_in['w3'], 'L0_ffn_w2': _L0_ffn_in['w2'], 'L1_xattn_w': _L1_xattn_in['w'], 'L1_xattn_u': _L1_xattn_in['u'], 'L1_ffn_router_w': _L1_ffn_in['router_w'], 'L1_ffn_shared_gate': _L1_ffn_in['shared_gate'], 'L1_ffn_shared_up': _L1_ffn_in['shared_up'], 'L1_ffn_shared_down': _L1_ffn_in['shared_down'], 'L1_ffn_w_gate': _L1_ffn_in['w_gate'], 'L1_ffn_w_up': _L1_ffn_in['w_up'], 'L1_ffn_w_down': _L1_ffn_in['w_down']}

def reference(x, ctx_2048, mask_BxSx4224_bf0, g_xattn, g_ffn, L0_xattn_wq, L0_xattn_wk, L0_xattn_wv, L0_xattn_wo, L0_ffn_w1, L0_ffn_w3, L0_ffn_w2, L1_xattn_w, L1_xattn_u, L1_ffn_router_w, L1_ffn_shared_gate, L1_ffn_shared_up, L1_ffn_shared_down, L1_ffn_w_gate, L1_ffn_w_up, L1_ffn_w_down):
    import jax
    import jax.numpy as jnp

    def _L0_xattn_ref(x, mask, k_cache, v_cache, wq, wk, wv, wo):
        import jax, jax.numpy as jnp
        import numpy as np
        import math
        DIM = 256
        B, Q_LEN, KV_LEN = (8, 128, 512)
        q = jnp.einsum('bsd,ed->bse', x, wq)
        k_new = jnp.einsum('bsd,ed->bse', x, wk)
        v_new = jnp.einsum('bsd,ed->bse', x, wv)
        k = jnp.concatenate([k_cache, k_new], axis=1)
        v = jnp.concatenate([v_cache, v_new], axis=1)
        scale = 1.0 / math.sqrt(q.shape[-1])
        scores = jnp.einsum('bqd,bkd->bqk', q, k) * scale
        attn = jax.nn.softmax(scores, axis=-1)
        out = jnp.einsum('bqk,bkd->bqd', attn, v)
        return jnp.einsum('bqd,ed->bqe', out, wo)

    def _L0_ffn_ref(x, w1, w3, w2):
        import jax, jax.numpy as jnp
        import numpy as np
        D_MODEL = 256
        HIDDEN = int(2 * D_MODEL * 4 / 3)

        def ternary_quant(w):
            s = jnp.mean(jnp.abs(w))
            q = jnp.clip(jnp.round(w / s), -1.0, 1.0) * s
            return w + jax.lax.stop_gradient(q - w)
        w1q = ternary_quant(w1)
        w3q = ternary_quant(w3)
        w2q = ternary_quant(w2)
        h1 = jnp.einsum('bsd,hd->bsh', x, w1q)
        h3 = jnp.einsum('bsd,hd->bsh', x, w3q)
        g = jax.nn.silu(h1) * h3
        return jnp.einsum('bsh,dh->bsd', g, w2q)

    def _L1_xattn_ref(B, T, C, w, u, k, v):
        import jax, jax.numpy as jnp
        import numpy as np
        B_DIM, T_DIM, C_DIM = (16, 128, 256)

        def _wkv(w, u, k, v):
            Bn, Tn, Cn = k.shape
            NEG_INF = jnp.float32(-1e+38)

            def step(carry, kv_t):
                p, q, o = carry
                kt, vt = kv_t
                no = jnp.maximum(o, u + kt)
                A = jnp.exp(o - no)
                E = jnp.exp(u + kt - no)
                y = (A * p + E * vt) / (A * q + E)
                no2 = jnp.maximum(w + o, kt)
                A2 = jnp.exp(w + o - no2)
                E2 = jnp.exp(kt - no2)
                return ((A2 * p + E2 * vt, A2 * q + E2, no2), y)
            init = (jnp.zeros((Bn, Cn), k.dtype), jnp.zeros((Bn, Cn), k.dtype), jnp.full((Bn, Cn), NEG_INF, k.dtype))
            kT = jnp.moveaxis(k, 1, 0)
            vT = jnp.moveaxis(v, 1, 0)
            _, yT = jax.lax.scan(step, init, (kT, vT))
            return jnp.moveaxis(yT, 0, 1)
        return _wkv(w, u, k, v)

    def _L1_ffn_ref(x, router_w, shared_gate, shared_up, shared_down, w_gate, w_up, w_down):
        import jax, jax.numpy as jnp
        import numpy as np
        E = 8
        TOP_K = 2
        D = 256
        F = 128
        FS = 256
        B, T = (2, 128)
        Bx, Tx, Dx = x.shape
        N = Bx * Tx
        xf = x.reshape(N, Dx)
        shared = jax.nn.silu(xf @ shared_gate) * (xf @ shared_up) @ shared_down
        probs = jax.nn.softmax(xf @ router_w, axis=-1)
        topk_vals, topk_ids = jax.lax.top_k(probs, TOP_K)
        combine = jnp.zeros((N, E), dtype=xf.dtype).at[jnp.arange(N)[:, None], topk_ids].add(topk_vals)
        gated = jax.nn.silu(jnp.einsum('nd,edf->enf', xf, w_gate))
        up = jnp.einsum('nd,edf->enf', xf, w_up)
        y = jnp.einsum('enf,efd->end', gated * up, w_down)
        routed = jnp.einsum('ne,end->nd', combine, y)
        return (shared + routed).reshape(Bx, Tx, Dx)
    x = x + jnp.tanh(g_xattn[0]) * _L0_xattn_ref(_layernorm(x, axis=-1), mask_BxSx4224_bf0, ctx_2048, ctx_2048, L0_xattn_wq, L0_xattn_wk, L0_xattn_wv, L0_xattn_wo)
    x = x + jnp.tanh(g_ffn[0]) * _L0_ffn_ref(_layernorm(x, axis=-1), L0_ffn_w1, L0_ffn_w3, L0_ffn_w2)
    x = x + jnp.tanh(g_xattn[1]) * _L1_xattn_ref(64, 64, 256, L1_xattn_w, L1_xattn_u, _layernorm(x, axis=-1), ctx_2048)
    x = x + jnp.tanh(g_ffn[1]) * _L1_ffn_ref(_layernorm(x, axis=-1), L1_ffn_router_w, L1_ffn_shared_gate, L1_ffn_shared_up, L1_ffn_shared_down, L1_ffn_w_gate, L1_ffn_w_up, L1_ffn_w_down)
    return x

_drawn_inputs = setup_inputs


def setup_inputs(seed=0):
    import zlib

    import numpy as np

    out = dict(_drawn_inputs(seed))
    spreads = {'g_ffn': (-1.0, 0.6)}
    factors = {'L1_ffn_router_w': 8.0,
     'L1_ffn_shared_gate': 5.137,
     'L1_ffn_shared_up': 5.081,
     'L1_ffn_shared_down': 5.074,
     'L1_ffn_w_gate': 8.0,
     'L1_ffn_w_up': 8.0,
     'L1_ffn_w_down': 8.0}
    for name, (base, spread) in spreads.items():
        noise = np.random.default_rng([zlib.crc32(name.encode()), seed]).standard_normal(out[name].shape)
        drawn = base * np.exp(spread * noise) if base else spread * noise
        out[name] = jnp.asarray(drawn.astype(out[name].dtype))
    for name, factor in factors.items():
        out[name] = (out[name] * factor).astype(out[name].dtype)
    return out
```

```python
from contextlib import ExitStack

import concourse.bass as bass
from concourse import mybir

ALU = mybir.AluOpType
ACT = mybir.ActivationFunctionType
AX = mybir.AxisListType
F32 = mybir.dt.float32
F32R = mybir.dt.float32r

P = 128
EPS = 1e-5
NEG = -1e38

TRANSIT = [
    ("A", "ctxT0"), ("A", "ctxT1"), ("W", "z2T0"), ("W", "z2T1"), ("M", "c2"), ("A", "z0T0"), ("A", "z0T1"), ("M", "c3"),
    ("A", "q0"), ("A", "q1"), ("A", "k0"), ("A", "k1"), ("A", "v0"), ("A", "v1"), ("M", "c4"),
    ("A", "scores"), ("M", "c5"), ("A", "pT"), ("M", "c6"), ("A", "oT0"), ("A", "oT1"), ("M", "c7"),
    ("A", "wo0"), ("A", "wo1"), ("M", "c8"), ("M", "c9"), ("A", "z1T0"), ("A", "z1T1"),
    ("W", "yT0"), ("W", "yT1"), ("W", "z3T0"), ("W", "z3T1"), ("W", "route"),
]
CHUNKS = [("M", c) for c in range(10)] + [("A", c) for c in range(6)]
SUMS = [("M", "y"), ("A", "y")]
LAG = {"A": 0, "W": 1, "M": 2}


class Turn:

    def __init__(self, i, blocks, fixed):
        self.i, self.fixed = i, fixed
        self.on = {s: not fixed or 0 <= i - lag < blocks for s, lag in LAG.items()}
        self.blocks = blocks

    def count(self, stage, per, k):
        if self.fixed:
            return (self.i - LAG[stage]) * per + k
        return self.i * per + (k - LAG[stage] * per)

    def shared(self, order, name, bank=None):
        mine = [e for n, e in enumerate(order) if bank is None or n % 2 == bank]
        now = 0
        for e in mine:
            now += self.on[e[0]]
            if e == name:
                break
        if self.fixed:
            done = {s: min(max(self.i - lag, 0), self.blocks) for s, lag in LAG.items()}
            return sum(done[s] for s, _ in mine) + now
        return self.i * len(mine) + (now - sum(LAG[s] for s, _ in mine))

    def before(self, order):
        if self.fixed:
            return sum(min(max(self.i - LAG[s], 0), self.blocks) for s, _ in order)
        return self.i * len(order) - sum(LAG[s] for s, _ in order)


def build(nc, x, ctx_in, g_xattn, g_ffn, wqT, wkT, wvT, woT, w1T, w3T, w2T, decay, bonus, router,
          s_gate, s_up, s_down, e_gate, e_up, e_down, out):
    B, S, D = x.shape
    HID = w1T.shape[1]
    E, _, F = e_gate.shape
    NT = 4
    TOK = NT * P
    NB = B * S // TOK
    NS = TOK // S
    KH = D // P
    HC = -(-HID // P)
    HR = HID - (HC - 1) * P
    SC = s_gate.shape[1] // P
    MC = SC + E
    S1 = S + 1
    SCALE = float(D) ** -0.5
    assert (S, D, F, KH, HC, MC) == (64, 256, P, 2, 6, 10)

    def rows(a):
        return a.rearrange("b s d -> (b s) d").rearrange("(n t p) d -> n p t d", t=NT, p=P)

    x_rows, ctx_rows, out_rows = rows(x), rows(ctx_in), rows(out)
    ctx_seqs = ctx_in.rearrange("(n t q) s d -> n q s t d", t=NT, q=2)

    with ExitStack() as stack:
        def sb(name, shape, dt=F32):
            return stack.enter_context(nc.sbuf_tensor(name, shape, dt))

        def sem(name):
            return stack.enter_context(nc.semaphore(name))

        transit = [stack.enter_context(nc.psum_tensor(f"transit{n}", [P, TOK], F32)) for n in range(2)]
        gate_ps = [stack.enter_context(nc.psum_tensor(f"gate_ps{n}", [P, TOK], F32)) for n in range(2)]
        up_ps = [stack.enter_context(nc.psum_tensor(f"up_ps{n}", [P, TOK], F32)) for n in range(2)]
        sums = [stack.enter_context(nc.psum_tensor(f"sums{n}", [P, TOK], F32)) for n in range(2)]

        qkv_h = sb("qkv_h", [P, 3, KH, D], F32R)
        qkv_l = sb("qkv_l", [P, 3, KH, D], F32R)
        wo = sb("wo", [P, KH, D])
        w13 = sb("w13", [P, 2, KH, HC * P], F32R)
        w2 = sb("w2", [P, HC, D], F32R)
        gate_h = sb("gate_h", [P, KH, MC, P], F32R)
        gate_l = sb("gate_l", [P, KH, MC, P], F32R)
        up_h = sb("up_h", [P, KH, MC, P], F32R)
        up_l = sb("up_l", [P, KH, MC, P], F32R)
        down_h = sb("down_h", [P, MC, D], F32R)
        down_l = sb("down_l", [P, MC, D], F32R)
        route_w = sb("route_w", [P, KH, E])
        route_h = sb("route_h", [P, KH, E], F32R)
        route_l = sb("route_l", [P, KH, E], F32R)

        ident = sb("ident", [P, P])
        ones = sb("ones", [P, P])
        minus_half = sb("minus_half", [P, NT])
        minus_one = sb("minus_one", [P, NT])
        eps_row = sb("eps_row", [P, NT])
        before = sb("before", [P, E, E])
        gains = sb("gains", [P, 4])
        gain_m = sb("gain_m", [P, 1])
        gain_f = sb("gain_f", [P, 1])
        decay_sb = sb("decay_sb", [P, KH])
        bonus_sb = sb("bonus_sb", [P, KH])
        abs_sum = sb("abs_sum", [P, 6])
        abs_tot = sb("abs_tot", [P, 3])
        scales = sb("scales", [P, 3])
        half_s = sb("half_s", [P, 3])
        neg_half_s = sb("neg_half_s", [P, 3])
        s_prod = sb("s_prod", [P, 2])

        xa = sb("xa", [P, NT, D])
        ctx_tok = sb("ctx_tok", [P, NT * D])
        probs = ctx_tok[:, 0:TOK].rearrange("p (t k) -> p t k", t=NT)
        probsT = ctx_tok[:, TOK:2 * TOK]
        ctx_row = ctx_tok[:, :].rearrange("p (t d) -> p t d", t=NT)
        vals = sb("vals", [P, NT, 2, D])
        keys = sb("keys", [P, KH, NT, 4, S])
        zqo = sb("zqo", [P, NT * D])
        za_row = zqo[:, :].rearrange("p (t d) -> p t d", t=NT)
        qo = zqo[:, :].rearrange("p (h n) -> p h n", h=KH)
        za_h = sb("za_h", [P, KH, TOK], F32R)
        za_l = sb("za_l", [P, KH, TOK], F32R)
        bn_a = sb("bn_a", [P, NT, 6])
        mv_a = sb("mv_a", [P, NT, 2])
        nmean_a = sb("nmean_a", [P, NT])
        var_a = sb("var_a", [P, NT])
        rstd_a = sb("rstd_a", [P, NT])
        shift_a = sb("shift_a", [P, NT])
        smax = sb("smax", [P, NT])
        nsmax = sb("nsmax", [P, NT])
        psum_row = sb("psum_row", [P, NT])
        rinv = sb("rinv", [P, NT])
        rgain = sb("rgain", [P, NT])

        x2 = sb("x2", [P, NT, D])
        vw = sb("vw", [P, KH, TOK])
        kw = sb("kw", [P, KH, NS, S1])
        decay_row = sb("decay_row", [P, KH, NS, S1])
        wide = NS * S1
        wk = sb("wk", [P, KH * 7 * wide])
        wk_parts = wk[:, :].rearrange("p (h c n) -> p h c n", h=KH, c=7)
        zw_row = wk[:, 4 * wide:4 * wide + NT * D].rearrange("p (t d) -> p t d", t=NT)
        bn_w = sb("bn_w", [P, NT, 6])
        mv_w = sb("mv_w", [P, NT, 2])
        nmean_w = sb("nmean_w", [P, NT])
        var_w = sb("var_w", [P, NT])
        rstd_w = sb("rstd_w", [P, NT])
        shift_w = sb("shift_w", [P, NT])

        def flat(h, c):
            return wk_parts[:, h, c, :]

        def seqs(h, c, first):
            return flat(h, c).rearrange("p (b s) -> p b s", b=NS)[:, :, first:first + S]

        OMAX, A2, E2, EV, DELTA, EA, EE = range(7)

        x3 = sb("x3", [P, NT, D])
        out_row = sb("out_row", [P, NT, D])
        zm_h = sb("zm_h", [P, KH, TOK], F32R)
        zm_l = sb("zm_l", [P, KH, TOK], F32R)
        lmax = sb("lmax", [P, NT])
        pexp = sb("pexp", [P, NT, E])
        psum_e = sb("psum_e", [P, NT])
        pinv = sb("pinv", [P, NT])
        rank = sb("rank", [P, NT])
        beats, ties = (flat(1, c)[:, 0:NT * E * E].rearrange("p (r e f) -> p r e f", r=NT, e=E) for c in (DELTA, EA))
        ranks = sb("ranks", [P, NT, E])
        combine = sb("combine", [P, NT, E])

        act_sb = sb("act_sb", [P, 2, TOK])
        comb_sb = sb("comb_sb", [P, 2, TOK])
        hid_h = sb("hid_h", [P, 2, TOK], F32R)
        hid_l = sb("hid_l", [P, 2, TOK], F32R)

        small_in = sem("small_in")
        raw_qkv_in, raw_tern_in, raw_down_in, raw_gate_in, raw_up_in = (
            sem("raw_qkv_in"), sem("raw_tern_in"), sem("raw_down_in"), sem("raw_gate_in"), sem("raw_up_in"))
        ident_zero, consts_set, tri_ones, tri_set = (sem("ident_zero"), sem("consts_set"), sem("tri_ones"), sem("tri_set"))
        gains_set, gain_chain, abs_set, abs_all, tern_chain, tern_set = (
            sem("gains_set"), sem("gain_chain"), sem("abs_set"), sem("abs_all"), sem("tern_chain"), sem("tern_set"))
        pads_set, high_set, low_set, scan_zero, scan_set = (
            sem("pads_set"), sem("high_set"), sem("low_set"), sem("scan_zero"), sem("scan_set"))
        x_in, ctx_row_in, ctx_val_in, out_done = sem("x_in"), sem("ctx_row_in"), sem("ctx_val_in"), sem("out_done")
        t_full = [sem(f"t_full{n}") for n in range(2)]
        t_free = [sem(f"t_free{n}") for n in range(2)]
        bn_done = {"A": sem("bn_done_a"), "W": sem("bn_done_w")}
        bn_seen = sem("bn_seen")
        mv_done = {"A": sem("mv_done_a"), "W": sem("mv_done_w")}
        var_done = {"A": sem("var_done_a"), "W": sem("var_done_w")}
        rstd_done = {"A": sem("rstd_done_a"), "W": sem("rstd_done_w")}
        shift_done = {"A": sem("shift_done_a"), "W": sem("shift_done_w")}
        z_done = {"A": sem("z_done_a"), "W": sem("z_done_w")}
        za_h_set, zm_h_set, smax_set, nsmax_set, rinv_set, rgain_set, vw_set = (
            sem("za_h_set"), sem("zm_h_set"), sem("smax_set"), sem("nsmax_set"), sem("rinv_set"), sem("rgain_set"), sem("vw_set"))
        omax_set, a2arg_set, e2arg_set, delta_set, clamp_set = (
            sem("omax_set"), sem("a2arg_set"), sem("e2arg_set"), sem("delta_set"), sem("clamp_set"))
        a2_set, e2_set, ea_set, ee_set, ev_set, scans_done, eev_set = (
            sem("a2_set"), sem("e2_set"), sem("ea_set"), sem("ee_set"), sem("ev_set"), sem("scans_done"), sem("eev_set"))
        ap_set, aq_set, num_set, den_set, dinv_set, yw_set = (
            sem("ap_set"), sem("aq_set"), sem("num_set"), sem("den_set"), sem("dinv_set"), sem("yw_set"))
        lmax_set, pexp_set, route_chain, combine_set = (
            sem("lmax_set"), sem("pexp_set"), sem("route_chain"), sem("combine_set"))
        up_full, tanh_done, gated_one, gated, weighted, hid_h_set, hid_l_set, down_done, sums_free = (
            sem("up_full"), sem("tanh_done"), sem("gated_one"), sem("gated"), sem("weighted"), sem("hid_h_set"),
            sem("hid_l_set"), sem("down_done"), sem("sums_free"))

        def bank_of(use):
            return TRANSIT.index(use) % 2

        def wait_full(eng, t, stage, name):
            n = bank_of((stage, name))
            eng.wait_ge(t_full[n], t.shared(TRANSIT, (stage, name), n))
            return transit[n]

        def wait_taken(eng, t, stage, *names, claims=None):
            last = {bank_of((stage, name)): name for name in names}
            for n, name in last.items():
                if claims is None or n != bank_of(claims):
                    eng.wait_ge(t_free[n], t.shared(TRANSIT, (stage, name), n))

        def free_of(stage, name):
            return t_free[bank_of((stage, name))]

        def chunk_no(t, chunk):
            return t.shared(CHUNKS, chunk)

        def wait_back(eng, s, t, chunk, back):
            n = chunk_no(t, chunk) - back
            if not t.fixed or n > 0:
                eng.wait_ge(s, n)

        def scaled_chunk(t, c):
            return t.count("M", E, c - SC + 1)

        def turns(eng, body):
            for i in range(3):
                body(Turn(i, NB, True))
            with eng.Fori(3, NB) as i:
                body(Turn(i, NB, False))
            for i in range(NB, NB + 2):
                body(Turn(i, NB, True))

        raw_qkv = keys[:, :, :, :, :].rearrange("p h t c s -> p (h t c s)")[:, 0:3 * KH * D].rearrange(
            "p (w k e) -> p w k e", w=3, k=KH)
        n13 = 2 * KH * HID
        raw13 = wk[:, 0:n13].rearrange("p (w k e) -> p w k e", w=2, k=KH)
        raw2 = wk[:, n13:n13 + HC * D].rearrange("p (c e) -> p c e", c=HC)
        MW = MC * D
        raw_down = wk[:, 4304:4304 + MW].rearrange("p (c e) -> p c e", c=MC)
        raw_gate = wk[:, 0:MW].rearrange("p (k c f) -> p k c f", k=KH, c=MC)
        raw_up = wk[:, MW:2 * MW].rearrange("p (k c f) -> p k c f", k=KH, c=MC)
        assert n13 + HC * D <= 4304 and 4304 + MW <= KH * 7 * wide

        block = stack.enter_context(nc.Block())

        @block.sync
        def _(sp):
            for n, w in enumerate((wqT, wkT, wvT)):
                sp.dma_start(raw_qkv[:, n], w.rearrange("(k p) e -> p k e", p=P)).then_inc(raw_qkv_in, 16)
            sp.dma_start(raw13[:, 0], w1T.rearrange("(k p) e -> p k e", p=P)).then_inc(raw_tern_in, 16)
            sp.dma_start(raw13[:, 1], w3T.rearrange("(k p) e -> p k e", p=P)).then_inc(raw_tern_in, 16)
            full = (HC - 1) * P
            sp.dma_start(raw2[:, 0:HC - 1], w2T[0:full].rearrange("(c p) e -> p c e", p=P)).then_inc(raw_tern_in, 16)
            sp.wait_ge(pads_set, 2)
            sp.dma_start(raw2[0:HR, HC - 1], w2T[full:HID]).then_inc(raw_tern_in, 16)
            sp.dma_start(wo[:], woT.rearrange("(k p) e -> p k e", p=P)).then_inc(small_in, 16)
            sp.dma_start(route_w[:], router.rearrange("(k p) e -> p k e", p=P)).then_inc(small_in, 16)
            sp.dma_start(decay_sb[:], decay.rearrange("(h p) -> p h", p=P), allow_slow_non_contiguous=True).then_inc(small_in, 16)
            sp.dma_start(bonus_sb[:], bonus.rearrange("(h p) -> p h", p=P), allow_slow_non_contiguous=True).then_inc(small_in, 16)
            sp.dma_start(gains[:, 0:2], g_xattn.partition_broadcast(P)).then_inc(small_in, 16)
            sp.dma_start(gains[:, 2:4], g_ffn.partition_broadcast(P)).then_inc(small_in, 16)
            sp.dma_start(raw_down[:, 0:SC], s_down.rearrange("(c p) e -> p c e", p=P)).then_inc(raw_down_in, 16)
            sp.dma_start(raw_down[:, SC:MC], e_down.rearrange("e f d -> f e d")).then_inc(raw_down_in, 16)
            sp.wait_ge(tern_set, 3)
            sp.wait_ge(low_set, 2)
            for raw, shared, expert, s in ((raw_gate, s_gate, e_gate, raw_gate_in), (raw_up, s_up, e_up, raw_up_in)):
                for k in range(KH):
                    sp.dma_start(raw[:, k, 0:SC], shared[k * P:(k + 1) * P].rearrange("p (c f) -> p c f", f=P)).then_inc(s, 16)
                    sp.dma_start(raw[:, k, SC:MC], expert[:, k * P:(k + 1) * P].rearrange("e p f -> p e f")).then_inc(s, 16)

            def turn(t):
                if t.on["A"]:
                    if not t.fixed or t.i > 0:
                        sp.wait_ge(rstd_done["A"], t.count("A", 2, 0))
                    sp.dma_start(ctx_row, ctx_rows[t.i]).then_inc(ctx_row_in, 16)
                    sp.dma_start(vals[S:P, :, 0], ctx_seqs[t.i, 0]).then_inc(ctx_val_in, 16)
                    sp.dma_start(vals[0:S, :, 1], ctx_seqs[t.i, 1]).then_inc(ctx_val_in, 16)
                    if not t.fixed or t.i > 0:
                        sp.wait_ge(sums_free, t.before(SUMS))
                    sp.dma_start(xa[:], x_rows[t.i]).then_inc(x_in, 16)
                if t.on["M"]:
                    sp.wait_ge(sums_free, t.shared(SUMS, ("M", "y")))
                    sp.dma_start(out_rows[t.i - LAG["M"]], out_row[:]).then_inc(out_done, 16)

            turns(sp, turn)
            sp.wait_ge(out_done, 16 * NB)

        @block.tensor
        def _(pe):
            pe.wait_ge(consts_set, 2)
            pe.wait_ge(abs_set, 6)
            nc.tensor.matmul(gate_ps[0][:, 0:6], ones[:], abs_sum[:], start=True, stop=True).then_inc(abs_all, 1)
            pe.wait_ge(low_set, 5)
            pe.wait_ge(high_set, 5)
            pe.wait_ge(tern_chain, 1)

            def claim(t, stage, name):
                n = bank_of((stage, name))
                before_me = t.shared(TRANSIT, (stage, name), n) - 1
                if not t.fixed or before_me > 0:
                    pe.wait_ge(t_free[n], before_me)
                return transit[n], t_full[n]

            def turn_rows(t, stage, name, source, h):
                bank, full = claim(t, stage, name)
                for r in range(NT):
                    last = nc.tensor.transpose(bank[:, r * P:(r + 1) * P], source[:, r, h * P:(h + 1) * P], ident[:])
                last.then_inc(full, 1)

            def split_product(o, lhs, rhs, first, final, group=True):
                (lh, ll), (rh, rl) = lhs, rhs
                pairs = [(lh, rh)] + ([(lh, rl)] if rl is not None else []) + ([(ll, rh)] if ll is not None else [])
                for n, (a, b) in enumerate(pairs):
                    last = nc.tensor.matmul(o, a, b, start=first and n == 0, stop=final and n == len(pairs) - 1,
                                            skip_group_check=not group)
                return last

            def context_T(t):
                pe.wait_ge(ctx_row_in, t.count("A", 16, 16))
                for h in range(KH):
                    turn_rows(t, "A", f"ctxT{h}", ctx_row, h)

            def z_T(t, stage, which, source, n):
                pe.wait_ge(z_done[stage], t.count(stage, 2, n))
                for h in range(KH):
                    turn_rows(t, stage, f"{which}{h}", source, h)

            def q_and_k(t):
                wait_taken(pe, t, "A", "z0T0", "z0T1", claims=("A", "q0"))
                for w, name in enumerate("qk"):
                    for m in range(KH):
                        bank, full = claim(t, "A", f"{name}{m}")
                        cols = slice(m * P, (m + 1) * P)
                        for k in range(KH):
                            last = split_product(bank[:], (qkv_h[:, w, k, cols], qkv_l[:, w, k, cols]),
                                                 (za_h[:, k], za_l[:, k]), k == 0, k == KH - 1)
                        last.then_inc(full, 1)

            def values(t):
                for pair in range(2):
                    bank, full = claim(t, "A", f"v{pair}")
                    for r in range(2):
                        rows_ = slice((2 * pair + r) * P, (2 * pair + r + 1) * P)
                        for k in range(KH):
                            last = split_product(bank[:, r * D:(r + 1) * D], (za_h[:, k, rows_], za_l[:, k, rows_]),
                                                 (qkv_h[:, 2, k], qkv_l[:, 2, k]), k == 0, k == KH - 1)
                    last.then_inc(full, 1)

            def scores(t):
                wait_taken(pe, t, "A", "k0", "k1", claims=("A", "scores"))
                bank, full = claim(t, "A", "scores")
                for r in range(NT):
                    for q in range(2):
                        for h in range(KH):
                            last = nc.tensor.matmul(
                                bank[q * S:(q + 1) * S, r * P:(r + 1) * P], qo[:, h, (2 * r + q) * S:(2 * r + q + 1) * S],
                                keys[:, h, r, 2 * q:2 * q + 2].rearrange("p c s -> p (c s)"), start=h == 0, stop=h == KH - 1)
                last.then_inc(full, 1)

            def probs_T(t):
                wait_taken(pe, t, "A", "scores", claims=("A", "pT"))
                bank, full = claim(t, "A", "pT")
                for r in range(NT):
                    last = nc.tensor.transpose(bank[:, r * P:(r + 1) * P], probs[:, r], ident[:])
                last.then_inc(full, 1)

            def attend(t):
                wait_taken(pe, t, "A", "v0", "v1", "pT", claims=("A", "oT0"))
                pe.wait_ge(ctx_val_in, t.count("A", 32, 32))
                for h in range(KH):
                    bank, full = claim(t, "A", f"oT{h}")
                    for r in range(NT):
                        for q in range(2):
                            cols = slice((2 * r + q) * S, (2 * r + q + 1) * S)
                            last = nc.tensor.matmul(bank[:, cols], vals[:, r, q, h * P:(h + 1) * P], probsT[:, cols],
                                                    start=True, stop=True)
                    last.then_inc(full, 1)

            def project(t):
                wait_taken(pe, t, "A", "oT0", "oT1", claims=("A", "wo0"))
                for pair in range(2):
                    bank, full = claim(t, "A", f"wo{pair}")
                    for r in range(2):
                        for k in range(KH):
                            last = nc.tensor.matmul(bank[:, r * D:(r + 1) * D], qo[:, k, (2 * pair + r) * P:(2 * pair + r + 1) * P],
                                                    wo[:, k], start=k == 0, stop=k == KH - 1)
                    last.then_inc(full, 1)

            def y_T(t):
                pe.wait_ge(yw_set, t.count("W", KH, KH))
                for pair in range(2):
                    bank, full = claim(t, "W", f"yT{pair}")
                    for r in range(2):
                        for h in range(KH):
                            last = nc.tensor.transpose(bank[:, r * D + h * P:r * D + (h + 1) * P],
                                                       vw[:, h, (2 * pair + r) * P:(2 * pair + r + 1) * P], ident[:])
                    last.then_inc(full, 1)

            def route(t):
                wait_taken(pe, t, "W", "z3T0", "z3T1", claims=("W", "route"))
                bank, full = claim(t, "W", "route")
                for r in range(NT):
                    rows_ = slice(r * P, (r + 1) * P)
                    for k in range(KH):
                        last = split_product(bank[:, r * E:(r + 1) * E], (zm_h[:, k, rows_], zm_l[:, k, rows_]),
                                             (route_h[:, k], route_l[:, k]), k == 0, k == KH - 1)
                last.then_inc(full, 1)

            def up(t, chunk):
                stage, c = chunk
                pos = CHUNKS.index(chunk) % 2
                wait_back(pe, gated, t, chunk, 2)
                if stage == "M":
                    parts = ((gate_ps, gate_h, gate_l), (up_ps, up_h, up_l))
                    for ps, wh, wl in parts:
                        for k in range(KH):
                            last = split_product(ps[pos][:], (wh[:, k, c], wl[:, k, c]), (zm_h[:, k], zm_l[:, k]),
                                                 k == 0, k == KH - 1)
                else:
                    if c == 0:
                        wait_taken(pe, t, "A", "z1T0", "z1T1")
                    cols = slice(c * P, (c + 1) * P)
                    for w, ps in enumerate((gate_ps, up_ps)):
                        for k in range(KH):
                            last = split_product(ps[pos][:], (w13[:, w, k, cols], None), (za_h[:, k], za_l[:, k]),
                                                 k == 0, k == KH - 1)
                last.then_inc(up_full, 1)
                if stage == "M" and c >= SC:
                    if c == SC:
                        pe.wait_ge(combine_set, t.count("M", 1, 1))
                    bank, full = claim(t, "M", f"c{c}")
                    for r in range(NT):
                        last = nc.tensor.transpose(bank[:, r * P:(r + 1) * P],
                                                   combine[:, r, c - SC:c - SC + 1].broadcast_to([P, P]), ident[:])
                    last.then_inc(full, 1)

            def down(t, chunk):
                stage, c = chunk
                pos = CHUNKS.index(chunk) % 2
                final = c == (MC if stage == "M" else HC) - 1
                pe.wait_ge(hid_h_set, chunk_no(t, chunk))
                pe.wait_ge(hid_l_set, chunk_no(t, chunk))
                if c == 0:
                    n = t.shared(SUMS, (stage, "y")) - 1
                    if not t.fixed or n > 0:
                        pe.wait_ge(sums_free, n)
                w = (down_h[:, c], down_l[:, c]) if stage == "M" else (w2[:, c], None)
                for r in range(NT):
                    rows_ = slice(r * P, (r + 1) * P)
                    last = split_product(sums[r // 2][:, (r % 2) * D:(r % 2 + 1) * D],
                                         (hid_h[:, pos, rows_], hid_l[:, pos, rows_]), w, c == 0 and r % 2 == 0, final, group=False)
                last.then_inc(down_done, 1)

            def turn(t):
                a, w, m = t.on["A"], t.on["W"], t.on["M"]

                def m_up(c):
                    if m:
                        up(t, ("M", c))
                        if c >= 2:
                            down(t, ("M", c - 2))

                def f_up(c):
                    if a:
                        up(t, ("A", c))
                        if c >= 2:
                            down(t, ("A", c - 2))
                m_up(0)
                if a:
                    context_T(t)
                m_up(1)
                if w:
                    z_T(t, "W", "z2T", zw_row, 1)
                m_up(2)
                if a:
                    z_T(t, "A", "z0T", za_row, 1)
                m_up(3)
                if a:
                    q_and_k(t)
                    values(t)
                m_up(4)
                if a:
                    scores(t)
                m_up(5)
                if a:
                    probs_T(t)
                m_up(6)
                if a:
                    attend(t)
                m_up(7)
                if a:
                    project(t)
                m_up(8)
                m_up(9)
                if a:
                    z_T(t, "A", "z1T", za_row, 2)
                if m:
                    down(t, ("M", MC - 2))
                f_up(0)
                if m:
                    down(t, ("M", MC - 1))
                if w:
                    y_T(t)
                f_up(1)
                f_up(2)
                f_up(3)
                if w:
                    z_T(t, "W", "z3T", zw_row, 2)
                f_up(4)
                f_up(5)
                if w:
                    route(t)
                if a:
                    down(t, ("A", HC - 2))
                    down(t, ("A", HC - 1))

            turns(pe, turn)

        @block.scalar
        def _(act):
            def high(n, dst, src):
                nc.scalar.activation(dst, src, ACT.Copy).then_inc(high_set, 1)

            act.wait_ge(small_in, 96)
            nc.scalar.activation(gains[:], gains[:], ACT.Tanh).then_inc(gains_set, 1)
            act.wait_ge(raw_qkv_in, 48)
            high(1, qkv_h[:].rearrange("p w k e -> p (w k e)"), raw_qkv.rearrange("p w k e -> p (w k e)"))
            act.wait_ge(raw_tern_in, 64)
            scratch = act_sb[:, :, :].rearrange("p a n -> p (a n)")
            for w in range(2):
                for k in range(KH):
                    nc.scalar.activation(scratch[:, 0:HID], raw13[:, w, k], ACT.Abs,
                                         accum_out=abs_sum[:, 2 * w + k:2 * w + k + 1]).then_inc(abs_set, 1)
                    act.wait_ge(abs_set, 2 * w + k + 1)
            for n in range(2):
                half = HC // 2
                nc.scalar.activation(scratch[:, 0:half * D], raw2[:, n * half:(n + 1) * half].rearrange("p c e -> p (c e)"), ACT.Abs,
                                     accum_out=abs_sum[:, 4 + n:5 + n]).then_inc(abs_set, 1)
                act.wait_ge(abs_set, 5 + n)
            act.wait_ge(raw_down_in, 32)
            high(2, down_h[:].rearrange("p c e -> p (c e)"), raw_down.rearrange("p c e -> p (c e)"))
            high(3, route_h[:], route_w[:])
            act.wait_ge(raw_gate_in, 16 * 2 * KH)
            high(4, gate_h[:].rearrange("p k c f -> p (k c f)"), raw_gate.rearrange("p k c f -> p (k c f)"))
            act.wait_ge(raw_up_in, 16 * 2 * KH)
            high(5, up_h[:].rearrange("p k c f -> p (k c f)"), raw_up.rearrange("p k c f -> p (k c f)"))
            act.wait_ge(tern_set, 3)

            def normalise(t, stage, n, rows_in, rows_out, rstd, shift):
                act.wait_ge(shift_done[stage], t.count(stage, 2, n))
                for r in range(NT):
                    last = nc.scalar.activation(rows_out[:, r], rows_in[:, r], ACT.Identity, bias=shift[:, r:r + 1],
                                                scale=rstd[:, r:r + 1])
                last.then_inc(z_done[stage], 1)

            def high_parts(t, stage, which, dst, done):
                for h in range(KH):
                    bank = wait_full(act, t, stage, f"{which}{h}")
                    nc.scalar.activation(dst[:, h], bank[:], ACT.Copy).then_inc(done, 1)

            def context_T(t):
                if not t.fixed or t.i > 0:
                    act.wait_ge(vw_set, t.count("A", 1, 0))
                for h in range(KH):
                    bank = wait_full(act, t, "A", f"ctxT{h}")
                    nc.scalar.activation(keys[:, h, :, 1:3].rearrange("p t c s -> p t (c s)"),
                                         bank[:].rearrange("p (t n) -> p t n", t=NT), ACT.Copy).then_inc(free_of("A", f"ctxT{h}"), 1)

            def q_and_k(t):
                for m in range(KH):
                    bank = wait_full(act, t, "A", f"q{m}")
                    nc.scalar.activation(qo[:, m], bank[:], ACT.Copy).then_inc(free_of("A", f"q{m}"), 1)
                for m in range(KH):
                    bank = wait_full(act, t, "A", f"k{m}")
                    nc.scalar.activation(keys[:, m, :, 0:4:3], bank[:].rearrange("p (t q s) -> p t q s", t=NT, q=2),
                                         ACT.Copy).then_inc(free_of("A", f"k{m}"), 1)

            def values(t):
                for pair in range(2):
                    bank = wait_full(act, t, "A", f"v{pair}")
                    for q in range(2):
                        half = slice(q * S, (q + 1) * S)
                        last = nc.scalar.activation(vals[half, 2 * pair:2 * pair + 2, q],
                                                    bank[half].rearrange("p (r d) -> p r d", r=2), ACT.Copy)
                    last.then_inc(free_of("A", f"v{pair}"), 1)

            def softmax(t):
                bank = wait_full(act, t, "A", "scores")
                act.wait_ge(nsmax_set, t.count("A", 1, 1))
                for r in range(NT):
                    last = nc.scalar.activation(probs[:, r], bank[:, r * P:(r + 1) * P], ACT.Exp, bias=nsmax[:, r:r + 1],
                                                scale=SCALE, accum_out=psum_row[:, r:r + 1])
                last.then_inc(free_of("A", "scores"), 1)

            def probs_T(t):
                bank = wait_full(act, t, "A", "pT")
                nc.scalar.activation(probsT, bank[:], ACT.Copy).then_inc(free_of("A", "pT"), 1)

            def attend(t):
                for h in range(KH):
                    bank = wait_full(act, t, "A", f"oT{h}")
                    nc.scalar.activation(qo[:, h], bank[:], ACT.Copy).then_inc(free_of("A", f"oT{h}"), 1)

            def k_wide(t):
                for h in range(KH):
                    bank = wait_full(act, t, "W", f"z2T{h}")
                    nc.scalar.activation(kw[:, h, :, 1:S1], bank[:].rearrange("p (b s) -> p b s", b=NS), ACT.Copy).then_inc(free_of("W", f"z2T{h}"), 1)

            def decays(t, h):
                act.wait_ge(a2arg_set, t.count("W", KH, h + 1))
                nc.scalar.activation(seqs(h, A2, 1), seqs(h, A2, 1), ACT.Exp).then_inc(a2_set, 1)
                act.wait_ge(e2arg_set, t.count("W", KH, h + 1))
                nc.scalar.activation(seqs(h, E2, 1), seqs(h, E2, 1), ACT.Exp).then_inc(e2_set, 1)

            def readouts(t, h):
                act.wait_ge(clamp_set, t.count("W", 2 * KH, 2 * h + 2))
                nc.scalar.activation(flat(h, EA)[:, 0:TOK], flat(h, EA)[:, 0:TOK], ACT.Exp, scale=-1.0).then_inc(ea_set, 1)
                nc.scalar.activation(flat(h, EE)[:, 0:TOK], flat(h, EE)[:, 0:TOK], ACT.Exp).then_inc(ee_set, 1)

            def route(t):
                wait_taken(act, t, "W", "route")
                nc.scalar.activation(pexp[:], pexp[:], ACT.Exp).then_inc(pexp_set, 1)

            def squash(t, chunk):
                stage, c = chunk
                pos = CHUNKS.index(chunk) % 2
                act.wait_ge(up_full, chunk_no(t, chunk))
                wait_back(act, hid_l_set, t, chunk, 2)
                nc.scalar.activation(act_sb[:, pos], gate_ps[pos][:], ACT.Tanh,
                                     scale=0.5 if stage == "M" else half_s[:, 0:1]).then_inc(tanh_done, 1)
                if stage == "M" and c >= SC:
                    bank = wait_full(act, t, "M", f"c{c}")
                    nc.scalar.activation(comb_sb[:, pos], bank[:], ACT.Copy).then_inc(free_of("M", f"c{c}"), 1)

            def high_hidden(t, chunk):
                stage, c = chunk
                pos = CHUNKS.index(chunk) % 2
                if stage == "M" and c >= SC:
                    act.wait_ge(weighted, scaled_chunk(t, c))
                else:
                    act.wait_ge(gated, chunk_no(t, chunk))
                wait_back(act, down_done, t, chunk, 2)
                nc.scalar.activation(hid_h[:, pos], act_sb[:, pos], ACT.Copy).then_inc(hid_h_set, 1)

            def turn(t):
                a, w, m = t.on["A"], t.on["W"], t.on["M"]

                def m_chunk(c):
                    if m:
                        if c >= 1:
                            high_hidden(t, ("M", c - 1))
                        squash(t, ("M", c))

                def f_chunk(c):
                    if a:
                        if c >= 1:
                            high_hidden(t, ("A", c - 1))
                        squash(t, ("A", c))
                m_chunk(0)
                if a:
                    context_T(t)
                if w:
                    normalise(t, "W", 1, x2, zw_row, rstd_w, shift_w)
                m_chunk(1)
                if a:
                    normalise(t, "A", 1, xa, za_row, rstd_a, shift_a)
                if w:
                    k_wide(t)
                m_chunk(2)
                if a:
                    high_parts(t, "A", "z0T", za_h, za_h_set)
                m_chunk(3)
                if w:
                    for h in range(KH):
                        decays(t, h)
                if a:
                    q_and_k(t)
                    values(t)
                m_chunk(4)
                if w:
                    for h in range(KH):
                        readouts(t, h)
                if a:
                    softmax(t)
                m_chunk(5)
                if a:
                    probs_T(t)
                m_chunk(6)
                if a:
                    attend(t)
                m_chunk(7)
                m_chunk(8)
                if a:
                    normalise(t, "A", 2, xa, za_row, rstd_a, shift_a)
                m_chunk(9)
                if a:
                    high_parts(t, "A", "z1T", za_h, za_h_set)
                if m:
                    high_hidden(t, ("M", MC - 1))
                f_chunk(0)
                f_chunk(1)
                f_chunk(2)
                if w:
                    normalise(t, "W", 2, x3, zw_row, rstd_w, shift_w)
                f_chunk(3)
                if w:
                    high_parts(t, "W", "z3T", zm_h, zm_h_set)
                f_chunk(4)
                f_chunk(5)
                if a:
                    high_hidden(t, ("A", HC - 1))
                if w:
                    route(t)
                if a:
                    if w:
                        wait_full(act, t, "W", "yT1")
                    for h in range(KH):
                        last = nc.scalar.activation(vw[:, h].rearrange("p (t n) -> p t n", t=NT),
                                                    keys[:, h, :, 1:3].rearrange("p t c s -> p t (c s)"), ACT.Copy)
                    last.then_inc(vw_set, 1)

            turns(act, turn)

        @block.gpsimd
        def _(pool):
            nc.gpsimd.memset(ident[:], 0.0).then_inc(ident_zero, 1)
            nc.gpsimd.memset(before[:], 1.0).then_inc(ident_zero, 1)
            nc.gpsimd.memset(raw2[:, HC - 1], 0.0).then_inc(pads_set, 1)
            nc.gpsimd.memset(w13[:, :, :, HID:].bitcast(F32), 0.0).then_inc(pads_set, 1)
            nc.gpsimd.memset(ones[:], 1.0)
            nc.gpsimd.memset(minus_half[:], -0.5)
            nc.gpsimd.memset(minus_one[:], -1.0)
            nc.gpsimd.memset(eps_row[:], EPS)
            pool.wait_ge(ident_zero, 2)
            nc.gpsimd.affine_select(out=before[:], in_=before[:], compare_op=ALU.is_gt, fill=0.0, base=0,
                                    pattern=[[1, E], [-1, E]], channel_multiplier=0).then_inc(consts_set, 1)
            nc.gpsimd.affine_select(out=ident[:], in_=ident[:], compare_op=ALU.not_equal, fill=1.0, base=0,
                                    pattern=[[-1, P]], channel_multiplier=1).then_inc(consts_set, 1)

            def row_factors(t, stage, n, stats, nmean, var, rstd, shift):
                pool.wait_ge(mv_done[stage], t.count(stage, 2, n))
                nc.gpsimd.tensor_tensor(var[:], stats[:, :, 1], eps_row[:], ALU.add).then_inc(var_done[stage], 1)
                nc.gpsimd.tensor_tensor(nmean[:], stats[:, :, 0], minus_one[:], ALU.mult)
                pool.wait_ge(var_done[stage], t.count(stage, 2, n))
                nc.gpsimd.tensor_tensor(rstd[:], var[:], minus_half[:], ALU.pow).then_inc(rstd_done[stage], 1)
                pool.wait_ge(rstd_done[stage], t.count(stage, 2, n))
                nc.gpsimd.tensor_tensor(shift[:], nmean[:], rstd[:], ALU.mult).then_inc(shift_done[stage], 1)

            def inputs(t, h):
                pool.wait_ge(omax_set, t.count("W", KH, h + 1))
                nc.gpsimd.tensor_tensor(seqs(h, E2, 1), kw[:, h, :, 1:S1], seqs(h, OMAX, 1), ALU.subtract).then_inc(e2arg_set, 1)

            def weigh_inputs(t, h):
                pool.wait_ge(e2_set, t.count("W", KH, h + 1))
                pool.wait_ge(vw_set, t.count("W", 1, 1))
                nc.gpsimd.tensor_tensor(seqs(h, EV, 1), seqs(h, E2, 1), vw[:, h].rearrange("p (b s) -> p b s", b=NS),
                                        ALU.mult).then_inc(ev_set, 1)

            def weigh_now(t, h):
                pool.wait_ge(ee_set, t.count("W", KH, h + 1))
                pool.wait_ge(scans_done, t.count("W", 2 * KH, 2 * h + 2))
                nc.gpsimd.tensor_tensor(seqs(h, A2, 1), flat(h, EE)[:, 0:TOK].rearrange("p (b s) -> p b s", b=NS),
                                        vw[:, h].rearrange("p (b s) -> p b s", b=NS), ALU.mult).then_inc(eev_set, 1)

            def low_hidden(t, chunk):
                pos = CHUNKS.index(chunk) % 2
                pool.wait_ge(hid_h_set, chunk_no(t, chunk))
                nc.gpsimd.tensor_tensor(hid_l[:, pos], act_sb[:, pos], hid_h[:, pos].bitcast(F32), ALU.subtract).then_inc(hid_l_set, 1)

            def weigh_chunk(t, chunk):
                c = chunk[1]
                pos = CHUNKS.index(chunk) % 2
                if c >= SC:
                    pool.wait_ge(gated, chunk_no(t, chunk))
                    wait_taken(pool, t, "M", f"c{c}")
                    nc.gpsimd.tensor_tensor(act_sb[:, pos], act_sb[:, pos], comb_sb[:, pos], ALU.mult).then_inc(weighted, 1)

            def turn(t):
                a, w, m = t.on["A"], t.on["W"], t.on["M"]

                def m_chunk(c):
                    if m:
                        if c >= 1:
                            low_hidden(t, ("M", c - 1))
                        weigh_chunk(t, ("M", c))
                if w:
                    row_factors(t, "W", 1, mv_w, nmean_w, var_w, rstd_w, shift_w)
                if a:
                    row_factors(t, "A", 1, mv_a, nmean_a, var_a, rstd_a, shift_a)
                m_chunk(0)
                m_chunk(1)
                if w:
                    for h in range(KH):
                        inputs(t, h)
                m_chunk(2)
                m_chunk(3)
                if w:
                    for h in range(KH):
                        weigh_inputs(t, h)
                m_chunk(4)
                m_chunk(5)
                if w:
                    weigh_now(t, 0)
                m_chunk(6)
                if w:
                    weigh_now(t, 1)
                m_chunk(7)
                if m:
                    low_hidden(t, ("M", 7))
                if a:
                    row_factors(t, "A", 2, mv_a, nmean_a, var_a, rstd_a, shift_a)
                if m:
                    weigh_chunk(t, ("M", 8))
                m_chunk(9)
                if m:
                    low_hidden(t, ("M", MC - 1))
                if a:
                    for c in range(2):
                        low_hidden(t, ("A", c))
                if w:
                    row_factors(t, "W", 2, mv_w, nmean_w, var_w, rstd_w, shift_w)
                if a:
                    for c in range(2, HC):
                        low_hidden(t, ("A", c))

            turns(pool, turn)

        @block.vector
        def _(dve):
            dve.wait_ge(gains_set, 1)
            nc.vector.tensor_scalar(gain_m[:], gains[:, 3:4], 0.5, None, ALU.mult)
            nc.vector.memset(decay_row[:], 0.0).then_inc(scan_zero, 1)
            dve.wait_ge(scan_zero, 1)
            for h in range(KH):
                nc.vector.tensor_scalar(decay_row[:, h, :, 1:S1], decay_row[:, h, :, 1:S1], decay_sb[:, h:h + 1], None, ALU.add)
            nc.vector.memset(decay_row[:, :, :, 0:1], NEG)
            nc.vector.memset(kw[:, :, :, 0:1], NEG).then_inc(scan_set, 1)

            def low(n, dst, src, high_part):
                dve.wait_ge(high_set, n)
                nc.vector.tensor_tensor(dst, src, high_part.bitcast(F32), ALU.subtract).then_inc(low_set, 1)

            low(1, qkv_l[:].rearrange("p w k e -> p (w k e)"), raw_qkv.rearrange("p w k e -> p (w k e)"),
                qkv_h[:].rearrange("p w k e -> p (w k e)"))
            dve.wait_ge(abs_all, 1)
            nc.vector.tensor_reduce(abs_tot[:], gate_ps[0][:, 0:6].rearrange("p (w k) -> p w k", w=3), AX.X, ALU.add).then_inc(tern_chain, 1)
            dve.wait_ge(tern_chain, 1)
            nc.vector.tensor_scalar(scales[:], abs_tot[:], 1.0 / (HID * D), None, ALU.mult)
            nc.vector.tensor_scalar(half_s[:], abs_tot[:], 0.5 / (HID * D), None, ALU.mult)
            nc.vector.tensor_scalar(neg_half_s[:], abs_tot[:], -0.5 / (HID * D), None, ALU.mult).then_inc(tern_chain, 1)
            dve.wait_ge(tern_chain, 2)
            nc.vector.tensor_scalar(s_prod[:, 0:1], scales[:, 0:1], scales[:, 1:2], scales[:, 2:3], ALU.mult, ALU.mult).then_inc(tern_chain, 1)
            dve.wait_ge(tern_chain, 3)
            nc.vector.tensor_scalar(gain_f[:], s_prod[:, 0:1], gains[:, 2:3], 0.5, ALU.mult, ALU.mult)

            def ternary(dst, raw, w, below):
                if w:
                    dve.wait_ge(tern_set, w)
                nc.vector.tensor_scalar(below, raw, neg_half_s[:, w:w + 1], None, ALU.is_lt).then_inc(tern_chain, 1)
                dve.wait_ge(tern_chain, 4 + w)
                nc.vector.scalar_tensor_tensor(dst, raw, half_s[:, w:w + 1], below, ALU.is_gt, ALU.subtract).then_inc(tern_set, 1)

            tern_tmp = vals[:].rearrange("p t q d -> p (t q d)")
            ternary(w13[:, 0, :, 0:HID], raw13[:, 0], 0, tern_tmp[:, 0:2 * HID].rearrange("p (k e) -> p k e", k=KH))
            ternary(w13[:, 1, :, 0:HID], raw13[:, 1], 1, tern_tmp[:, 0:2 * HID].rearrange("p (k e) -> p k e", k=KH))
            ternary(w2[:], raw2, 2, tern_tmp[:, 0:HC * D].rearrange("p (c e) -> p c e", c=HC))
            low(2, down_l[:].rearrange("p c e -> p (c e)"), raw_down.rearrange("p c e -> p (c e)"), down_h[:].rearrange("p c e -> p (c e)"))
            low(3, route_l[:], route_w[:], route_h[:])
            low(4, gate_l[:].rearrange("p k c f -> p (k c f)"), raw_gate.rearrange("p k c f -> p (k c f)"),
                gate_h[:].rearrange("p k c f -> p (k c f)"))
            low(5, up_l[:].rearrange("p k c f -> p (k c f)"), raw_up.rearrange("p k c f -> p (k c f)"),
                up_h[:].rearrange("p k c f -> p (k c f)"))
            dve.wait_ge(low_set, 5)
            for h in range(KH):
                for c in (A2, E2, EV):
                    last = nc.vector.memset(flat(h, c).rearrange("p (b s) -> p b s", b=NS)[:, :, 0:1], 0.0)
            last.then_inc(scan_set, 1)

            def statistics(t, stage, n, rows_in, bn, mv):
                if not t.fixed or t.count(stage, 2, n) > 1:
                    dve.wait_ge(z_done[stage], t.count(stage, 2, n - 1))
                for r in range(NT):
                    last = nc.vector.bn_stats(bn[:, r], rows_in[:, r])
                last.then_inc(bn_done[stage], 1)
                dve.wait_ge(bn_done[stage], t.count(stage, 2, n))
                dve.sem_inc(bn_seen, 1)
                for r in range(NT):
                    last = nc.vector.bn_aggr(mv[:, r], bn[:, r])
                last.then_inc(mv_done[stage], 1)

            def low_parts(t, stage, which, high_part, low_part, done_high, n, per):
                for h in range(KH):
                    bank = wait_full(dve, t, stage, f"{which}{h}")
                    dve.wait_ge(done_high, t.count(stage, per, n + h + 1))
                    nc.vector.tensor_tensor(low_part[:, h], bank[:], high_part[:, h].bitcast(F32),
                                            ALU.subtract).then_inc(free_of(stage, f"{which}{h}"), 1)

            def row_max(t):
                bank = wait_full(dve, t, "A", "scores")
                nc.vector.tensor_reduce(smax[:], bank[:].rearrange("p (r k) -> p r k", r=NT), AX.X, ALU.max).then_inc(smax_set, 1)
                dve.wait_ge(smax_set, t.count("A", 1, 1))
                nc.vector.tensor_scalar(nsmax[:], smax[:], -SCALE, None, ALU.mult).then_inc(nsmax_set, 1)

            def row_scale(t):
                wait_taken(dve, t, "A", "scores")
                nc.vector.reciprocal(rinv[:], psum_row[:]).then_inc(rinv_set, 1)
                dve.wait_ge(rinv_set, t.count("A", 1, 1))
                nc.vector.tensor_scalar(rgain[:], rinv[:], gains[:, 0:1], None, ALU.mult).then_inc(rgain_set, 1)

            def add_attention(t):
                dve.wait_ge(rgain_set, t.count("A", 1, 1))
                for pair in range(2):
                    bank = wait_full(dve, t, "A", f"wo{pair}")
                    for r in range(2):
                        row = 2 * pair + r
                        last = nc.vector.scalar_tensor_tensor(xa[:, row], bank[:, r * D:(r + 1) * D], rgain[:, row:row + 1],
                                                              xa[:, row], ALU.mult, ALU.add)
                    last.then_inc(free_of("A", f"wo{pair}"), 1)

            def add_sums(t, stage, gain, rows_in, rows_out):
                dve.wait_ge(down_done, chunk_no(t, (stage, (MC if stage == "M" else HC) - 1)))
                if stage == "M" and (not t.fixed or t.count("M", 1, 0) > 0):
                    dve.wait_ge(out_done, t.count("M", 16, 0))
                for pair in range(2):
                    two = slice(2 * pair, 2 * pair + 2)
                    last = nc.vector.scalar_tensor_tensor(rows_out[:, two].rearrange("p r d -> p (r d)"), sums[pair][:], gain,
                                                          rows_in[:, two].rearrange("p r d -> p (r d)"), ALU.mult, ALU.add)
                last.then_inc(sums_free, 1)

            def gate(t, chunk):
                pos = CHUNKS.index(chunk) % 2
                n = chunk_no(t, chunk)
                dve.wait_ge(tanh_done, n)
                nc.vector.scalar_tensor_tensor(act_sb[:, pos], act_sb[:, pos], 1.0, gate_ps[pos][:], ALU.add, ALU.mult).then_inc(gated_one, 1)
                dve.wait_ge(gated_one, n)
                nc.vector.tensor_tensor(act_sb[:, pos], act_sb[:, pos], up_ps[pos][:], ALU.mult).then_inc(gated, 1)

            def running_max(t, h):
                wait_taken(dve, t, "W", f"z2T{h}")
                nc.vector.tensor_tensor_scan(flat(h, OMAX), decay_row[:, h].rearrange("p b s -> p (b s)"),
                                             kw[:, h].rearrange("p b s -> p (b s)"), NEG, ALU.add, ALU.max).then_inc(omax_set, 1)

            def exponents(t, h):
                dve.wait_ge(omax_set, t.count("W", KH, h + 1))
                nc.vector.scalar_tensor_tensor(seqs(h, A2, 1), seqs(h, OMAX, 0), decay_sb[:, h:h + 1], seqs(h, OMAX, 1),
                                               ALU.add, ALU.subtract).then_inc(a2arg_set, 1)
                nc.vector.scalar_tensor_tensor(flat(h, DELTA)[:, 0:TOK].rearrange("p (b s) -> p b s", b=NS), kw[:, h, :, 1:S1],
                                               bonus_sb[:, h:h + 1], seqs(h, OMAX, 0), ALU.add, ALU.subtract).then_inc(delta_set, 1)

            def clamps(t, h):
                dve.wait_ge(delta_set, t.count("W", KH, h + 1))
                nc.vector.tensor_scalar(flat(h, EA)[:, 0:TOK], flat(h, DELTA)[:, 0:TOK], 0.0, None, ALU.max).then_inc(clamp_set, 1)
                nc.vector.tensor_scalar(flat(h, EE)[:, 0:TOK], flat(h, DELTA)[:, 0:TOK], 0.0, None, ALU.min).then_inc(clamp_set, 1)

            def scans(t, h):
                dve.wait_ge(a2_set, t.count("W", KH, h + 1))
                dve.wait_ge(ev_set, t.count("W", KH, h + 1))
                nc.vector.tensor_tensor_scan(flat(h, EV), flat(h, A2), flat(h, EV), 0.0, ALU.mult, ALU.add).then_inc(scans_done, 1)
                nc.vector.tensor_tensor_scan(flat(h, E2), flat(h, A2), flat(h, E2), 0.0, ALU.mult, ALU.add).then_inc(scans_done, 1)

            def in_seqs(part):
                return part[:, 0:TOK].rearrange("p (b s) -> p b s", b=NS)

            def read_states(t, h):
                dve.wait_ge(ea_set, t.count("W", KH, h + 1))
                dve.wait_ge(scans_done, t.count("W", 2 * KH, 2 * h + 2))
                nc.vector.tensor_tensor(in_seqs(flat(h, DELTA)), in_seqs(flat(h, EA)), seqs(h, EV, 0), ALU.mult).then_inc(ap_set, 1)
                nc.vector.tensor_tensor(in_seqs(flat(h, EA)), in_seqs(flat(h, EA)), seqs(h, E2, 0), ALU.mult).then_inc(aq_set, 1)
                dve.wait_ge(eev_set, t.count("W", KH, h + 1))
                dve.wait_ge(ap_set, t.count("W", KH, h + 1))
                nc.vector.tensor_tensor(in_seqs(flat(h, DELTA)), in_seqs(flat(h, DELTA)), seqs(h, A2, 1), ALU.add).then_inc(num_set, 1)
                dve.wait_ge(aq_set, t.count("W", KH, h + 1))
                nc.vector.tensor_tensor(flat(h, EE)[:, 0:TOK], flat(h, EA)[:, 0:TOK], flat(h, EE)[:, 0:TOK], ALU.add).then_inc(den_set, 1)

            def divide(t, h, piece):
                part = flat(h, EE)[:, piece * TOK // 2:(piece + 1) * TOK // 2]
                dve.wait_ge(den_set, t.count("W", KH, h + 1))
                nc.vector.reciprocal(part, part).then_inc(dinv_set, 1)

            def quotient(t, h):
                dve.wait_ge(dinv_set, t.count("W", 2 * KH, 2 * h + 2))
                dve.wait_ge(num_set, t.count("W", KH, h + 1))
                nc.vector.tensor_tensor(vw[:, h], flat(h, DELTA)[:, 0:TOK], flat(h, EE)[:, 0:TOK], ALU.mult).then_inc(yw_set, 1)

            def add_recurrence(t):
                if t.on["M"]:
                    dve.wait_ge(sums_free, t.shared(SUMS, ("M", "y")))
                for pair in range(2):
                    bank = wait_full(dve, t, "W", f"yT{pair}")
                    two = slice(2 * pair, 2 * pair + 2)
                    last = nc.vector.scalar_tensor_tensor(x3[:, two].rearrange("p r d -> p (r d)"), bank[:], gains[:, 1:2],
                                                          x2[:, two].rearrange("p r d -> p (r d)"), ALU.mult, ALU.add)
                    last.then_inc(free_of("W", f"yT{pair}"), 1)

            def route(t):
                bank = wait_full(dve, t, "W", "route")
                logits = bank[:, 0:NT * E].rearrange("p (r e) -> p r e", r=NT)
                step = [0]

                def chained(ins):
                    step[0] += 1
                    ins.then_inc(route_chain, 1)
                    dve.wait_ge(route_chain, t.count("W", 7, step[0]))

                chained(nc.vector.tensor_reduce(lmax[:], logits, AX.X, ALU.max))
                nc.vector.tensor_tensor(pexp[:], logits, lmax[:].unsqueeze(2).broadcast_to([P, NT, E]), ALU.subtract).then_inc(free_of("W", "route"), 1)
                dve.wait_ge(pexp_set, t.count("W", 1, 1))
                mine = pexp[:].unsqueeze(3).broadcast_to([P, NT, E, E])
                other = pexp[:].unsqueeze(2).broadcast_to([P, NT, E, E])
                nc.vector.tensor_reduce(psum_e[:], pexp[:], AX.X, ALU.add)
                nc.vector.tensor_tensor(beats[:], other, mine, ALU.is_gt)
                chained(nc.vector.tensor_tensor(ties[:], other, mine, ALU.is_equal))
                chained(nc.vector.tensor_tensor(ties[:], ties[:], before[:].unsqueeze(1).broadcast_to([P, NT, E, E]), ALU.mult))
                chained(nc.vector.tensor_tensor(beats[:], beats[:], ties[:], ALU.add))
                nc.vector.reciprocal(pinv[:], psum_e[:])
                chained(nc.vector.tensor_reduce(ranks[:], beats[:], AX.X, ALU.add))
                chained(nc.vector.tensor_scalar(ranks[:], ranks[:], 1.5, None, ALU.is_lt))
                chained(nc.vector.tensor_tensor(ranks[:], ranks[:], pexp[:], ALU.mult))
                if t.on["M"]:
                    wait_taken(dve, t, "M", f"c{MC - 1}")
                nc.vector.tensor_tensor(combine[:], ranks[:], pinv[:].unsqueeze(2).broadcast_to([P, NT, E]), ALU.mult).then_inc(combine_set, 1)

            def turn(t):
                a, w, m = t.on["A"], t.on["W"], t.on["M"]

                def m_gate(c):
                    if m:
                        gate(t, ("M", c))
                if w:
                    dve.wait_ge(sums_free, t.before(SUMS))
                    statistics(t, "W", 1, x2, bn_w, mv_w)
                m_gate(0)
                if a:
                    dve.wait_ge(x_in, t.count("A", 16, 16))
                    statistics(t, "A", 1, xa, bn_a, mv_a)
                m_gate(1)
                if w:
                    for h in range(KH):
                        running_max(t, h)
                    for h in range(KH):
                        exponents(t, h)
                m_gate(2)
                if a:
                    low_parts(t, "A", "z0T", za_h, za_l, za_h_set, 0, 2 * KH)
                if w:
                    for h in range(KH):
                        clamps(t, h)
                m_gate(3)
                if w:
                    scans(t, 0)
                m_gate(4)
                if a:
                    row_max(t)
                if w:
                    scans(t, 1)
                m_gate(5)
                if a:
                    row_scale(t)
                if w:
                    read_states(t, 0)
                m_gate(6)
                if w:
                    read_states(t, 1)
                m_gate(7)
                if a:
                    add_attention(t)
                    wait_taken(dve, t, "A", "wo0", "wo1")
                    statistics(t, "A", 2, xa, bn_a, mv_a)
                if w:
                    divide(t, 0, 0)
                m_gate(8)
                if w:
                    divide(t, 0, 1)
                    quotient(t, 0)
                m_gate(9)
                if w:
                    divide(t, 1, 0)
                if a:
                    low_parts(t, "A", "z1T", za_h, za_l, za_h_set, KH, 2 * KH)
                if w:
                    divide(t, 1, 1)
                    quotient(t, 1)
                if a:
                    gate(t, ("A", 0))
                if m:
                    add_sums(t, "M", gain_m[:, 0:1], x3, out_row)
                if a:
                    gate(t, ("A", 1))
                if w:
                    add_recurrence(t)
                    wait_taken(dve, t, "W", "yT0", "yT1")
                    statistics(t, "W", 2, x3, bn_w, mv_w)
                if a:
                    gate(t, ("A", 2))
                    gate(t, ("A", 3))
                if w:
                    low_parts(t, "W", "z3T", zm_h, zm_l, zm_h_set, 0, KH)
                if a:
                    gate(t, ("A", 4))
                    gate(t, ("A", 5))
                if w:
                    route(t)
                if a:
                    add_sums(t, "A", gain_f[:, 0:1], xa, x2)

            turns(dve, turn)


def kernel(**inputs):
    import numpy as _np
    import concourse.bacc as _bacc
    from concourse import mybir as _mybir
    from concourse.bass_utils import run_bass_kernel_spmd as _run

    nc = _bacc.Bacc("TRN2", target_bir_lowering=False, num_devices=1)
    names = ["x", "ctx_2048", "g_xattn", "g_ffn", "L0_xattn_wq", "L0_xattn_wk", "L0_xattn_wv", "L0_xattn_wo", "L0_ffn_w1",
             "L0_ffn_w3", "L0_ffn_w2", "L1_xattn_w", "L1_xattn_u", "L1_ffn_router_w", "L1_ffn_shared_gate",
             "L1_ffn_shared_up", "L1_ffn_shared_down", "L1_ffn_w_gate", "L1_ffn_w_up", "L1_ffn_w_down"]
    turned = {"L0_xattn_wq", "L0_xattn_wk", "L0_xattn_wv", "L0_xattn_wo", "L0_ffn_w1", "L0_ffn_w3", "L0_ffn_w2"}
    arrays, args = {}, []
    for name in names:
        a = _np.asarray(inputs[name])
        a = _np.ascontiguousarray(a.T if name in turned else a)
        arrays[f"in_{name}"] = a
        args.append(nc.dram_tensor(f"in_{name}", a.shape, _mybir.dt.from_np(a.dtype), kind="ExternalInput").ap())
    shape = tuple(inputs["x"].shape)
    args.append(nc.dram_tensor("out_x", shape, _mybir.dt.float32, kind="ExternalOutput").ap())
    build(nc, *args)
    return _run(nc, [arrays], core_ids=[0]).results[0]["out_x"]
```

```python
from contextlib import ExitStack

import concourse.bass as bass
from concourse import mybir

ALU = mybir.AluOpType
ACT = mybir.ActivationFunctionType
AX = mybir.AxisListType
F32 = mybir.dt.float32
F32R = mybir.dt.float32r

P = 128
EPS = 1e-5
NEG = -1e38

TRANSIT = [
    ("A", "ctxT0"), ("A", "ctxT1"), ("M", "combT"), ("W", "z2T0"), ("W", "z2T1"), ("A", "z0T0"), ("A", "z0T1"),
    ("A", "q0"), ("A", "q1"), ("A", "k0"), ("A", "k1"), ("A", "v0"), ("A", "v1"), ("A", "scores"), ("A", "pT"),
    ("A", "oT0"), ("A", "oT1"), ("A", "wo0"), ("A", "wo1"), ("A", "z1T0"), ("A", "z1T1"), ("W", "yT0"), ("W", "yT1"),
    ("W", "z3T0"), ("W", "z3T1"), ("W", "route"),
]
CHUNKS = [("M", c) for c in range(10)] + [("A", c) for c in range(6)]
SUMS = [("M", "y"), ("A", "y")]
LAG = {"A": 0, "W": 1, "M": 2}


class Turn:

    def __init__(self, i, blocks, fixed):
        self.i, self.fixed = i, fixed
        self.on = {s: not fixed or 0 <= i - lag < blocks for s, lag in LAG.items()}
        self.blocks = blocks
        self.closing = fixed and i == blocks
        self.last = fixed and i == blocks + 1

    def count(self, stage, per, k):
        if self.fixed:
            return (self.i - LAG[stage]) * per + k
        return self.i * per + (k - LAG[stage] * per)

    def shared(self, order, name, bank=None):
        mine = [e for n, e in enumerate(order) if bank is None or n % 2 == bank]
        now = 0
        for e in mine:
            now += self.on[e[0]]
            if e == name:
                break
        if self.fixed:
            done = {s: min(max(self.i - lag, 0), self.blocks) for s, lag in LAG.items()}
            return sum(done[s] for s, _ in mine) + now
        return self.i * len(mine) + (now - sum(LAG[s] for s, _ in mine))

    def before(self, order):
        if self.fixed:
            return sum(min(max(self.i - LAG[s], 0), self.blocks) for s, _ in order)
        return self.i * len(order) - sum(LAG[s] for s, _ in order)


def build(nc, x, ctx_in, g_xattn, g_ffn, wqT, wkT, wvT, woT, w1T, w3T, w2T, decay, bonus, router,
          s_gate, s_up, s_down, e_gate, e_up, e_down, out, comb_dram):
    B, S, D = x.shape
    HID = w1T.shape[1]
    E, _, F = e_gate.shape
    NT = 4
    TOK = NT * P
    NB = B * S // TOK
    NS = TOK // S
    KH = D // P
    HC = -(-HID // P)
    HR = HID - (HC - 1) * P
    SC = s_gate.shape[1] // P
    MC = SC + E
    S1 = S + 1
    SCALE = float(D) ** -0.5
    assert (S, D, F, KH, HC, MC) == (64, 256, P, 2, 6, 10)

    def rows(a):
        return a.rearrange("b s d -> (b s) d").rearrange("(n t p) d -> n p t d", t=NT, p=P)

    x_rows, ctx_rows, out_rows = rows(x), rows(ctx_in), rows(out)
    ctx_seqs = ctx_in.rearrange("(n t q) s d -> n q s t d", t=NT, q=2)

    with ExitStack() as stack:
        def sb(name, shape, dt=F32):
            return stack.enter_context(nc.sbuf_tensor(name, shape, dt))

        def sem(name):
            return stack.enter_context(nc.semaphore(name))

        transit = [stack.enter_context(nc.psum_tensor(f"transit{n}", [P, TOK], F32)) for n in range(2)]
        gate_ps = [stack.enter_context(nc.psum_tensor(f"gate_ps{n}", [P, TOK], F32)) for n in range(2)]
        up_ps = [stack.enter_context(nc.psum_tensor(f"up_ps{n}", [P, TOK], F32)) for n in range(2)]
        sums = [stack.enter_context(nc.psum_tensor(f"sums{n}", [P, TOK], F32)) for n in range(2)]

        qkv_h = sb("qkv_h", [P, 3, KH, D], F32R)
        qkv_l = sb("qkv_l", [P, 3, KH, D], F32R)
        wo = sb("wo", [P, KH, D])
        w13 = sb("w13", [P, 2, KH, HC * P], F32R)
        w2 = sb("w2", [P, HC, D], F32R)
        gate_h = sb("gate_h", [P, KH, MC, P], F32R)
        gate_l = sb("gate_l", [P, KH, MC, P], F32R)
        up_h = sb("up_h", [P, KH, MC, P], F32R)
        up_l = sb("up_l", [P, KH, MC, P], F32R)
        down_h = sb("down_h", [P, MC, D], F32R)
        down_l = sb("down_l", [P, MC, D], F32R)
        route_w = sb("route_w", [P, KH, E])
        route_h = sb("route_h", [P, KH, E], F32R)
        route_l = sb("route_l", [P, KH, E], F32R)

        ident = sb("ident", [P, P])
        ones = sb("ones", [P, P])
        minus_half = sb("minus_half", [P, NT])
        minus_one = sb("minus_one", [P, NT])
        eps_row = sb("eps_row", [P, NT])
        before = sb("before", [P, E, E])
        gains = sb("gains", [P, 4])
        gain_m = sb("gain_m", [P, 1])
        gain_f = sb("gain_f", [P, 1])
        decay_sb = sb("decay_sb", [P, KH])
        bonus_sb = sb("bonus_sb", [P, KH])
        abs_sum = sb("abs_sum", [P, 3])
        scales = sb("scales", [P, 3])
        half_s = sb("half_s", [P, 3])
        neg_half_s = sb("neg_half_s", [P, 3])
        s_prod = sb("s_prod", [P, 2])

        xa = sb("xa", [P, NT, D])
        ctx_tok = sb("ctx_tok", [P, NT * D])
        probs = ctx_tok[:, 0:TOK].rearrange("p (t k) -> p t k", t=NT)
        probsT = ctx_tok[:, TOK:2 * TOK]
        ctx_row = ctx_tok[:, :].rearrange("p (t d) -> p t d", t=NT)
        vals = sb("vals", [P, NT, 2, D])
        keys = sb("keys", [P, KH, NT, 4, S])
        zqo = sb("zqo", [P, NT * D])
        za_row = zqo[:, :].rearrange("p (t d) -> p t d", t=NT)
        qo = zqo[:, :].rearrange("p (h n) -> p h n", h=KH)
        za_h = sb("za_h", [P, KH, TOK], F32R)
        za_l = sb("za_l", [P, KH, TOK], F32R)
        bn_a = sb("bn_a", [P, NT, 6])
        mv_a = sb("mv_a", [P, NT, 2])
        nmean_a = sb("nmean_a", [P, NT])
        var_a = sb("var_a", [P, NT])
        rstd_a = sb("rstd_a", [P, NT])
        shift_a = sb("shift_a", [P, NT])
        smax = sb("smax", [P, NT])
        nsmax = sb("nsmax", [P, NT])
        psum_row = sb("psum_row", [P, NT])
        rinv = sb("rinv", [P, NT])
        rgain = sb("rgain", [P, NT])

        x2 = sb("x2", [P, NT, D])
        vw = sb("vw", [P, KH, TOK])
        kw = sb("kw", [P, KH, NS, S1])
        decay_row = sb("decay_row", [P, KH, NS, S1])
        wide = NS * S1
        wk = sb("wk", [P, KH * 7 * wide])
        wk_parts = wk[:, :].rearrange("p (h c n) -> p h c n", h=KH, c=7)
        zw_row = wk[:, 4 * wide:4 * wide + NT * D].rearrange("p (t d) -> p t d", t=NT)
        bn_w = sb("bn_w", [P, NT, 6])
        mv_w = sb("mv_w", [P, NT, 2])
        nmean_w = sb("nmean_w", [P, NT])
        var_w = sb("var_w", [P, NT])
        rstd_w = sb("rstd_w", [P, NT])
        shift_w = sb("shift_w", [P, NT])

        def flat(h, c):
            return wk_parts[:, h, c, :]

        def seqs(h, c, first):
            return flat(h, c).rearrange("p (b s) -> p b s", b=NS)[:, :, first:first + S]

        OMAX, A2, E2, EV, DELTA, EA, EE = range(7)

        late = sb("late", [P, 3 * NT * D])
        x3, out_row = (late[:, n * NT * D:(n + 1) * NT * D].rearrange("p (t d) -> p t d", t=NT) for n in range(2))
        comb_sb = late[:, 2 * NT * D:].rearrange("p (a n) -> p a n", a=2)
        assert 2 * TOK == NT * D and MC * D <= 3 * NT * D
        zm_h = sb("zm_h", [P, KH, TOK], F32R)
        zm_l = sb("zm_l", [P, KH, TOK], F32R)
        lmax = sb("lmax", [P, NT])
        pexp = sb("pexp", [P, NT, E])
        psum_e = sb("psum_e", [P, NT])
        pinv = sb("pinv", [P, NT])
        rank = sb("rank", [P, NT])
        beats, ties = (flat(1, c)[:, 0:NT * E * E].rearrange("p (r e f) -> p r e f", r=NT, e=E) for c in (DELTA, EA))
        ranks = sb("ranks", [P, NT, E])
        combine = sb("combine", [P, NT, E])
        combT_sb = flat(0, OMAX)[0:E, 0:TOK]

        act_sb = sb("act_sb", [P, 2, TOK])
        hid_h = sb("hid_h", [P, 2, TOK], F32R)
        hid_l = sb("hid_l", [P, 2, TOK], F32R)

        consts_in, wo_in, route_in = sem("consts_in"), sem("wo_in"), sem("route_in")
        qkv_in = [sem(f"{name}_in") for name in ("wq", "wk", "wv")]
        tern_in, gate_in, up_in, down_in = sem("tern_in"), sem("gate_in"), sem("up_in"), sem("down_in")
        ident_zero, consts_set, gains_set, scan_zero, scan_set = (
            sem("ident_zero"), sem("consts_set"), sem("gains_set"), sem("scan_zero"), sem("scan_set"))
        abs_set, abs_all, tern_chain, tern_set = sem("abs_set"), sem("abs_all"), sem("tern_chain"), sem("tern_set")
        pads_set, high_set, low_set = sem("pads_set"), sem("high_set"), sem("low_set")
        x_in, ctx_row_in, ctx_val_in, out_done = sem("x_in"), sem("ctx_row_in"), sem("ctx_val_in"), sem("out_done")
        t_full = [sem(f"t_full{n}") for n in range(2)]
        t_free = [sem(f"t_free{n}") for n in range(2)]
        bn_done = {"A": sem("bn_done_a"), "W": sem("bn_done_w")}
        bn_seen = sem("bn_seen")
        mv_done = {"A": sem("mv_done_a"), "W": sem("mv_done_w")}
        var_done = {"A": sem("var_done_a"), "W": sem("var_done_w")}
        rstd_done = {"A": sem("rstd_done_a"), "W": sem("rstd_done_w")}
        shift_done = {"A": sem("shift_done_a"), "W": sem("shift_done_w")}
        z_done = {"A": sem("z_done_a"), "W": sem("z_done_w")}
        za_h_set, zm_h_set, smax_set, nsmax_set, rinv_set, rgain_set, vw_set = (
            sem("za_h_set"), sem("zm_h_set"), sem("smax_set"), sem("nsmax_set"), sem("rinv_set"), sem("rgain_set"), sem("vw_set"))
        omax_set, a2arg_set, e2arg_set, delta_set, clamp_set = (
            sem("omax_set"), sem("a2arg_set"), sem("e2arg_set"), sem("delta_set"), sem("clamp_set"))
        a2_set, e2_set, ea_set, ee_set, ev_set, scans_done, eev_set = (
            sem("a2_set"), sem("e2_set"), sem("ea_set"), sem("ee_set"), sem("ev_set"), sem("scans_done"), sem("eev_set"))
        ap_set, aq_set, num_set, den_set, dinv_set, yw_set = (
            sem("ap_set"), sem("aq_set"), sem("num_set"), sem("den_set"), sem("dinv_set"), sem("yw_set"))
        lmax_set, pexp_set, route_chain, combine_set, combT_out = (
            sem("lmax_set"), sem("pexp_set"), sem("route_chain"), sem("combine_set"), sem("combT_out"))
        comb_in = [sem(f"comb_in{n}") for n in range(2)]
        up_full, tanh_done, gated_one, gated, weighted, hid_h_set, hid_l_set, down_done, sums_free = (
            sem("up_full"), sem("tanh_done"), sem("gated_one"), sem("gated"), sem("weighted"), sem("hid_h_set"),
            sem("hid_l_set"), sem("down_done"), sem("sums_free"))

        def bank_of(use):
            return TRANSIT.index(use) % 2

        def wait_full(eng, t, stage, name):
            n = bank_of((stage, name))
            eng.wait_ge(t_full[n], t.shared(TRANSIT, (stage, name), n))
            return transit[n]

        def wait_taken(eng, t, stage, *names, claims=None):
            last = {bank_of((stage, name)): name for name in names}
            for n, name in last.items():
                if claims is None or n != bank_of(claims):
                    eng.wait_ge(t_free[n], t.shared(TRANSIT, (stage, name), n))

        def free_of(stage, name):
            return t_free[bank_of((stage, name))]

        def chunk_no(t, chunk):
            return t.shared(CHUNKS, chunk)

        def wait_back(eng, s, t, chunk, back):
            n = chunk_no(t, chunk) - back
            if not t.fixed or n > 0:
                eng.wait_ge(s, n)

        def scaled_chunk(t, c):
            return t.count("M", E, c - SC + 1)

        def between(t):
            return (xa, za_h, za_l) if t.closing else (x3, zm_h, zm_l)

        def experts_in(t):
            return (xa, za_h, za_l) if t.last else (x3, zm_h, zm_l)

        def turns(eng, body, closing, last):
            for i in range(3):
                body(Turn(i, NB, True))
            with eng.Fori(3, NB) as i:
                body(Turn(i, NB, False))
            closing(Turn(NB, NB, True))
            last(Turn(NB + 1, NB, True))

        n_qkv, n13, n2, MW = 3 * KH * D, 2 * KH * HID, HC * D, MC * D
        raw_qkv = wk[:, 0:n_qkv]
        raw13 = wk[:, n_qkv:n_qkv + n13].rearrange("p (w k e) -> p w k e", w=2, k=KH)
        raw2 = wk[:, n_qkv + n13:n_qkv + n13 + n2].rearrange("p (c e) -> p c e", c=HC)
        raw_gate, raw_up = (wk[:, n_qkv + n * MW:n_qkv + (n + 1) * MW] for n in range(2))
        raw_down = late[:, 0:MW]
        assert MW <= n13 and n_qkv + 2 * MW <= KH * 7 * wide
        spare13 = wk[:, n_qkv + n13 + n2:n_qkv + n13 + n2 + KH * HID].rearrange("p (k e) -> p k e", k=KH)
        spare2 = wk[:, 0:n2].rearrange("p (c e) -> p c e", c=HC)
        assert n_qkv + n13 + n2 + KH * HID <= KH * 7 * wide and n2 <= n_qkv

        SPLITS = {name: n + 1 for n, name in enumerate(("wq", "wk", "wv", "route", "down", "gate", "up"))}
        flat4 = "p k c f -> p (k c f)"
        parts = {
            "route": (route_w[:], route_h[:], route_l[:]),
            "gate": (raw_gate, gate_h[:].rearrange(flat4), gate_l[:].rearrange(flat4)),
            "up": (raw_up, up_h[:].rearrange(flat4), up_l[:].rearrange(flat4)),
            "down": (raw_down, down_h[:].rearrange("p c e -> p (c e)"), down_l[:].rearrange("p c e -> p (c e)")),
        }
        for n, name in enumerate(("wq", "wk", "wv")):
            parts[name] = (raw_qkv[:, n * KH * D:(n + 1) * KH * D], qkv_h[:, n].rearrange("p k e -> p (k e)"),
                           qkv_l[:, n].rearrange("p k e -> p (k e)"))
        loaded = {"wq": (qkv_in[0], 16), "wk": (qkv_in[1], 16), "wv": (qkv_in[2], 16), "route": (route_in, 16),
                  "gate": (gate_in, 32 * KH), "up": (up_in, 32 * KH), "down": (down_in, 32)}

        block = stack.enter_context(nc.Block())

        @block.sync
        def _(sp):
            def attention_weights():
                for n, w in enumerate((wqT, wkT, wvT)):
                    sp.dma_start(parts[f"w{'qkv'[n]}"][0].rearrange("p (k e) -> p k e", k=KH),
                                 w.rearrange("(k p) e -> p k e", p=P)).then_inc(qkv_in[n], 16)

            def other_weights():
                sp.dma_start(raw13[:, 0], w1T.rearrange("(k p) e -> p k e", p=P)).then_inc(tern_in, 16)
                sp.dma_start(raw13[:, 1], w3T.rearrange("(k p) e -> p k e", p=P)).then_inc(tern_in, 16)
                full = (HC - 1) * P
                sp.dma_start(raw2[:, 0:HC - 1], w2T[0:full].rearrange("(c p) e -> p c e", p=P)).then_inc(tern_in, 16)
                sp.wait_ge(pads_set, 2)
                sp.dma_start(raw2[0:HR, HC - 1], w2T[full:HID]).then_inc(tern_in, 16)
                sp.dma_start(decay_sb[:], decay.rearrange("(h p) -> p h", p=P), allow_slow_non_contiguous=True).then_inc(consts_in, 16)
                sp.dma_start(bonus_sb[:], bonus.rearrange("(h p) -> p h", p=P), allow_slow_non_contiguous=True).then_inc(consts_in, 16)
                sp.dma_start(gains[:, 0:2], g_xattn.partition_broadcast(P)).then_inc(consts_in, 16)
                sp.dma_start(gains[:, 2:4], g_ffn.partition_broadcast(P)).then_inc(consts_in, 16)
                sp.dma_start(wo[:], woT.rearrange("(k p) e -> p k e", p=P)).then_inc(wo_in, 16)
                sp.dma_start(route_w[:], router.rearrange("(k p) e -> p k e", p=P)).then_inc(route_in, 16)
                down = raw_down.rearrange("p (c e) -> p c e", c=MC)
                sp.dma_start(down[:, 0:SC], s_down.rearrange("(c p) e -> p c e", p=P)).then_inc(down_in, 16)
                sp.dma_start(down[:, SC:MC], e_down.rearrange("e f d -> f e d")).then_inc(down_in, 16)
                for n, (raw, shared, expert, s) in enumerate(((raw_gate, s_gate, e_gate, gate_in), (raw_up, s_up, e_up, up_in))):
                    sp.wait_ge(tern_set, n + 2)
                    four = raw.rearrange("p (k c f) -> p k c f", k=KH, c=MC)
                    for k in range(KH):
                        sp.dma_start(four[:, k, 0:SC], shared[k * P:(k + 1) * P].rearrange("p (c f) -> p c f", f=P)).then_inc(s, 16)
                        sp.dma_start(four[:, k, SC:MC], expert[:, k * P:(k + 1) * P].rearrange("e p f -> p e f")).then_inc(s, 16)

            def turn(t):
                first = t.fixed and t.i == 0
                if first:
                    sp.dma_start(xa[:], x_rows[0]).then_inc(x_in, 16)
                    attention_weights()
                if t.on["A"]:
                    if not first:
                        sp.wait_ge(rstd_done["A"], t.count("A", 2, 0))
                    sp.dma_start(ctx_row, ctx_rows[t.i]).then_inc(ctx_row_in, 16)
                    sp.dma_start(vals[S:P, :, 0], ctx_seqs[t.i, 0]).then_inc(ctx_val_in, 16)
                    sp.dma_start(vals[0:S, :, 1], ctx_seqs[t.i, 1]).then_inc(ctx_val_in, 16)
                    if not first:
                        sp.wait_ge(sums_free, t.before(SUMS))
                        sp.dma_start(xa[:], x_rows[t.i]).then_inc(x_in, 16)
                if first:
                    other_weights()
                if t.on["M"]:
                    wait_taken(sp, t, "M", "combT")
                    if not t.fixed or t.count("M", 1, 0) > 0:
                        for half in comb_in:
                            sp.wait_ge(half, t.count("M", 8 * E, 0))
                    sp.dma_start(comb_dram, combT_sb).then_inc(combT_out, 16)
                    sp.wait_ge(combT_out, t.count("M", 16, 16))
                    for c in range(SC, MC):
                        n = scaled_chunk(t, c)
                        if not t.fixed or n > 2:
                            sp.wait_ge(weighted, n - 2)
                        sp.dma_start(comb_sb[:, c % 2], comb_dram[c - SC].partition_broadcast(P)).then_inc(comb_in[c % 2], 16)
                    sp.wait_ge(sums_free, t.shared(SUMS, ("M", "y")))
                    sp.dma_start(out_rows[t.i - LAG["M"]], out_row[:]).then_inc(out_done, 16)

            turns(sp, turn, turn, turn)
            sp.wait_ge(out_done, 16 * NB)
            sp.wait_ge(combT_out, 16 * NB)

        @block.tensor
        def _(pe):
            pe.wait_ge(consts_set, 2)

            def weights_split(name):
                pe.wait_ge(low_set, SPLITS[name])

            def abs_sums():
                pe.wait_ge(abs_set, 6)
                nc.tensor.matmul(gate_ps[0][:, 0:3], ones[:], abs_sum[:], start=True, stop=True).then_inc(abs_all, 1)

            def claim(t, stage, name):
                n = bank_of((stage, name))
                before_me = t.shared(TRANSIT, (stage, name), n) - 1
                if not t.fixed or before_me > 0:
                    pe.wait_ge(t_free[n], before_me)
                return transit[n], t_full[n]

            def turn_rows(t, stage, name, source, h):
                bank, full = claim(t, stage, name)
                for r in range(NT):
                    last = nc.tensor.transpose(bank[:, r * P:(r + 1) * P], source[:, r, h * P:(h + 1) * P], ident[:])
                last.then_inc(full, 1)

            def split_product(o, lhs, rhs, first, final, group=True):
                (lh, ll), (rh, rl) = lhs, rhs
                pairs = [(lh, rh)] + ([(lh, rl)] if rl is not None else []) + ([(ll, rh)] if ll is not None else [])
                for n, (a, b) in enumerate(pairs):
                    last = nc.tensor.matmul(o, a, b, start=first and n == 0, stop=final and n == len(pairs) - 1,
                                            skip_group_check=not group)
                return last

            def context_T(t):
                pe.wait_ge(ctx_row_in, t.count("A", 16, 16))
                for h in range(KH):
                    turn_rows(t, "A", f"ctxT{h}", ctx_row, h)

            def z_T(t, stage, which, source, n):
                pe.wait_ge(z_done[stage], t.count(stage, 2, n))
                for h in range(KH):
                    turn_rows(t, stage, f"{which}{h}", source, h)

            def q_and_k(t):
                wait_taken(pe, t, "A", "z0T0", "z0T1", claims=("A", "q0"))
                for w, name in enumerate("qk"):
                    if t.fixed and t.i == 0:
                        weights_split(f"w{name}")
                    for m in range(KH):
                        bank, full = claim(t, "A", f"{name}{m}")
                        cols = slice(m * P, (m + 1) * P)
                        for k in range(KH):
                            last = split_product(bank[:], (qkv_h[:, w, k, cols], qkv_l[:, w, k, cols]),
                                                 (za_h[:, k], za_l[:, k]), k == 0, k == KH - 1)
                        last.then_inc(full, 1)

            def values(t):
                if t.fixed and t.i == 0:
                    weights_split("wv")
                for pair in range(2):
                    bank, full = claim(t, "A", f"v{pair}")
                    for r in range(2):
                        rows_ = slice((2 * pair + r) * P, (2 * pair + r + 1) * P)
                        for k in range(KH):
                            last = split_product(bank[:, r * D:(r + 1) * D], (za_h[:, k, rows_], za_l[:, k, rows_]),
                                                 (qkv_h[:, 2, k], qkv_l[:, 2, k]), k == 0, k == KH - 1)
                    last.then_inc(full, 1)

            def scores(t):
                wait_taken(pe, t, "A", "k0", "k1", claims=("A", "scores"))
                bank, full = claim(t, "A", "scores")
                for r in range(NT):
                    for q in range(2):
                        for h in range(KH):
                            last = nc.tensor.matmul(
                                bank[q * S:(q + 1) * S, r * P:(r + 1) * P], qo[:, h, (2 * r + q) * S:(2 * r + q + 1) * S],
                                keys[:, h, r, 2 * q:2 * q + 2].rearrange("p c s -> p (c s)"), start=h == 0, stop=h == KH - 1)
                last.then_inc(full, 1)

            def probs_T(t):
                wait_taken(pe, t, "A", "scores", claims=("A", "pT"))
                bank, full = claim(t, "A", "pT")
                for r in range(NT):
                    last = nc.tensor.transpose(bank[:, r * P:(r + 1) * P], probs[:, r], ident[:])
                last.then_inc(full, 1)

            def attend(t):
                wait_taken(pe, t, "A", "v0", "v1", "pT", claims=("A", "oT0"))
                pe.wait_ge(ctx_val_in, t.count("A", 32, 32))
                for h in range(KH):
                    bank, full = claim(t, "A", f"oT{h}")
                    for r in range(NT):
                        for q in range(2):
                            cols = slice((2 * r + q) * S, (2 * r + q + 1) * S)
                            last = nc.tensor.matmul(bank[:, cols], vals[:, r, q, h * P:(h + 1) * P], probsT[:, cols],
                                                    start=True, stop=True)
                    last.then_inc(full, 1)

            def project(t):
                wait_taken(pe, t, "A", "oT0", "oT1", claims=("A", "wo0"))
                if t.fixed and t.i == 0:
                    pe.wait_ge(wo_in, 16)
                for pair in range(2):
                    bank, full = claim(t, "A", f"wo{pair}")
                    for r in range(2):
                        for k in range(KH):
                            last = nc.tensor.matmul(bank[:, r * D:(r + 1) * D], qo[:, k, (2 * pair + r) * P:(2 * pair + r + 1) * P],
                                                    wo[:, k], start=k == 0, stop=k == KH - 1)
                    last.then_inc(full, 1)

            def y_T(t):
                pe.wait_ge(yw_set, t.count("W", KH, KH))
                for pair in range(2):
                    bank, full = claim(t, "W", f"yT{pair}")
                    for r in range(2):
                        for h in range(KH):
                            last = nc.tensor.transpose(bank[:, r * D + h * P:r * D + (h + 1) * P],
                                                       vw[:, h, (2 * pair + r) * P:(2 * pair + r + 1) * P], ident[:])
                    last.then_inc(full, 1)

            def route(t):
                wait_taken(pe, t, "W", "z3T0", "z3T1", claims=("W", "route"))
                if t.fixed and t.i == LAG["W"]:
                    weights_split("route")
                bank, full = claim(t, "W", "route")
                _, z_h, z_l = between(t)
                for r in range(NT):
                    rows_ = slice(r * P, (r + 1) * P)
                    for k in range(KH):
                        last = split_product(bank[:, r * E:(r + 1) * E], (z_h[:, k, rows_], z_l[:, k, rows_]),
                                             (route_h[:, k], route_l[:, k]), k == 0, k == KH - 1)
                last.then_inc(full, 1)

            def up(t, chunk):
                stage, c = chunk
                pos = CHUNKS.index(chunk) % 2
                wait_back(pe, gated, t, chunk, 2)
                if stage == "M":
                    _, z_h, z_l = experts_in(t)
                    for ps, wh, wl in ((gate_ps, gate_h, gate_l), (up_ps, up_h, up_l)):
                        for k in range(KH):
                            last = split_product(ps[pos][:], (wh[:, k, c], wl[:, k, c]), (z_h[:, k], z_l[:, k]),
                                                 k == 0, k == KH - 1)
                else:
                    if c == 0:
                        wait_taken(pe, t, "A", "z1T0", "z1T1")
                        if t.fixed and t.i == 0:
                            pe.wait_ge(tern_set, 3)
                    cols = slice(c * P, (c + 1) * P)
                    for w, ps in enumerate((gate_ps, up_ps)):
                        for k in range(KH):
                            last = split_product(ps[pos][:], (w13[:, w, k, cols], None), (za_h[:, k], za_l[:, k]),
                                                 k == 0, k == KH - 1)
                last.then_inc(up_full, 1)

            def combine_T(t):
                pe.wait_ge(combine_set, t.count("M", 1, 1))
                bank, full = claim(t, "M", "combT")
                for r in range(NT):
                    last = nc.tensor.transpose(bank[0:E, r * P:(r + 1) * P], combine[:, r], ident[:])
                last.then_inc(full, 1)

            def down(t, chunk):
                stage, c = chunk
                pos = CHUNKS.index(chunk) % 2
                final = c == (MC if stage == "M" else HC) - 1
                pe.wait_ge(hid_h_set, chunk_no(t, chunk))
                pe.wait_ge(hid_l_set, chunk_no(t, chunk))
                if c == 0:
                    n = t.shared(SUMS, (stage, "y")) - 1
                    if not t.fixed or n > 0:
                        pe.wait_ge(sums_free, n)
                w = (down_h[:, c], down_l[:, c]) if stage == "M" else (w2[:, c], None)
                for r in range(NT):
                    rows_ = slice(r * P, (r + 1) * P)
                    last = split_product(sums[r // 2][:, (r % 2) * D:(r % 2 + 1) * D],
                                         (hid_h[:, pos, rows_], hid_l[:, pos, rows_]), w, c == 0 and r % 2 == 0, final, group=False)
                last.then_inc(down_done, 1)

            def turn(t):
                a, w, m = t.on["A"], t.on["W"], t.on["M"]

                def m_up(*chunks):
                    for c in chunks if m else ():
                        up(t, ("M", c))

                def m_down(*chunks):
                    for c in chunks if m else ():
                        down(t, ("M", c))

                def f_up(c):
                    if a:
                        up(t, ("A", c))
                        if c >= 2:
                            down(t, ("A", c - 2))
                if t.fixed and t.i == LAG["M"]:
                    weights_split("up")
                m_up(0)
                if a:
                    context_T(t)
                m_up(1)
                if m:
                    combine_T(t)
                m_up(2)
                m_down(0)
                if w:
                    z_T(t, "W", "z2T", zw_row, 1)
                m_up(3)
                m_down(1)
                if a:
                    z_T(t, "A", "z0T", za_row, 1)
                m_up(4)
                m_down(2)
                if a:
                    q_and_k(t)
                    values(t)
                m_down(3)
                if t.fixed and t.i == 0:
                    abs_sums()
                if a:
                    scores(t)
                m_up(5)
                if a:
                    probs_T(t)
                m_down(4)
                if a:
                    attend(t)
                m_up(6)
                if a:
                    project(t)
                m_up(7)
                m_down(5)
                m_up(8)
                m_down(6)
                if a:
                    z_T(t, "A", "z1T", za_row, 2)
                m_up(9)
                m_down(7)
                f_up(0)
                m_down(8)
                f_up(1)
                m_down(9)
                if w:
                    y_T(t)
                f_up(2)
                f_up(3)
                f_up(4)
                f_up(5)
                if w:
                    z_T(t, "W", "z3T", zw_row, 2)
                if a:
                    down(t, ("A", HC - 2))
                if w:
                    route(t)
                if a:
                    down(t, ("A", HC - 1))

            def closing(t):
                def m_up(*chunks):
                    for c in chunks:
                        up(t, ("M", c))

                def m_down(*chunks):
                    for c in chunks:
                        down(t, ("M", c))
                m_up(0, 1)
                combine_T(t)
                m_up(2)
                m_down(0)
                z_T(t, "W", "z2T", zw_row, 1)
                for c in range(3, MC - 1):
                    m_up(c)
                    m_down(c - 2)
                m_up(MC - 1)
                y_T(t)
                m_down(MC - 3, MC - 2)
                z_T(t, "W", "z3T", zw_row, 2)
                m_down(MC - 1)
                route(t)

            def last(t):
                for c in range(MC):
                    up(t, ("M", c))
                    if c == 1:
                        combine_T(t)
                    if c >= 3:
                        down(t, ("M", c - 3))
                for c in range(MC - 3, MC):
                    down(t, ("M", c))

            turns(pe, turn, closing, last)

        @block.scalar
        def _(act):
            def high(name):
                act.wait_ge(*loaded[name])
                raw, high_part, _ = parts[name]
                nc.scalar.activation(high_part, raw, ACT.Copy).then_inc(high_set, 1)

            def normalise(t, stage, n, rows_in, rows_out, rstd, shift):
                act.wait_ge(shift_done[stage], t.count(stage, 2, n))
                for r in range(NT):
                    last = nc.scalar.activation(rows_out[:, r], rows_in[:, r], ACT.Identity, bias=shift[:, r:r + 1],
                                                scale=rstd[:, r:r + 1])
                last.then_inc(z_done[stage], 1)

            def high_parts(t, stage, which, dst, done):
                for h in range(KH):
                    bank = wait_full(act, t, stage, f"{which}{h}")
                    nc.scalar.activation(dst[:, h], bank[:], ACT.Copy).then_inc(done, 1)

            def context_T(t):
                if not t.fixed or t.i > 0:
                    act.wait_ge(vw_set, t.count("A", 1, 0))
                for h in range(KH):
                    bank = wait_full(act, t, "A", f"ctxT{h}")
                    nc.scalar.activation(keys[:, h, :, 1:3].rearrange("p t c s -> p t (c s)"),
                                         bank[:].rearrange("p (t n) -> p t n", t=NT), ACT.Copy).then_inc(free_of("A", f"ctxT{h}"), 1)

            def queries(t):
                for m in range(KH):
                    bank = wait_full(act, t, "A", f"q{m}")
                    nc.scalar.activation(qo[:, m], bank[:], ACT.Copy).then_inc(free_of("A", f"q{m}"), 1)

            def own_keys(t):
                for m in range(KH):
                    bank = wait_full(act, t, "A", f"k{m}")
                    nc.scalar.activation(keys[:, m, :, 0:4:3], bank[:].rearrange("p (t q s) -> p t q s", t=NT, q=2),
                                         ACT.Copy).then_inc(free_of("A", f"k{m}"), 1)

            def values(t):
                for pair in range(2):
                    bank = wait_full(act, t, "A", f"v{pair}")
                    for q in range(2):
                        half = slice(q * S, (q + 1) * S)
                        last = nc.scalar.activation(vals[half, 2 * pair:2 * pair + 2, q],
                                                    bank[half].rearrange("p (r d) -> p r d", r=2), ACT.Copy)
                    last.then_inc(free_of("A", f"v{pair}"), 1)

            def softmax(t):
                bank = wait_full(act, t, "A", "scores")
                act.wait_ge(nsmax_set, t.count("A", 1, 1))
                for r in range(NT):
                    last = nc.scalar.activation(probs[:, r], bank[:, r * P:(r + 1) * P], ACT.Exp, bias=nsmax[:, r:r + 1],
                                                scale=SCALE, accum_out=psum_row[:, r:r + 1])
                last.then_inc(free_of("A", "scores"), 1)

            def probs_T(t):
                bank = wait_full(act, t, "A", "pT")
                nc.scalar.activation(probsT, bank[:], ACT.Copy).then_inc(free_of("A", "pT"), 1)

            def attend(t):
                for h in range(KH):
                    bank = wait_full(act, t, "A", f"oT{h}")
                    nc.scalar.activation(qo[:, h], bank[:], ACT.Copy).then_inc(free_of("A", f"oT{h}"), 1)

            def k_wide(t):
                for h in range(KH):
                    bank = wait_full(act, t, "W", f"z2T{h}")
                    nc.scalar.activation(kw[:, h, :, 1:S1], bank[:].rearrange("p (b s) -> p b s", b=NS), ACT.Copy).then_inc(free_of("W", f"z2T{h}"), 1)

            def decays(t, h):
                act.wait_ge(a2arg_set, t.count("W", KH, h + 1))
                nc.scalar.activation(seqs(h, A2, 1), seqs(h, A2, 1), ACT.Exp).then_inc(a2_set, 1)
                act.wait_ge(e2arg_set, t.count("W", KH, h + 1))
                nc.scalar.activation(seqs(h, E2, 1), seqs(h, E2, 1), ACT.Exp).then_inc(e2_set, 1)

            def readouts(t, h):
                act.wait_ge(clamp_set, t.count("W", 2 * KH, 2 * h + 2))
                nc.scalar.activation(flat(h, EA)[:, 0:TOK], flat(h, EA)[:, 0:TOK], ACT.Exp, scale=-1.0).then_inc(ea_set, 1)
                nc.scalar.activation(flat(h, EE)[:, 0:TOK], flat(h, EE)[:, 0:TOK], ACT.Exp).then_inc(ee_set, 1)

            def route(t):
                wait_taken(act, t, "W", "route")
                nc.scalar.activation(pexp[:], pexp[:], ACT.Exp).then_inc(pexp_set, 1)

            def squash(t, chunk):
                stage, c = chunk
                pos = CHUNKS.index(chunk) % 2
                act.wait_ge(up_full, chunk_no(t, chunk))
                wait_back(act, hid_l_set, t, chunk, 2)
                nc.scalar.activation(act_sb[:, pos], gate_ps[pos][:], ACT.Tanh,
                                     scale=0.5 if stage == "M" else half_s[:, 0:1]).then_inc(tanh_done, 1)

            def combine_T(t):
                bank = wait_full(act, t, "M", "combT")
                nc.scalar.activation(combT_sb, bank[0:E], ACT.Copy).then_inc(free_of("M", "combT"), 1)

            def high_hidden(t, chunk):
                stage, c = chunk
                pos = CHUNKS.index(chunk) % 2
                if stage == "M" and c >= SC:
                    act.wait_ge(weighted, scaled_chunk(t, c))
                else:
                    act.wait_ge(gated, chunk_no(t, chunk))
                wait_back(act, down_done, t, chunk, 2)
                nc.scalar.activation(hid_h[:, pos], act_sb[:, pos], ACT.Copy).then_inc(hid_h_set, 1)

            def turn(t):
                first = t.fixed and t.i == 0
                a, w, m = t.on["A"], t.on["W"], t.on["M"]

                def m_high(c):
                    if m:
                        high_hidden(t, ("M", c))

                def m_chunk(c, high=True):
                    if m:
                        if c >= 1 and high:
                            high_hidden(t, ("M", c - 1))
                        squash(t, ("M", c))

                def f_chunk(c):
                    if a:
                        if c >= 1:
                            high_hidden(t, ("A", c - 1))
                        squash(t, ("A", c))
                if first:
                    for name in ("wq", "wk", "wv"):
                        high(name)
                m_chunk(0)
                if a:
                    context_T(t)
                m_chunk(1)
                if m:
                    combine_T(t)
                if w:
                    normalise(t, "W", 1, x2, zw_row, rstd_w, shift_w)
                m_chunk(2)
                if w:
                    k_wide(t)
                if a:
                    normalise(t, "A", 1, xa, za_row, rstd_a, shift_a)
                m_chunk(3)
                if a:
                    high_parts(t, "A", "z0T", za_h, za_h_set)
                m_chunk(4)
                if a:
                    queries(t)
                if w:
                    decays(t, 0)
                if a:
                    own_keys(t)
                if w:
                    decays(t, 1)
                    readouts(t, 0)
                if a:
                    values(t)
                if first:
                    act.wait_ge(consts_in, 64)
                    nc.scalar.activation(gains[:], gains[:], ACT.Tanh).then_inc(gains_set, 1)
                m_high(4)
                if a:
                    softmax(t)
                m_chunk(5, high=False)
                if a:
                    probs_T(t)
                if w:
                    readouts(t, 1)
                if a:
                    attend(t)
                if first:
                    for name in ("route", "down", "gate", "up"):
                        high(name)
                m_chunk(6)
                m_chunk(7)
                if a:
                    normalise(t, "A", 2, xa, za_row, rstd_a, shift_a)
                m_chunk(8)
                if a:
                    high_parts(t, "A", "z1T", za_h, za_h_set)
                m_chunk(9)
                if m:
                    high_hidden(t, ("M", MC - 1))
                if first:
                    act.wait_ge(tern_set, 3)
                f_chunk(0)
                f_chunk(1)
                f_chunk(2)
                f_chunk(3)
                f_chunk(4)
                if w:
                    normalise(t, "W", 2, x3, zw_row, rstd_w, shift_w)
                f_chunk(5)
                if w:
                    high_parts(t, "W", "z3T", zm_h, zm_h_set)
                if a:
                    high_hidden(t, ("A", HC - 1))
                if w:
                    route(t)
                if a:
                    if w:
                        wait_full(act, t, "W", "yT1")
                    for h in range(KH):
                        last = nc.scalar.activation(vw[:, h].rearrange("p (t n) -> p t n", t=NT),
                                                    keys[:, h, :, 1:3].rearrange("p t c s -> p t (c s)"), ACT.Copy)
                    last.then_inc(vw_set, 1)

            def closing(t):
                def m_chunk(c):
                    if c >= 1:
                        high_hidden(t, ("M", c - 1))
                    squash(t, ("M", c))
                m_chunk(0)
                m_chunk(1)
                combine_T(t)
                normalise(t, "W", 1, x2, zw_row, rstd_w, shift_w)
                m_chunk(2)
                k_wide(t)
                m_chunk(3)
                decays(t, 0)
                decays(t, 1)
                readouts(t, 0)
                m_chunk(4)
                readouts(t, 1)
                for c in range(5, MC - 1):
                    m_chunk(c)
                squash(t, ("M", MC - 1))
                high_hidden(t, ("M", MC - 2))
                normalise(t, "W", 2, between(t)[0], zw_row, rstd_w, shift_w)
                high_hidden(t, ("M", MC - 1))
                high_parts(t, "W", "z3T", between(t)[1], zm_h_set)
                route(t)

            def last(t):
                for c in range(MC):
                    squash(t, ("M", c))
                    if c == 1:
                        combine_T(t)
                    if c >= 1:
                        high_hidden(t, ("M", c - 1))
                high_hidden(t, ("M", MC - 1))

            turns(act, turn, closing, last)

        @block.gpsimd
        def _(pool):
            nc.gpsimd.memset(raw2[:, HC - 1], 0.0).then_inc(pads_set, 1)
            nc.gpsimd.memset(w13[:, :, :, HID:].bitcast(F32), 0.0).then_inc(pads_set, 1)
            nc.gpsimd.memset(ones[:], 1.0)
            nc.gpsimd.memset(minus_half[:], -0.5)
            nc.gpsimd.memset(minus_one[:], -1.0)
            nc.gpsimd.memset(eps_row[:], EPS)
            nc.gpsimd.memset(ident[:], 0.0).then_inc(ident_zero, 1)
            nc.gpsimd.memset(before[:], 1.0).then_inc(ident_zero, 1)
            pool.wait_ge(ident_zero, 2)
            nc.gpsimd.affine_select(out=before[:], in_=before[:], compare_op=ALU.is_gt, fill=0.0, base=0,
                                    pattern=[[1, E], [-1, E]], channel_multiplier=0).then_inc(consts_set, 1)
            nc.gpsimd.affine_select(out=ident[:], in_=ident[:], compare_op=ALU.not_equal, fill=1.0, base=0,
                                    pattern=[[-1, P]], channel_multiplier=1).then_inc(consts_set, 1)

            def row_factors(t, stage, n, stats, nmean, var, rstd, shift):
                pool.wait_ge(mv_done[stage], t.count(stage, 2, n))
                nc.gpsimd.tensor_tensor(var[:], stats[:, :, 1], eps_row[:], ALU.add).then_inc(var_done[stage], 1)
                nc.gpsimd.tensor_tensor(nmean[:], stats[:, :, 0], minus_one[:], ALU.mult)
                pool.wait_ge(var_done[stage], t.count(stage, 2, n))
                nc.gpsimd.tensor_tensor(rstd[:], var[:], minus_half[:], ALU.pow).then_inc(rstd_done[stage], 1)
                pool.wait_ge(rstd_done[stage], t.count(stage, 2, n))
                nc.gpsimd.tensor_tensor(shift[:], nmean[:], rstd[:], ALU.mult).then_inc(shift_done[stage], 1)

            def inputs(t, h):
                pool.wait_ge(omax_set, t.count("W", KH, h + 1))
                nc.gpsimd.tensor_tensor(seqs(h, E2, 1), kw[:, h, :, 1:S1], seqs(h, OMAX, 1), ALU.subtract).then_inc(e2arg_set, 1)

            def weigh_inputs(t, h):
                pool.wait_ge(e2_set, t.count("W", KH, h + 1))
                pool.wait_ge(vw_set, t.count("W", 1, 1))
                nc.gpsimd.tensor_tensor(seqs(h, EV, 1), seqs(h, E2, 1), vw[:, h].rearrange("p (b s) -> p b s", b=NS),
                                        ALU.mult).then_inc(ev_set, 1)

            def weigh_now(t, h):
                pool.wait_ge(ee_set, t.count("W", KH, h + 1))
                pool.wait_ge(scans_done, t.count("W", 2 * KH, 2 * h + 2))
                nc.gpsimd.tensor_tensor(seqs(h, A2, 1), flat(h, EE)[:, 0:TOK].rearrange("p (b s) -> p b s", b=NS),
                                        vw[:, h].rearrange("p (b s) -> p b s", b=NS), ALU.mult).then_inc(eev_set, 1)

            def low_hidden(t, chunk):
                pos = CHUNKS.index(chunk) % 2
                pool.wait_ge(hid_h_set, chunk_no(t, chunk))
                nc.gpsimd.tensor_tensor(hid_l[:, pos], act_sb[:, pos], hid_h[:, pos].bitcast(F32), ALU.subtract).then_inc(hid_l_set, 1)

            def weigh_chunk(t, chunk):
                c = chunk[1]
                pos = CHUNKS.index(chunk) % 2
                if c >= SC:
                    pool.wait_ge(gated, chunk_no(t, chunk))
                    pool.wait_ge(comb_in[c % 2], t.count("M", 8 * E, 16 * ((c - SC) // 2 + 1)))
                    nc.gpsimd.tensor_tensor(act_sb[:, pos], act_sb[:, pos], comb_sb[:, pos], ALU.mult).then_inc(weighted, 1)

            def turn(t):
                a, w, m = t.on["A"], t.on["W"], t.on["M"]

                def m_low(c):
                    if m:
                        low_hidden(t, ("M", c))

                def m_weigh(c):
                    if m:
                        weigh_chunk(t, ("M", c))
                if w:
                    row_factors(t, "W", 1, mv_w, nmean_w, var_w, rstd_w, shift_w)
                m_low(0)
                if a:
                    row_factors(t, "A", 1, mv_a, nmean_a, var_a, rstd_a, shift_a)
                m_low(1)
                m_weigh(2)
                if w:
                    for h in range(KH):
                        inputs(t, h)
                m_low(2)
                m_weigh(3)
                m_low(3)
                m_weigh(4)
                if w:
                    for h in range(KH):
                        weigh_inputs(t, h)
                m_low(4)
                m_weigh(5)
                if w:
                    weigh_now(t, 0)
                m_low(5)
                m_weigh(6)
                if w:
                    weigh_now(t, 1)
                m_low(6)
                if a:
                    row_factors(t, "A", 2, mv_a, nmean_a, var_a, rstd_a, shift_a)
                m_weigh(7)
                m_low(7)
                m_weigh(8)
                m_low(8)
                m_weigh(9)
                m_low(9)
                if a:
                    for c in range(3):
                        low_hidden(t, ("A", c))
                if w:
                    row_factors(t, "W", 2, mv_w, nmean_w, var_w, rstd_w, shift_w)
                if a:
                    for c in range(3, HC):
                        low_hidden(t, ("A", c))

            def closing(t):
                def m_low(c):
                    low_hidden(t, ("M", c))

                def m_weigh(c):
                    weigh_chunk(t, ("M", c))
                row_factors(t, "W", 1, mv_w, nmean_w, var_w, rstd_w, shift_w)
                m_low(0)
                m_low(1)
                m_weigh(2)
                for h in range(KH):
                    inputs(t, h)
                m_low(2)
                m_weigh(3)
                weigh_inputs(t, 0)
                m_low(3)
                weigh_inputs(t, 1)
                m_weigh(4)
                m_low(4)
                weigh_now(t, 0)
                m_weigh(5)
                m_low(5)
                weigh_now(t, 1)
                for c in range(6, MC - 1):
                    m_weigh(c)
                    m_low(c)
                row_factors(t, "W", 2, mv_w, nmean_w, var_w, rstd_w, shift_w)
                m_weigh(MC - 1)
                m_low(MC - 1)

            def last(t):
                for c in range(MC):
                    if c >= 1:
                        low_hidden(t, ("M", c - 1))
                    weigh_chunk(t, ("M", c))
                low_hidden(t, ("M", MC - 1))

            turns(pool, turn, closing, last)

        @block.vector
        def _(dve):
            def low(name):
                raw, high_part, low_part = parts[name]
                dve.wait_ge(high_set, SPLITS[name])
                nc.vector.tensor_tensor(low_part, raw, high_part.bitcast(F32), ALU.subtract).then_inc(low_set, 1)

            def decay_rows():
                nc.vector.memset(decay_row[:], 0.0).then_inc(scan_zero, 1)
                dve.wait_ge(consts_in, 64)
                dve.wait_ge(scan_zero, 1)
                for h in range(KH):
                    nc.vector.tensor_scalar(decay_row[:, h, :, 1:S1], decay_row[:, h, :, 1:S1], decay_sb[:, h:h + 1], None, ALU.add)
                nc.vector.memset(decay_row[:, :, :, 0:1], NEG)
                nc.vector.memset(kw[:, :, :, 0:1], NEG)

            def scan_slots():
                dve.wait_ge(low_set, SPLITS["up"])
                for h in range(KH):
                    for c in (A2, E2, EV):
                        last = nc.vector.memset(flat(h, c).rearrange("p (b s) -> p b s", b=NS)[:, :, 0:1], 0.0)
                last.then_inc(scan_set, 1)

            def ternary_scales():
                dve.wait_ge(gains_set, 1)
                nc.vector.tensor_scalar(gain_m[:], gains[:, 3:4], 0.5, None, ALU.mult)
                dve.wait_ge(abs_all, 1)
                abs_tot = gate_ps[0][:, 0:3]
                nc.vector.tensor_scalar(scales[:], abs_tot, 1.0 / (HID * D), None, ALU.mult)
                nc.vector.tensor_scalar(half_s[:], abs_tot, 0.5 / (HID * D), None, ALU.mult)
                nc.vector.tensor_scalar(neg_half_s[:], abs_tot, -0.5 / (HID * D), None, ALU.mult).then_inc(tern_chain, 1)
                dve.wait_ge(tern_chain, 1)
                nc.vector.tensor_scalar(s_prod[:, 0:1], scales[:, 0:1], scales[:, 1:2], scales[:, 2:3], ALU.mult, ALU.mult).then_inc(tern_chain, 1)
                dve.wait_ge(tern_chain, 2)
                nc.vector.tensor_scalar(gain_f[:], s_prod[:, 0:1], gains[:, 2:3], 0.5, ALU.mult, ALU.mult)

            TERNARY = [(w13[:, 0, :, 0:HID], raw13[:, 0], spare13), (w13[:, 1, :, 0:HID], raw13[:, 1], spare13), (w2[:], raw2, spare2)]

            def absolute_sums():
                dve.wait_ge(tern_in, 64)
                dve.wait_ge(low_set, SPLITS["wv"])
                for w, (_, raw, spare) in enumerate(TERNARY):
                    if w:
                        dve.wait_ge(abs_set, 2 * w)
                    nc.vector.scalar_tensor_tensor(spare, raw, -1.0, raw, ALU.mult, ALU.max).then_inc(abs_set, 1)
                    dve.wait_ge(abs_set, 2 * w + 1)
                    nc.vector.tensor_reduce(abs_sum[:, w:w + 1], spare, AX.XY, ALU.add).then_inc(abs_set, 1)

            def ternary_weights():
                dve.wait_ge(abs_set, 6)
                for w, (weight, raw, below) in enumerate(TERNARY):
                    if w:
                        dve.wait_ge(tern_set, w)
                    nc.vector.tensor_scalar(below, raw, neg_half_s[:, w:w + 1], None, ALU.is_lt).then_inc(tern_chain, 1)
                    dve.wait_ge(tern_chain, 3 + w)
                    nc.vector.scalar_tensor_tensor(weight, raw, half_s[:, w:w + 1], below, ALU.is_gt, ALU.subtract).then_inc(tern_set, 1)

            def statistics(t, stage, n, rows_in, bn, mv):
                if not t.fixed or t.count(stage, 2, n) > 1:
                    dve.wait_ge(z_done[stage], t.count(stage, 2, n - 1))
                for r in range(NT):
                    last = nc.vector.bn_stats(bn[:, r], rows_in[:, r])
                last.then_inc(bn_done[stage], 1)
                dve.wait_ge(bn_done[stage], t.count(stage, 2, n))
                dve.sem_inc(bn_seen, 1)
                for r in range(NT):
                    last = nc.vector.bn_aggr(mv[:, r], bn[:, r])
                last.then_inc(mv_done[stage], 1)

            def low_parts(t, stage, which, high_part, low_part, done_high, n, per):
                for h in range(KH):
                    bank = wait_full(dve, t, stage, f"{which}{h}")
                    dve.wait_ge(done_high, t.count(stage, per, n + h + 1))
                    nc.vector.tensor_tensor(low_part[:, h], bank[:], high_part[:, h].bitcast(F32),
                                            ALU.subtract).then_inc(free_of(stage, f"{which}{h}"), 1)

            def row_max(t):
                bank = wait_full(dve, t, "A", "scores")
                nc.vector.tensor_reduce(smax[:], bank[:].rearrange("p (r k) -> p r k", r=NT), AX.X, ALU.max).then_inc(smax_set, 1)
                dve.wait_ge(smax_set, t.count("A", 1, 1))
                nc.vector.tensor_scalar(nsmax[:], smax[:], -SCALE, None, ALU.mult).then_inc(nsmax_set, 1)

            def row_scale(t):
                wait_taken(dve, t, "A", "scores")
                nc.vector.reciprocal(rinv[:], psum_row[:]).then_inc(rinv_set, 1)
                dve.wait_ge(rinv_set, t.count("A", 1, 1))
                nc.vector.tensor_scalar(rgain[:], rinv[:], gains[:, 0:1], None, ALU.mult).then_inc(rgain_set, 1)

            def add_attention(t):
                dve.wait_ge(rgain_set, t.count("A", 1, 1))
                for pair in range(2):
                    bank = wait_full(dve, t, "A", f"wo{pair}")
                    for r in range(2):
                        row = 2 * pair + r
                        last = nc.vector.scalar_tensor_tensor(xa[:, row], bank[:, r * D:(r + 1) * D], rgain[:, row:row + 1],
                                                              xa[:, row], ALU.mult, ALU.add)
                    last.then_inc(free_of("A", f"wo{pair}"), 1)

            def add_sums(t, stage, gain, rows_in, rows_out):
                dve.wait_ge(down_done, chunk_no(t, (stage, (MC if stage == "M" else HC) - 1)))
                if stage == "M" and (not t.fixed or t.count("M", 1, 0) > 0):
                    dve.wait_ge(out_done, t.count("M", 16, 0))
                for pair in range(2):
                    two = slice(2 * pair, 2 * pair + 2)
                    last = nc.vector.scalar_tensor_tensor(rows_out[:, two].rearrange("p r d -> p (r d)"), sums[pair][:], gain,
                                                          rows_in[:, two].rearrange("p r d -> p (r d)"), ALU.mult, ALU.add)
                last.then_inc(sums_free, 1)

            def gate(t, chunk):
                pos = CHUNKS.index(chunk) % 2
                n = chunk_no(t, chunk)
                dve.wait_ge(tanh_done, n)
                nc.vector.scalar_tensor_tensor(act_sb[:, pos], act_sb[:, pos], 1.0, gate_ps[pos][:], ALU.add, ALU.mult).then_inc(gated_one, 1)
                dve.wait_ge(gated_one, n)
                nc.vector.tensor_tensor(act_sb[:, pos], act_sb[:, pos], up_ps[pos][:], ALU.mult).then_inc(gated, 1)

            def running_max(t, h):
                wait_taken(dve, t, "W", f"z2T{h}")
                if h == 0 and t.on["M"]:
                    dve.wait_ge(combT_out, t.count("M", 16, 16))
                nc.vector.tensor_tensor_scan(flat(h, OMAX), decay_row[:, h].rearrange("p b s -> p (b s)"),
                                             kw[:, h].rearrange("p b s -> p (b s)"), NEG, ALU.add, ALU.max).then_inc(omax_set, 1)

            def exponents(t, h):
                dve.wait_ge(omax_set, t.count("W", KH, h + 1))
                nc.vector.scalar_tensor_tensor(seqs(h, A2, 1), seqs(h, OMAX, 0), decay_sb[:, h:h + 1], seqs(h, OMAX, 1),
                                               ALU.add, ALU.subtract).then_inc(a2arg_set, 1)
                nc.vector.scalar_tensor_tensor(flat(h, DELTA)[:, 0:TOK].rearrange("p (b s) -> p b s", b=NS), kw[:, h, :, 1:S1],
                                               bonus_sb[:, h:h + 1], seqs(h, OMAX, 0), ALU.add, ALU.subtract).then_inc(delta_set, 1)

            def clamps(t, h):
                dve.wait_ge(delta_set, t.count("W", KH, h + 1))
                nc.vector.tensor_scalar(flat(h, EA)[:, 0:TOK], flat(h, DELTA)[:, 0:TOK], 0.0, None, ALU.max).then_inc(clamp_set, 1)
                nc.vector.tensor_scalar(flat(h, EE)[:, 0:TOK], flat(h, DELTA)[:, 0:TOK], 0.0, None, ALU.min).then_inc(clamp_set, 1)

            def scans(t, h):
                dve.wait_ge(a2_set, t.count("W", KH, h + 1))
                dve.wait_ge(ev_set, t.count("W", KH, h + 1))
                nc.vector.tensor_tensor_scan(flat(h, EV), flat(h, A2), flat(h, EV), 0.0, ALU.mult, ALU.add).then_inc(scans_done, 1)
                nc.vector.tensor_tensor_scan(flat(h, E2), flat(h, A2), flat(h, E2), 0.0, ALU.mult, ALU.add).then_inc(scans_done, 1)

            def in_seqs(part):
                return part[:, 0:TOK].rearrange("p (b s) -> p b s", b=NS)

            def read_states(t, h):
                dve.wait_ge(ea_set, t.count("W", KH, h + 1))
                dve.wait_ge(scans_done, t.count("W", 2 * KH, 2 * h + 2))
                nc.vector.tensor_tensor(in_seqs(flat(h, DELTA)), in_seqs(flat(h, EA)), seqs(h, EV, 0), ALU.mult).then_inc(ap_set, 1)
                nc.vector.tensor_tensor(in_seqs(flat(h, EA)), in_seqs(flat(h, EA)), seqs(h, E2, 0), ALU.mult).then_inc(aq_set, 1)

            def add_now(t, h):
                dve.wait_ge(eev_set, t.count("W", KH, h + 1))
                dve.wait_ge(ap_set, t.count("W", KH, h + 1))
                nc.vector.tensor_tensor(in_seqs(flat(h, DELTA)), in_seqs(flat(h, DELTA)), seqs(h, A2, 1), ALU.add).then_inc(num_set, 1)
                dve.wait_ge(aq_set, t.count("W", KH, h + 1))
                nc.vector.tensor_tensor(flat(h, EE)[:, 0:TOK], flat(h, EA)[:, 0:TOK], flat(h, EE)[:, 0:TOK], ALU.add).then_inc(den_set, 1)

            def divide(t, h, piece):
                part = flat(h, EE)[:, piece * TOK // 2:(piece + 1) * TOK // 2]
                dve.wait_ge(den_set, t.count("W", KH, h + 1))
                nc.vector.reciprocal(part, part).then_inc(dinv_set, 1)

            def quotient(t, h):
                dve.wait_ge(dinv_set, t.count("W", 2 * KH, 2 * h + 2))
                dve.wait_ge(num_set, t.count("W", KH, h + 1))
                nc.vector.tensor_tensor(vw[:, h], flat(h, DELTA)[:, 0:TOK], flat(h, EE)[:, 0:TOK], ALU.mult).then_inc(yw_set, 1)

            def add_recurrence(t):
                x3 = between(t)[0]
                if t.on["M"] and not t.closing:
                    dve.wait_ge(sums_free, t.shared(SUMS, ("M", "y")))
                for pair in range(2):
                    bank = wait_full(dve, t, "W", f"yT{pair}")
                    two = slice(2 * pair, 2 * pair + 2)
                    last = nc.vector.scalar_tensor_tensor(x3[:, two].rearrange("p r d -> p (r d)"), bank[:], gains[:, 1:2],
                                                          x2[:, two].rearrange("p r d -> p (r d)"), ALU.mult, ALU.add)
                    last.then_inc(free_of("W", f"yT{pair}"), 1)

            def route(t):
                bank = wait_full(dve, t, "W", "route")
                logits = bank[:, 0:NT * E].rearrange("p (r e) -> p r e", r=NT)
                step = [0]

                def chained(ins):
                    step[0] += 1
                    ins.then_inc(route_chain, 1)
                    dve.wait_ge(route_chain, t.count("W", 7, step[0]))

                chained(nc.vector.tensor_reduce(lmax[:], logits, AX.X, ALU.max))
                nc.vector.tensor_tensor(pexp[:], logits, lmax[:].unsqueeze(2).broadcast_to([P, NT, E]), ALU.subtract).then_inc(free_of("W", "route"), 1)
                dve.wait_ge(pexp_set, t.count("W", 1, 1))
                mine = pexp[:].unsqueeze(3).broadcast_to([P, NT, E, E])
                other = pexp[:].unsqueeze(2).broadcast_to([P, NT, E, E])
                nc.vector.tensor_reduce(psum_e[:], pexp[:], AX.X, ALU.add)
                nc.vector.tensor_tensor(beats[:], other, mine, ALU.is_gt)
                chained(nc.vector.tensor_tensor(ties[:], other, mine, ALU.is_equal))
                chained(nc.vector.tensor_tensor(ties[:], ties[:], before[:].unsqueeze(1).broadcast_to([P, NT, E, E]), ALU.mult))
                chained(nc.vector.tensor_tensor(beats[:], beats[:], ties[:], ALU.add))
                nc.vector.reciprocal(pinv[:], psum_e[:])
                chained(nc.vector.tensor_reduce(ranks[:], beats[:], AX.X, ALU.add))
                chained(nc.vector.tensor_scalar(ranks[:], ranks[:], 1.5, None, ALU.is_lt))
                chained(nc.vector.tensor_tensor(ranks[:], ranks[:], pexp[:], ALU.mult))
                if t.on["M"]:
                    wait_taken(dve, t, "M", "combT")
                nc.vector.tensor_tensor(combine[:], ranks[:], pinv[:].unsqueeze(2).broadcast_to([P, NT, E]), ALU.mult).then_inc(combine_set, 1)

            def turn(t):
                first, second = (t.fixed and t.i == n for n in (0, 1))
                a, w, m = t.on["A"], t.on["W"], t.on["M"]

                def m_gate(c):
                    if m:
                        gate(t, ("M", c))
                if w:
                    dve.wait_ge(sums_free, t.before(SUMS))
                    statistics(t, "W", 1, x2, bn_w, mv_w)
                m_gate(0)
                if a:
                    dve.wait_ge(x_in, t.count("A", 16, 16))
                    statistics(t, "A", 1, xa, bn_a, mv_a)
                if first:
                    for name in ("wq", "wk", "wv"):
                        low(name)
                m_gate(1)
                m_gate(2)
                if w:
                    if second:
                        scan_slots()
                        dve.wait_ge(scan_set, 1)
                    for h in range(KH):
                        running_max(t, h)
                    for h in range(KH):
                        exponents(t, h)
                m_gate(3)
                if a:
                    low_parts(t, "A", "z0T", za_h, za_l, za_h_set, 0, 2 * KH)
                if first:
                    absolute_sums()
                    decay_rows()
                if w:
                    for h in range(KH):
                        clamps(t, h)
                m_gate(4)
                if w:
                    scans(t, 0)
                    scans(t, 1)
                if a:
                    row_max(t)
                m_gate(5)
                if a:
                    row_scale(t)
                if first:
                    ternary_scales()
                    ternary_weights()
                    low("route")
                    low("down")
                if w:
                    read_states(t, 0)
                    add_now(t, 0)
                    divide(t, 0, 0)
                    divide(t, 0, 1)
                m_gate(6)
                if w:
                    quotient(t, 0)
                if a:
                    add_attention(t)
                    wait_taken(dve, t, "A", "wo0", "wo1")
                    statistics(t, "A", 2, xa, bn_a, mv_a)
                if first:
                    low("gate")
                    low("up")
                m_gate(7)
                if w:
                    read_states(t, 1)
                    add_now(t, 1)
                m_gate(8)
                if a:
                    low_parts(t, "A", "z1T", za_h, za_l, za_h_set, KH, 2 * KH)
                if w:
                    divide(t, 1, 0)
                m_gate(9)
                if w:
                    divide(t, 1, 1)
                    quotient(t, 1)
                if a:
                    gate(t, ("A", 0))
                if m:
                    add_sums(t, "M", gain_m[:, 0:1], x3, out_row)
                if a:
                    gate(t, ("A", 1))
                if w:
                    add_recurrence(t)
                if a:
                    gate(t, ("A", 2))
                if w:
                    wait_taken(dve, t, "W", "yT0", "yT1")
                    statistics(t, "W", 2, x3, bn_w, mv_w)
                if a:
                    gate(t, ("A", 3))
                    gate(t, ("A", 4))
                    gate(t, ("A", 5))
                if w:
                    low_parts(t, "W", "z3T", zm_h, zm_l, zm_h_set, 0, KH)
                if w:
                    route(t)
                if a:
                    add_sums(t, "A", gain_f[:, 0:1], xa, x2)

            def closing(t):
                def m_gate(c):
                    gate(t, ("M", c))
                rows, z_h, z_l = between(t)
                dve.wait_ge(sums_free, t.before(SUMS))
                statistics(t, "W", 1, x2, bn_w, mv_w)
                m_gate(0)
                m_gate(1)
                m_gate(2)
                for h in range(KH):
                    running_max(t, h)
                for h in range(KH):
                    exponents(t, h)
                m_gate(3)
                for h in range(KH):
                    clamps(t, h)
                m_gate(4)
                for h in range(KH):
                    scans(t, h)
                for h in range(KH):
                    read_states(t, h)
                m_gate(5)
                add_now(t, 0)
                divide(t, 0, 0)
                divide(t, 0, 1)
                m_gate(6)
                quotient(t, 0)
                add_now(t, 1)
                divide(t, 1, 0)
                m_gate(7)
                divide(t, 1, 1)
                quotient(t, 1)
                m_gate(8)
                add_recurrence(t)
                wait_taken(dve, t, "W", "yT0", "yT1")
                statistics(t, "W", 2, rows, bn_w, mv_w)
                m_gate(9)
                low_parts(t, "W", "z3T", z_h, z_l, zm_h_set, 0, KH)
                route(t)
                add_sums(t, "M", gain_m[:, 0:1], x3, out_row)

            def last(t):
                for c in range(MC):
                    gate(t, ("M", c))
                add_sums(t, "M", gain_m[:, 0:1], experts_in(t)[0], out_row)

            turns(dve, turn, closing, last)


def kernel(**inputs):
    import numpy as _np
    import concourse.bacc as _bacc
    from concourse import mybir as _mybir
    from concourse.bass_utils import run_bass_kernel_spmd as _run

    nc = _bacc.Bacc("TRN2", target_bir_lowering=False, num_devices=1)
    names = ["x", "ctx_2048", "g_xattn", "g_ffn", "L0_xattn_wq", "L0_xattn_wk", "L0_xattn_wv", "L0_xattn_wo", "L0_ffn_w1",
             "L0_ffn_w3", "L0_ffn_w2", "L1_xattn_w", "L1_xattn_u", "L1_ffn_router_w", "L1_ffn_shared_gate",
             "L1_ffn_shared_up", "L1_ffn_shared_down", "L1_ffn_w_gate", "L1_ffn_w_up", "L1_ffn_w_down"]
    turned = {"L0_xattn_wq", "L0_xattn_wk", "L0_xattn_wv", "L0_xattn_wo", "L0_ffn_w1", "L0_ffn_w3", "L0_ffn_w2"}
    arrays, args = {}, []
    for name in names:
        a = _np.asarray(inputs[name])
        a = _np.ascontiguousarray(a.T if name in turned else a)
        arrays[f"in_{name}"] = a
        args.append(nc.dram_tensor(f"in_{name}", a.shape, _mybir.dt.from_np(a.dtype), kind="ExternalInput").ap())
    shape = tuple(inputs["x"].shape)
    args.append(nc.dram_tensor("out_x", shape, _mybir.dt.float32, kind="ExternalOutput").ap())
    args.append(nc.dram_tensor("combine_rows", (8, 512), _mybir.dt.float32, kind="Internal").ap())
    build(nc, *args)
    return _run(nc, [arrays], core_ids=[0]).results[0]["out_x"]
```

```python
from contextlib import ExitStack

import concourse.bass as bass
from concourse import mybir

ALU = mybir.AluOpType
ACT = mybir.ActivationFunctionType
AX = mybir.AxisListType
F32 = mybir.dt.float32
F32R = mybir.dt.float32r

P = 128
EPS = 1e-5
NEG = -1e38

TRANSIT = [
    ("A", "ctxT0"), ("A", "ctxT1"), ("M", "combT"), ("W", "z2T0"), ("W", "z2T1"), ("A", "z0T0"), ("A", "z0T1"),
    ("A", "q0"), ("A", "q1"), ("A", "k0"), ("A", "k1"), ("A", "v0"), ("A", "v1"), ("A", "scores"), ("A", "pT"),
    ("A", "oT0"), ("A", "oT1"), ("A", "wo0"), ("A", "wo1"), ("A", "z1T0"), ("A", "z1T1"), ("W", "yT0"), ("W", "yT1"),
    ("W", "z3T0"), ("W", "z3T1"), ("W", "route"),
]
SECOND = [("A", "z0T0"), ("A", "z0T1"), ("A", "q0"), ("A", "q1"), ("A", "k0"), ("A", "k1"), ("A", "v0"), ("A", "v1"),
          ("A", "ctxT0"), ("A", "ctxT1"), ("W", "z2T0"), ("W", "z2T1")] + TRANSIT[TRANSIT.index(("A", "scores")):]
CHUNKS = [("M", c) for c in range(10)] + [("A", c) for c in range(6)]
SUMS = [("M", "y"), ("A", "y")]
LAG = {"A": 0, "W": 1, "M": 2}


class Turn:

    def __init__(self, i, blocks, fixed):
        self.i, self.fixed = i, fixed
        self.on = {s: not fixed or 0 <= i - lag < blocks for s, lag in LAG.items()}
        self.blocks = blocks
        self.second = fixed and i == 1
        self.closing = fixed and i == blocks
        self.last = fixed and i == blocks + 1

    def count(self, stage, per, k):
        if self.fixed:
            return (self.i - LAG[stage]) * per + k
        return self.i * per + (k - LAG[stage] * per)

    def shared(self, order, name, bank=None):
        mine = [e for n, e in enumerate(order) if bank is None or n % 2 == bank]
        if order is TRANSIT and self.second:
            mine = [e for e in SECOND if e in mine]
        now = 0
        for e in mine:
            now += self.on[e[0]]
            if e == name:
                break
        if self.fixed:
            done = {s: min(max(self.i - lag, 0), self.blocks) for s, lag in LAG.items()}
            return sum(done[s] for s, _ in mine) + now
        return self.i * len(mine) + (now - sum(LAG[s] for s, _ in mine))

    def before(self, order):
        if self.fixed:
            return sum(min(max(self.i - LAG[s], 0), self.blocks) for s, _ in order)
        return self.i * len(order) - sum(LAG[s] for s, _ in order)


def build(nc, x, ctx_in, g_xattn, g_ffn, wqT, wkT, wvT, woT, w1T, w3T, w2T, decay, bonus, router,
          s_gate, s_up, s_down, e_gate, e_up, e_down, out, comb_dram):
    B, S, D = x.shape
    HID = w1T.shape[1]
    E, _, F = e_gate.shape
    NT = 4
    TOK = NT * P
    NB = B * S // TOK
    NS = TOK // S
    KH = D // P
    HC = -(-HID // P)
    HR = HID - (HC - 1) * P
    HALF = P // 2
    assert HR <= HALF
    SC = s_gate.shape[1] // P
    MC = SC + E
    S1 = S + 1
    SCALE = float(D) ** -0.5
    assert (S, D, F, KH, HC, MC) == (64, 256, P, 2, 6, 10)

    def rows(a):
        return a.rearrange("b s d -> (b s) d").rearrange("(n t p) d -> n p t d", t=NT, p=P)

    x_rows, ctx_rows, out_rows = rows(x), rows(ctx_in), rows(out)
    ctx_seqs = ctx_in.rearrange("(n t q) s d -> n q s t d", t=NT, q=2)

    with ExitStack() as stack:
        def sb(name, shape, dt=F32):
            return stack.enter_context(nc.sbuf_tensor(name, shape, dt))

        def sem(name):
            return stack.enter_context(nc.semaphore(name))

        transit = [stack.enter_context(nc.psum_tensor(f"transit{n}", [P, TOK], F32)) for n in range(2)]
        gate_ps = [stack.enter_context(nc.psum_tensor(f"gate_ps{n}", [P, TOK], F32)) for n in range(2)]
        up_ps = [stack.enter_context(nc.psum_tensor(f"up_ps{n}", [P, TOK], F32)) for n in range(2)]
        sums = [stack.enter_context(nc.psum_tensor(f"sums{n}", [P, TOK], F32)) for n in range(2)]

        qkv_h = sb("qkv_h", [P, 3, KH, D], F32R)
        qkv_l = sb("qkv_l", [P, 3, KH, D], F32R)
        wo = sb("wo", [P, KH, D])
        w13 = sb("w13", [P, 2, KH, HC * P], F32R)
        w2 = sb("w2", [P, HC, D], F32R)
        gate_h = sb("gate_h", [P, KH, MC, P], F32R)
        gate_l = sb("gate_l", [P, KH, MC, P], F32R)
        up_h = sb("up_h", [P, KH, MC, P], F32R)
        up_l = sb("up_l", [P, KH, MC, P], F32R)
        down_h = sb("down_h", [P, MC, D], F32R)
        down_l = sb("down_l", [P, MC, D], F32R)
        route_w = sb("route_w", [P, KH, E])
        route_hl = sb("route_hl", [P, KH, 2, E], F32R)

        ident = sb("ident", [P, P])
        ones = sb("ones", [P, P])
        minus_half = sb("minus_half", [P, NT])
        minus_one = sb("minus_one", [P, NT])
        eps_row = sb("eps_row", [P, NT])
        before = sb("before", [P, E, E])
        gains = sb("gains", [P, 4])
        gain_m = sb("gain_m", [P, 1])
        gain_f = sb("gain_f", [P, 1])
        decay_sb = sb("decay_sb", [P, KH])
        bonus_sb = sb("bonus_sb", [P, KH])
        abs_sum = sb("abs_sum", [P, 3])
        scales = sb("scales", [P, 3])
        half_s = sb("half_s", [P, 3])
        neg_half_s = sb("neg_half_s", [P, 3])
        s_prod = sb("s_prod", [P, 2])

        xa = sb("xa", [P, NT, D])
        ctx_tok = sb("ctx_tok", [P, NT * D])
        probs = ctx_tok[:, 0:TOK].rearrange("p (t k) -> p t k", t=NT)
        probsT = ctx_tok[:, TOK:2 * TOK]
        ctx_row = ctx_tok[:, :].rearrange("p (t d) -> p t d", t=NT)
        vals = sb("vals", [P, NT, 2, D])
        keys = sb("keys", [P, KH, NT, 4, S])
        zqo = sb("zqo", [P, NT * D])
        za_row = zqo[:, :].rearrange("p (t d) -> p t d", t=NT)
        qo = zqo[:, :].rearrange("p (h n) -> p h n", h=KH)
        za_h = sb("za_h", [P, KH, TOK], F32R)
        za_l = sb("za_l", [P, KH, TOK], F32R)
        bn_a = sb("bn_a", [P, NT, 6])
        mv_a = sb("mv_a", [P, NT, 2])
        nmean_a = sb("nmean_a", [P, NT])
        var_a = sb("var_a", [P, NT])
        rstd_a = sb("rstd_a", [P, NT])
        shift_a = sb("shift_a", [P, NT])
        smax = sb("smax", [P, NT])
        nsmax = sb("nsmax", [P, NT])
        psum_row = sb("psum_row", [P, NT])
        rinv = sb("rinv", [P, NT])
        rgain = sb("rgain", [P, NT])

        x2 = sb("x2", [P, NT, D])
        vw = sb("vw", [P, KH, TOK])
        kw = sb("kw", [P, KH, NS, S1])
        decay_row = sb("decay_row", [P, KH, NS, S1])
        wide = NS * S1
        wk = sb("wk", [P, KH * 7 * wide])
        wk_parts = wk[:, :].rearrange("p (h c n) -> p h c n", h=KH, c=7)
        zw_row = wk[:, 4 * wide:4 * wide + NT * D].rearrange("p (t d) -> p t d", t=NT)
        bn_w = sb("bn_w", [P, NT, 6])
        mv_w = sb("mv_w", [P, NT, 2])
        nmean_w = sb("nmean_w", [P, NT])
        var_w = sb("var_w", [P, NT])
        rstd_w = sb("rstd_w", [P, NT])
        shift_w = sb("shift_w", [P, NT])

        def flat(h, c):
            return wk_parts[:, h, c, :]

        def seqs(h, c, first):
            return flat(h, c).rearrange("p (b s) -> p b s", b=NS)[:, :, first:first + S]

        OMAX, A2, E2, EV, DELTA, EA, EE = range(7)

        late = sb("late", [P, 3 * NT * D])
        x3, out_row = (late[:, n * NT * D:(n + 1) * NT * D].rearrange("p (t d) -> p t d", t=NT) for n in range(2))
        comb_sb = late[:, 2 * NT * D:].rearrange("p (a n) -> p a n", a=2)
        assert 2 * TOK == NT * D and MC * D <= 3 * NT * D
        zm_h = sb("zm_h", [P, KH, TOK], F32R)
        zm_l = sb("zm_l", [P, KH, TOK], F32R)
        logits = sb("logits", [P, NT, E])
        lmax = sb("lmax", [P, NT])
        pexp = sb("pexp", [P, NT, E])
        psum_e = sb("psum_e", [P, NT])
        pinv = sb("pinv", [P, NT])
        rank = sb("rank", [P, NT])
        beats, ties = (flat(1, c)[:, 0:NT * E * E].rearrange("p (r e f) -> p r e f", r=NT, e=E) for c in (DELTA, EA))
        ranks = sb("ranks", [P, NT, E])
        combine = sb("combine", [P, NT, E])
        combT_sb = flat(0, OMAX)[0:E, 0:TOK]

        act_sb = sb("act_sb", [P, 2, TOK])
        hid_h = sb("hid_h", [P, 2, TOK], F32R)
        hid_l = sb("hid_l", [P, 2, TOK], F32R)

        consts_in, wo_in, route_in = sem("consts_in"), sem("wo_in"), sem("route_in")
        qkv_in = [sem(f"{name}_in") for name in ("wq", "wk", "wv")]
        tern_in, gate_in, up_in, down_in = sem("tern_in"), sem("gate_in"), sem("up_in"), sem("down_in")
        ident_zero, consts_set, gains_set, scan_zero, scan_set = (
            sem("ident_zero"), sem("consts_set"), sem("gains_set"), sem("scan_zero"), sem("scan_set"))
        abs_set, abs_w2_set, abs_all, tern_chain, tern_set = (
            sem("abs_set"), sem("abs_w2_set"), sem("abs_all"), sem("tern_chain"), sem("tern_set"))
        pads_set, high_set, low_set = sem("pads_set"), sem("high_set"), sem("low_set")
        x_in, ctx_row_in, ctx_val_in, out_done = sem("x_in"), sem("ctx_row_in"), sem("ctx_val_in"), sem("out_done")
        t_full = [sem(f"t_full{n}") for n in range(2)]
        t_free = [sem(f"t_free{n}") for n in range(2)]
        bn_done = {"A": sem("bn_done_a"), "W": sem("bn_done_w")}
        bn_seen = sem("bn_seen")
        mv_done = {"A": sem("mv_done_a"), "W": sem("mv_done_w")}
        var_done = {"A": sem("var_done_a"), "W": sem("var_done_w")}
        rstd_done = {"A": sem("rstd_done_a"), "W": sem("rstd_done_w")}
        shift_done = {"A": sem("shift_done_a"), "W": sem("shift_done_w")}
        z_done = {"A": sem("z_done_a"), "W": sem("z_done_w")}
        za_h_set, zm_h_set, smax_set, nsmax_set, rinv_set, rgain_set, vw_set = (
            sem("za_h_set"), sem("zm_h_set"), sem("smax_set"), sem("nsmax_set"), sem("rinv_set"), sem("rgain_set"), sem("vw_set"))
        omax_set, a2arg_set, e2arg_set, delta_set, clamp_set = (
            sem("omax_set"), sem("a2arg_set"), sem("e2arg_set"), sem("delta_set"), sem("clamp_set"))
        a2_set, e2_set, ea_set, ee_set, ev_set, scans_done, eev_set = (
            sem("a2_set"), sem("e2_set"), sem("ea_set"), sem("ee_set"), sem("ev_set"), sem("scans_done"), sem("eev_set"))
        ap_set, aq_set, num_set, den_set, dinv_set, yw_set = (
            sem("ap_set"), sem("aq_set"), sem("num_set"), sem("den_set"), sem("dinv_set"), sem("yw_set"))
        lmax_set, pexp_set, route_chain, combine_set, combT_out = (
            sem("lmax_set"), sem("pexp_set"), sem("route_chain"), sem("combine_set"), sem("combT_out"))
        rows_kept = sem("rows_kept")
        comb_in = [sem(f"comb_in{n}") for n in range(2)]
        up_full, tanh_done, gated_one, gated, weighted, hid_h_set, hid_l_set, down_done, sums_free = (
            sem("up_full"), sem("tanh_done"), sem("gated_one"), sem("gated"), sem("weighted"), sem("hid_h_set"),
            sem("hid_l_set"), sem("down_done"), sem("sums_free"))

        def bank_of(use):
            return TRANSIT.index(use) % 2

        def wait_full(eng, t, stage, name):
            n = bank_of((stage, name))
            eng.wait_ge(t_full[n], t.shared(TRANSIT, (stage, name), n))
            return transit[n]

        def wait_taken(eng, t, stage, *names, claims=None):
            last = {bank_of((stage, name)): name for name in names}
            for n, name in last.items():
                if claims is None or n != bank_of(claims):
                    eng.wait_ge(t_free[n], t.shared(TRANSIT, (stage, name), n))

        def free_of(stage, name):
            return t_free[bank_of((stage, name))]

        def is_tail(chunk):
            return chunk == ("A", HC - 1)

        def hidden_rows(chunk):
            return HALF if is_tail(chunk) else P

        def chunk_no(t, chunk):
            return t.shared(CHUNKS, chunk)

        def wait_back(eng, s, t, chunk, back):
            n = chunk_no(t, chunk) - back
            if not t.fixed or n > 0:
                eng.wait_ge(s, n)

        def scaled_chunk(t, c):
            return t.count("M", E, c - SC + 1)

        def recurrence_out(t):
            return (xa, za_h, za_l) if t.closing else (x2, zm_h, zm_l)

        def experts_in(t):
            return (xa, za_h, za_l) if t.last else (x3, zm_h, zm_l)

        def attention_rows(t):
            return out_row if t.second else xa

        def turns(eng, body, second, closing, last):
            body(Turn(0, NB, True))
            second(Turn(1, NB, True))
            body(Turn(2, NB, True))
            with eng.Fori(3, NB) as i:
                body(Turn(i, NB, False))
            closing(Turn(NB, NB, True))
            last(Turn(NB + 1, NB, True))

        n_qkv, n13, n2, MW = 3 * KH * D, 2 * KH * HID, HC * D, MC * D
        raw_qkv = wk[:, 0:n_qkv]
        raw13 = wk[:, n_qkv:n_qkv + n13].rearrange("p (w k e) -> p w k e", w=2, k=KH)
        raw2 = wk[:, n_qkv + n13:n_qkv + n13 + n2].rearrange("p (c e) -> p c e", c=HC)
        raw_gate, raw_up = (wk[:, n_qkv + n * MW:n_qkv + (n + 1) * MW] for n in range(2))
        raw_down = late[:, 0:MW]
        assert MW <= n13 and n_qkv + 2 * MW <= KH * 7 * wide
        spare13 = wk[:, n_qkv + n13 + n2:n_qkv + n13 + n2 + KH * HID].rearrange("p (k e) -> p k e", k=KH)
        spare2 = wk[:, 0:n2].rearrange("p (c e) -> p c e", c=HC)
        assert n_qkv + n13 + n2 + KH * HID <= KH * 7 * wide and n2 <= n_qkv

        SPLITS = {name: n + 1 for n, name in enumerate(("wq", "wk", "wv", "route", "down", "gate", "up"))}
        flat4 = "p k c f -> p (k c f)"
        parts = {
            "route": (route_w[:], route_hl[:, :, 0], route_hl[:, :, 1]),
            "gate": (raw_gate, gate_h[:].rearrange(flat4), gate_l[:].rearrange(flat4)),
            "up": (raw_up, up_h[:].rearrange(flat4), up_l[:].rearrange(flat4)),
            "down": (raw_down, down_h[:].rearrange("p c e -> p (c e)"), down_l[:].rearrange("p c e -> p (c e)")),
        }
        for n, name in enumerate(("wq", "wk", "wv")):
            parts[name] = (raw_qkv[:, n * KH * D:(n + 1) * KH * D], qkv_h[:, n].rearrange("p k e -> p (k e)"),
                           qkv_l[:, n].rearrange("p k e -> p (k e)"))
        loaded = {"wq": (qkv_in[0], 16), "wk": (qkv_in[1], 16), "wv": (qkv_in[2], 16), "route": (route_in, 16),
                  "gate": (gate_in, 32 * KH), "up": (up_in, 32 * KH), "down": (down_in, 32)}

        block = stack.enter_context(nc.Block())

        @block.sync
        def _(sp):
            def attention_weights():
                for n, w in enumerate((wqT, wkT, wvT)):
                    sp.dma_start(parts[f"w{'qkv'[n]}"][0].rearrange("p (k e) -> p k e", k=KH),
                                 w.rearrange("(k p) e -> p k e", p=P)).then_inc(qkv_in[n], 16)

            def other_weights():
                sp.dma_start(raw13[:, 0], w1T.rearrange("(k p) e -> p k e", p=P)).then_inc(tern_in, 16)
                sp.dma_start(raw13[:, 1], w3T.rearrange("(k p) e -> p k e", p=P)).then_inc(tern_in, 16)
                full = (HC - 1) * P
                sp.dma_start(raw2[:, 0:HC - 1], w2T[0:full].rearrange("(c p) e -> p c e", p=P)).then_inc(tern_in, 16)
                sp.wait_ge(pads_set, 2)
                sp.dma_start(raw2[0:HR, HC - 1], w2T[full:HID]).then_inc(tern_in, 16)
                sp.dma_start(decay_sb[:], decay.rearrange("(h p) -> p h", p=P), allow_slow_non_contiguous=True).then_inc(consts_in, 16)
                sp.dma_start(bonus_sb[:], bonus.rearrange("(h p) -> p h", p=P), allow_slow_non_contiguous=True).then_inc(consts_in, 16)
                sp.dma_start(gains[:, 0:2], g_xattn.partition_broadcast(P)).then_inc(consts_in, 16)
                sp.dma_start(gains[:, 2:4], g_ffn.partition_broadcast(P)).then_inc(consts_in, 16)
                sp.dma_start(wo[:], woT.rearrange("(k p) e -> p k e", p=P)).then_inc(wo_in, 16)
                sp.dma_start(route_w[:], router.rearrange("(k p) e -> p k e", p=P)).then_inc(route_in, 16)
                down = raw_down.rearrange("p (c e) -> p c e", c=MC)
                sp.dma_start(down[:, 0:SC], s_down.rearrange("(c p) e -> p c e", p=P)).then_inc(down_in, 16)
                sp.dma_start(down[:, SC:MC], e_down.rearrange("e f d -> f e d")).then_inc(down_in, 16)
                for n, (raw, shared, expert, s) in enumerate(((raw_gate, s_gate, e_gate, gate_in), (raw_up, s_up, e_up, up_in))):
                    sp.wait_ge(tern_set, n + 2)
                    four = raw.rearrange("p (k c f) -> p k c f", k=KH, c=MC)
                    for k in range(KH):
                        sp.dma_start(four[:, k, 0:SC], shared[k * P:(k + 1) * P].rearrange("p (c f) -> p c f", f=P)).then_inc(s, 16)
                        sp.dma_start(four[:, k, SC:MC], expert[:, k * P:(k + 1) * P].rearrange("e p f -> p e f")).then_inc(s, 16)

            def turn(t):
                first = t.fixed and t.i == 0
                if first:
                    sp.dma_start(xa[:], x_rows[0]).then_inc(x_in, 16)
                    attention_weights()
                if t.second:
                    sp.wait_ge(low_set, SPLITS["down"])
                    sp.dma_start(attention_rows(t), x_rows[t.i]).then_inc(x_in, 16)
                if t.on["A"]:
                    if not first:
                        sp.wait_ge(rstd_done["A"], t.count("A", 2, 0))
                    sp.dma_start(ctx_row, ctx_rows[t.i]).then_inc(ctx_row_in, 16)
                    sp.dma_start(vals[S:P, :, 0], ctx_seqs[t.i, 0]).then_inc(ctx_val_in, 16)
                    sp.dma_start(vals[0:S, :, 1], ctx_seqs[t.i, 1]).then_inc(ctx_val_in, 16)
                    if not first and not t.second:
                        sp.wait_ge(sums_free, t.before(SUMS))
                        sp.dma_start(xa[:], x_rows[t.i]).then_inc(x_in, 16)
                if first:
                    other_weights()
                if t.on["M"]:
                    wait_taken(sp, t, "M", "combT")
                    if not t.fixed or t.count("M", 1, 0) > 0:
                        for half in comb_in:
                            sp.wait_ge(half, t.count("M", 8 * E, 0))
                    sp.dma_start(comb_dram, combT_sb).then_inc(combT_out, 16)
                    sp.wait_ge(combT_out, t.count("M", 16, 16))
                    for c in range(SC, MC):
                        n = scaled_chunk(t, c)
                        if not t.fixed or n > 2:
                            sp.wait_ge(weighted, n - 2)
                        sp.dma_start(comb_sb[:, c % 2], comb_dram[c - SC].partition_broadcast(P)).then_inc(comb_in[c % 2], 16)
                    sp.wait_ge(sums_free, t.shared(SUMS, ("M", "y")))
                    sp.dma_start(out_rows[t.i - LAG["M"]], out_row[:]).then_inc(out_done, 16)

            turns(sp, turn, turn, turn, turn)
            sp.wait_ge(out_done, 16 * NB)
            sp.wait_ge(combT_out, 16 * NB)

        @block.tensor
        def _(pe):
            pe.wait_ge(consts_set, 2)

            def keep_clock(count):
                for _ in range(count):
                    nc.tensor.matmul(up_ps[1][:, 0:P], ones[:], ones[:], start=True, stop=True)

            def weights_split(name):
                pe.wait_ge(low_set, SPLITS[name])

            def abs_sums():
                pe.wait_ge(abs_set, 4)
                pe.wait_ge(abs_w2_set, 1)
                nc.tensor.matmul(gate_ps[0][:, 0:3], ones[:], abs_sum[:], start=True, stop=True).then_inc(abs_all, 1)

            def claim(t, stage, name):
                n = bank_of((stage, name))
                before_me = t.shared(TRANSIT, (stage, name), n) - 1
                if not t.fixed or before_me > 0:
                    pe.wait_ge(t_free[n], before_me)
                return transit[n], t_full[n]

            def turn_rows(t, stage, name, source, h):
                bank, full = claim(t, stage, name)
                for r in range(NT):
                    last = nc.tensor.transpose(bank[:, r * P:(r + 1) * P], source[:, r, h * P:(h + 1) * P], ident[:])
                last.then_inc(full, 1)

            def split_product(o, lhs, rhs, first, final, group=True):
                (lh, ll), (rh, rl) = lhs, rhs
                pairs = [(lh, rh)] + ([(lh, rl)] if rl is not None else []) + ([(ll, rh)] if ll is not None else [])
                for n, (a, b) in enumerate(pairs):
                    last = nc.tensor.matmul(o, a, b, start=first and n == 0, stop=final and n == len(pairs) - 1,
                                            skip_group_check=not group)
                return last

            def context_T(t):
                pe.wait_ge(ctx_row_in, t.count("A", 16, 16))
                for h in range(KH):
                    turn_rows(t, "A", f"ctxT{h}", ctx_row, h)

            def z_T(t, stage, which, source, n):
                pe.wait_ge(z_done[stage], t.count(stage, 2, n))
                for h in range(KH):
                    turn_rows(t, stage, f"{which}{h}", source, h)

            def q_and_k(t):
                wait_taken(pe, t, "A", "z0T0", "z0T1", claims=("A", "q0"))
                for w, name in enumerate("qk"):
                    if t.fixed and t.i == 0:
                        weights_split(f"w{name}")
                    for m in range(KH):
                        bank, full = claim(t, "A", f"{name}{m}")
                        cols = slice(m * P, (m + 1) * P)
                        for k in range(KH):
                            last = split_product(bank[:], (qkv_h[:, w, k, cols], qkv_l[:, w, k, cols]),
                                                 (za_h[:, k], za_l[:, k]), k == 0, k == KH - 1)
                        last.then_inc(full, 1)

            def values(t):
                if t.fixed and t.i == 0:
                    weights_split("wv")
                for pair in range(2):
                    bank, full = claim(t, "A", f"v{pair}")
                    for r in range(2):
                        rows_ = slice((2 * pair + r) * P, (2 * pair + r + 1) * P)
                        for k in range(KH):
                            last = split_product(bank[:, r * D:(r + 1) * D], (za_h[:, k, rows_], za_l[:, k, rows_]),
                                                 (qkv_h[:, 2, k], qkv_l[:, 2, k]), k == 0, k == KH - 1)
                    last.then_inc(full, 1)

            def scores(t):
                wait_taken(pe, t, "A", "k0", "k1", claims=("A", "scores"))
                bank, full = claim(t, "A", "scores")
                for r in range(NT):
                    for q in range(2):
                        for h in range(KH):
                            last = nc.tensor.matmul(
                                bank[q * S:(q + 1) * S, r * P:(r + 1) * P], qo[:, h, (2 * r + q) * S:(2 * r + q + 1) * S],
                                keys[:, h, r, 2 * q:2 * q + 2].rearrange("p c s -> p (c s)"), start=h == 0, stop=h == KH - 1)
                last.then_inc(full, 1)

            def probs_T(t):
                wait_taken(pe, t, "A", "scores", claims=("A", "pT"))
                bank, full = claim(t, "A", "pT")
                for r in range(NT):
                    last = nc.tensor.transpose(bank[:, r * P:(r + 1) * P], probs[:, r], ident[:])
                last.then_inc(full, 1)

            def attend(t):
                wait_taken(pe, t, "A", "v0", "v1", "pT", claims=("A", "oT0"))
                pe.wait_ge(ctx_val_in, t.count("A", 32, 32))
                for h in range(KH):
                    bank, full = claim(t, "A", f"oT{h}")
                    for r in range(NT):
                        for q in range(2):
                            cols = slice((2 * r + q) * S, (2 * r + q + 1) * S)
                            last = nc.tensor.matmul(bank[:, cols], vals[:, r, q, h * P:(h + 1) * P], probsT[:, cols],
                                                    start=True, stop=True)
                    last.then_inc(full, 1)

            def project(t):
                wait_taken(pe, t, "A", "oT0", "oT1", claims=("A", "wo0"))
                if t.fixed and t.i == 0:
                    pe.wait_ge(wo_in, 16)
                for pair in range(2):
                    bank, full = claim(t, "A", f"wo{pair}")
                    for r in range(2):
                        for k in range(KH):
                            last = nc.tensor.matmul(bank[:, r * D:(r + 1) * D], qo[:, k, (2 * pair + r) * P:(2 * pair + r + 1) * P],
                                                    wo[:, k], start=k == 0, stop=k == KH - 1)
                    last.then_inc(full, 1)

            def y_T(t):
                pe.wait_ge(yw_set, t.count("W", KH, KH))
                for pair in range(2):
                    bank, full = claim(t, "W", f"yT{pair}")
                    for r in range(2):
                        for h in range(KH):
                            last = nc.tensor.transpose(bank[:, r * D + h * P:r * D + (h + 1) * P],
                                                       vw[:, h, (2 * pair + r) * P:(2 * pair + r + 1) * P], ident[:])
                    last.then_inc(full, 1)

            def route(t):
                wait_taken(pe, t, "W", "z3T0", "z3T1", claims=("W", "route"))
                if t.fixed and t.i == LAG["W"]:
                    weights_split("route")
                bank, full = claim(t, "W", "route")
                _, z_h, z_l = recurrence_out(t)
                for r in range(NT):
                    rows_ = slice(r * P, (r + 1) * P)
                    for k in range(KH):
                        nc.tensor.matmul(bank[:, 2 * r * E:2 * (r + 1) * E], z_h[:, k, rows_], route_hl[:, k].rearrange("p a e -> p (a e)"),
                                         start=k == 0, stop=False)
                        last = nc.tensor.matmul(bank[:, 2 * r * E:(2 * r + 1) * E], z_l[:, k, rows_], route_hl[:, k, 0],
                                                start=False, stop=k == KH - 1)
                last.then_inc(full, 1)

            def up(t, chunk):
                stage, c = chunk
                pos = CHUNKS.index(chunk) % 2
                wait_back(pe, gated, t, chunk, 2)
                if stage == "M":
                    _, z_h, z_l = experts_in(t)
                    for ps, wh, wl in ((gate_ps, gate_h, gate_l), (up_ps, up_h, up_l)):
                        for k in range(KH):
                            last = split_product(ps[pos][:], (wh[:, k, c], wl[:, k, c]), (z_h[:, k], z_l[:, k]),
                                                 k == 0, k == KH - 1)
                else:
                    if c == 0:
                        wait_taken(pe, t, "A", "z1T0", "z1T1")
                        if t.fixed and t.i == 0:
                            pe.wait_ge(tern_set, 3)
                    cols = slice(c * P, (c + 1) * P)
                    for w, ps in enumerate((gate_ps,) if is_tail(chunk) else (gate_ps, up_ps)):
                        for k in range(KH):
                            last = split_product(ps[pos][:], (w13[:, w, k, cols], None), (za_h[:, k], za_l[:, k]),
                                                 k == 0, k == KH - 1)
                last.then_inc(up_full, 1)

            def combine_T(t):
                pe.wait_ge(combine_set, t.count("M", 1, 1))
                bank, full = claim(t, "M", "combT")
                for r in range(NT):
                    last = nc.tensor.transpose(bank[0:E, r * P:(r + 1) * P], combine[:, r], ident[:])
                last.then_inc(full, 1)

            def down(t, chunk):
                stage, c = chunk
                pos = CHUNKS.index(chunk) % 2
                final = c == (MC if stage == "M" else HC) - 1
                pe.wait_ge(hid_h_set, chunk_no(t, chunk))
                pe.wait_ge(hid_l_set, chunk_no(t, chunk))
                if c == 0:
                    n = t.shared(SUMS, (stage, "y")) - 1
                    if not t.fixed or n > 0:
                        pe.wait_ge(sums_free, n)
                n = hidden_rows(chunk)
                w = (down_h[:, c], down_l[:, c]) if stage == "M" else (w2[0:n, c], None)
                for r in range(NT):
                    rows_ = slice(r * P, (r + 1) * P)
                    last = split_product(sums[r // 2][:, (r % 2) * D:(r % 2 + 1) * D],
                                         (hid_h[0:n, pos, rows_], hid_l[0:n, pos, rows_]), w, c == 0 and r % 2 == 0, final, group=False)
                last.then_inc(down_done, 1)

            def turn(t):
                first, t1 = t.fixed and t.i == 0, Turn(1, NB, True)
                w, m = t.on["W"], t.on["M"]

                def m_up(*chunks):
                    for c in chunks if m else ():
                        up(t, ("M", c))

                def m_down(*chunks):
                    for c in chunks if m else ():
                        down(t, ("M", c))

                def f_up(c):
                    up(t, ("A", c))
                    if c >= 2:
                        down(t, ("A", c - 2))
                if t.fixed and t.i == LAG["M"]:
                    weights_split("up")
                m_up(0)
                if first:
                    keep_clock(12)
                context_T(t)
                m_up(1)
                if m:
                    combine_T(t)
                m_up(2)
                m_down(0)
                if w:
                    z_T(t, "W", "z2T", zw_row, 1)
                m_up(3)
                m_down(1)
                if first:
                    keep_clock(10)
                z_T(t, "A", "z0T", za_row, 1)
                m_up(4)
                m_down(2)
                if first:
                    keep_clock(6)
                q_and_k(t)
                values(t)
                m_down(3)
                scores(t)
                if t.fixed and t.i == 0:
                    abs_sums()
                m_up(5)
                if first:
                    keep_clock(10)
                probs_T(t)
                m_down(4)
                if first:
                    keep_clock(3)
                attend(t)
                m_up(6)
                if first:
                    keep_clock(3)
                project(t)
                m_up(7)
                m_down(5)
                m_up(8)
                m_down(6)
                if first:
                    keep_clock(30)
                z_T(t, "A", "z1T", za_row, 2)
                m_up(9)
                m_down(7)
                if first:
                    keep_clock(6)
                f_up(0)
                m_down(8)
                f_up(1)
                if w:
                    y_T(t)
                m_down(9)
                f_up(2)
                f_up(3)
                f_up(4)
                if w:
                    z_T(t, "W", "z3T", zw_row, 2)
                f_up(5)
                if first:
                    z_T(t1, "A", "z0T", za_row, 1)
                if w:
                    route(t)
                down(t, ("A", HC - 2))
                keep_clock(3)
                down(t, ("A", HC - 1))

            def second(t):
                def f_up(c):
                    up(t, ("A", c))
                    if c >= 2:
                        down(t, ("A", c - 2))
                q_and_k(t)
                values(t)
                keep_clock(6)
                context_T(t)
                z_T(t, "W", "z2T", zw_row, 1)
                scores(t)
                keep_clock(10)
                probs_T(t)
                keep_clock(3)
                attend(t)
                keep_clock(3)
                project(t)
                keep_clock(30)
                z_T(t, "A", "z1T", za_row, 2)
                keep_clock(6)
                f_up(0)
                f_up(1)
                f_up(2)
                y_T(t)
                for c in range(3, HC - 1):
                    f_up(c)
                z_T(t, "W", "z3T", zw_row, 2)
                f_up(HC - 1)
                route(t)
                down(t, ("A", HC - 2))
                keep_clock(3)
                down(t, ("A", HC - 1))

            def closing(t):
                def m_up(*chunks):
                    for c in chunks:
                        up(t, ("M", c))

                def m_down(*chunks):
                    for c in chunks:
                        down(t, ("M", c))
                m_up(0, 1)
                combine_T(t)
                m_up(2)
                m_down(0)
                z_T(t, "W", "z2T", zw_row, 1)
                for c in range(3, MC - 1):
                    m_up(c)
                    m_down(c - 2)
                y_T(t)
                m_up(MC - 1)
                m_down(MC - 3)
                z_T(t, "W", "z3T", zw_row, 2)
                m_down(MC - 2)
                route(t)
                m_down(MC - 1)

            def last(t):
                for c in range(MC):
                    up(t, ("M", c))
                    if c == 1:
                        combine_T(t)
                    if c >= 3:
                        down(t, ("M", c - 3))
                for c in range(MC - 3, MC):
                    down(t, ("M", c))

            turns(pe, turn, second, closing, last)

        @block.scalar
        def _(act):
            def high(name):
                act.wait_ge(*loaded[name])
                raw, high_part, _ = parts[name]
                nc.scalar.activation(high_part, raw, ACT.Copy).then_inc(high_set, 1)

            def normalise(t, stage, n, rows_in, rows_out, rstd, shift):
                act.wait_ge(shift_done[stage], t.count(stage, 2, n))
                for r in range(NT):
                    last = nc.scalar.activation(rows_out[:, r], rows_in[:, r], ACT.Identity, bias=shift[:, r:r + 1],
                                                scale=rstd[:, r:r + 1])
                last.then_inc(z_done[stage], 1)

            def high_parts(t, stage, which, dst, done):
                for h in range(KH):
                    bank = wait_full(act, t, stage, f"{which}{h}")
                    nc.scalar.activation(dst[:, h], bank[:], ACT.Copy).then_inc(done, 1)

            def context_T(t):
                if not t.fixed or t.i > 0:
                    act.wait_ge(vw_set, t.count("A", 1, 0))
                for h in range(KH):
                    bank = wait_full(act, t, "A", f"ctxT{h}")
                    nc.scalar.activation(keys[:, h, :, 1:3].rearrange("p t c s -> p t (c s)"),
                                         bank[:].rearrange("p (t n) -> p t n", t=NT), ACT.Copy).then_inc(free_of("A", f"ctxT{h}"), 1)

            def keep_context(t):
                if t.on["W"]:
                    wait_full(act, t, "W", "yT1")
                for h in range(KH):
                    last = nc.scalar.activation(vw[:, h].rearrange("p (t n) -> p t n", t=NT),
                                                keys[:, h, :, 1:3].rearrange("p t c s -> p t (c s)"), ACT.Copy)
                last.then_inc(vw_set, 1)

            def keep_rows(t):
                if t.on["M"]:
                    act.wait_ge(sums_free, t.shared(SUMS, ("M", "y")))
                wait_full(act, t, "W", "z3T1")
                nc.scalar.activation(x3.rearrange("p t d -> p (t d)"), x2[:].rearrange("p t d -> p (t d)"), ACT.Copy).then_inc(rows_kept, 1)

            def queries(t):
                for m in range(KH):
                    bank = wait_full(act, t, "A", f"q{m}")
                    nc.scalar.activation(qo[:, m], bank[:], ACT.Copy).then_inc(free_of("A", f"q{m}"), 1)

            def own_keys(t):
                for m in range(KH):
                    bank = wait_full(act, t, "A", f"k{m}")
                    nc.scalar.activation(keys[:, m, :, 0:4:3], bank[:].rearrange("p (t q s) -> p t q s", t=NT, q=2),
                                         ACT.Copy).then_inc(free_of("A", f"k{m}"), 1)

            def values(t):
                for pair in range(2):
                    bank = wait_full(act, t, "A", f"v{pair}")
                    for q in range(2):
                        half = slice(q * S, (q + 1) * S)
                        last = nc.scalar.activation(vals[half, 2 * pair:2 * pair + 2, q],
                                                    bank[half].rearrange("p (r d) -> p r d", r=2), ACT.Copy)
                    last.then_inc(free_of("A", f"v{pair}"), 1)

            def softmax(t):
                bank = wait_full(act, t, "A", "scores")
                act.wait_ge(nsmax_set, t.count("A", 1, 1))
                for r in range(NT):
                    last = nc.scalar.activation(probs[:, r], bank[:, r * P:(r + 1) * P], ACT.Exp, bias=nsmax[:, r:r + 1],
                                                scale=SCALE, accum_out=psum_row[:, r:r + 1])
                last.then_inc(free_of("A", "scores"), 1)

            def probs_T(t):
                bank = wait_full(act, t, "A", "pT")
                nc.scalar.activation(probsT, bank[:], ACT.Copy).then_inc(free_of("A", "pT"), 1)

            def attend(t):
                for h in range(KH):
                    bank = wait_full(act, t, "A", f"oT{h}")
                    nc.scalar.activation(qo[:, h], bank[:], ACT.Copy).then_inc(free_of("A", f"oT{h}"), 1)

            def k_wide(t):
                for h in range(KH):
                    bank = wait_full(act, t, "W", f"z2T{h}")
                    nc.scalar.activation(kw[:, h, :, 1:S1], bank[:].rearrange("p (b s) -> p b s", b=NS), ACT.Copy).then_inc(free_of("W", f"z2T{h}"), 1)

            def decays(t, h):
                act.wait_ge(a2arg_set, t.count("W", KH, h + 1))
                nc.scalar.activation(seqs(h, A2, 1), seqs(h, A2, 1), ACT.Exp).then_inc(a2_set, 1)
                act.wait_ge(e2arg_set, t.count("W", KH, h + 1))
                nc.scalar.activation(seqs(h, E2, 1), seqs(h, E2, 1), ACT.Exp).then_inc(e2_set, 1)

            def readouts(t, h):
                act.wait_ge(clamp_set, t.count("W", 2 * KH, 2 * h + 2))
                nc.scalar.activation(flat(h, EA)[:, 0:TOK], flat(h, EA)[:, 0:TOK], ACT.Exp, scale=-1.0).then_inc(ea_set, 1)
                nc.scalar.activation(flat(h, EE)[:, 0:TOK], flat(h, EE)[:, 0:TOK], ACT.Exp).then_inc(ee_set, 1)

            def route(t):
                wait_taken(act, t, "W", "route")
                nc.scalar.activation(pexp[:], pexp[:], ACT.Exp).then_inc(pexp_set, 1)

            def squash(t, chunk):
                stage, c = chunk
                pos = CHUNKS.index(chunk) % 2
                act.wait_ge(up_full, chunk_no(t, chunk))
                wait_back(act, hid_l_set, t, chunk, 2)
                n = hidden_rows(chunk)
                nc.scalar.activation(act_sb[0:n, pos], gate_ps[pos][0:n], ACT.Tanh,
                                     scale=0.5 if stage == "M" else half_s[0:n, 0:1]).then_inc(tanh_done, 1)

            def combine_T(t):
                bank = wait_full(act, t, "M", "combT")
                nc.scalar.activation(combT_sb, bank[0:E], ACT.Copy).then_inc(free_of("M", "combT"), 1)

            def high_hidden(t, chunk):
                stage, c = chunk
                pos = CHUNKS.index(chunk) % 2
                if stage == "M" and c >= SC:
                    act.wait_ge(weighted, scaled_chunk(t, c))
                else:
                    act.wait_ge(gated, chunk_no(t, chunk))
                wait_back(act, down_done, t, chunk, 2)
                n = hidden_rows(chunk)
                nc.scalar.activation(hid_h[0:n, pos], act_sb[0:n, pos], ACT.Copy).then_inc(hid_h_set, 1)

            def turn(t):
                first, t1 = t.fixed and t.i == 0, Turn(1, NB, True)
                w, m = t.on["W"], t.on["M"]

                def m_high(c):
                    if m:
                        high_hidden(t, ("M", c))

                def m_chunk(c, high=True):
                    if m:
                        if c >= 1 and high:
                            high_hidden(t, ("M", c - 1))
                        squash(t, ("M", c))

                def f_chunk(c):
                    squash(t, ("A", c))
                    if c >= 1:
                        high_hidden(t, ("A", c - 1))
                if first:
                    for name in ("wq", "wk", "wv"):
                        high(name)
                m_chunk(0)
                context_T(t)
                m_chunk(1)
                if m:
                    combine_T(t)
                if w:
                    normalise(t, "W", 1, x2, zw_row, rstd_w, shift_w)
                m_chunk(2)
                if w:
                    k_wide(t)
                normalise(t, "A", 1, xa, za_row, rstd_a, shift_a)
                m_chunk(3)
                high_parts(t, "A", "z0T", za_h, za_h_set)
                m_chunk(4)
                queries(t)
                if w:
                    decays(t, 0)
                own_keys(t)
                if w:
                    decays(t, 1)
                    readouts(t, 0)
                values(t)
                if first:
                    act.wait_ge(tern_in, 64)
                    act.wait_ge(low_set, SPLITS["wv"])
                    nc.scalar.activation(spare2, raw2, ACT.Abs, accum_out=abs_sum[:, 2:3]).then_inc(abs_w2_set, 1)
                    act.wait_ge(consts_in, 64)
                    nc.scalar.activation(gains[:], gains[:], ACT.Tanh).then_inc(gains_set, 1)
                m_high(4)
                softmax(t)
                m_chunk(5, high=False)
                probs_T(t)
                if w:
                    readouts(t, 1)
                attend(t)
                if first:
                    high("route")
                    high("down")
                m_chunk(6)
                m_chunk(7)
                normalise(t, "A", 2, xa, za_row, rstd_a, shift_a)
                m_chunk(8)
                high_parts(t, "A", "z1T", za_h, za_h_set)
                if first:
                    high("gate")
                m_chunk(9)
                if m:
                    high_hidden(t, ("M", MC - 1))
                if first:
                    act.wait_ge(tern_set, 3)
                f_chunk(0)
                f_chunk(1)
                if first:
                    high("up")
                f_chunk(2)
                f_chunk(3)
                if w:
                    normalise(t, "W", 2, x2, zw_row, rstd_w, shift_w)
                f_chunk(4)
                if first:
                    normalise(t1, "A", 1, attention_rows(t1), za_row, rstd_a, shift_a)
                if w:
                    high_parts(t, "W", "z3T", zm_h, zm_h_set)
                high_hidden(t, ("A", HC - 2))
                squash(t, ("A", HC - 1))
                high_hidden(t, ("A", HC - 1))
                if w:
                    keep_rows(t)
                if first:
                    high_parts(t1, "A", "z0T", za_h, za_h_set)
                if w:
                    route(t)
                keep_context(t)

            def second(t):
                rows = attention_rows(t)
                queries(t)
                own_keys(t)
                normalise(t, "W", 1, x2, zw_row, rstd_w, shift_w)
                values(t)
                context_T(t)
                k_wide(t)
                softmax(t)
                probs_T(t)
                for h in range(KH):
                    decays(t, h)
                readouts(t, 0)
                attend(t)
                readouts(t, 1)
                normalise(t, "A", 2, rows, za_row, rstd_a, shift_a)
                high_parts(t, "A", "z1T", za_h, za_h_set)
                squash(t, ("A", 0))
                for c in range(1, HC):
                    if c == HC - 1:
                        high_parts(t, "W", "z3T", zm_h, zm_h_set)
                    squash(t, ("A", c))
                    high_hidden(t, ("A", c - 1))
                    if c == 4:
                        normalise(t, "W", 2, x2, zw_row, rstd_w, shift_w)
                high_hidden(t, ("A", HC - 1))
                keep_rows(t)
                route(t)
                keep_context(t)

            def closing(t):
                def m_chunk(c):
                    squash(t, ("M", c))
                    if c >= 1:
                        high_hidden(t, ("M", c - 1))
                m_chunk(0)
                m_chunk(1)
                combine_T(t)
                normalise(t, "W", 1, x2, zw_row, rstd_w, shift_w)
                m_chunk(2)
                k_wide(t)
                m_chunk(3)
                decays(t, 0)
                decays(t, 1)
                readouts(t, 0)
                m_chunk(4)
                readouts(t, 1)
                for c in range(5, MC - 1):
                    m_chunk(c)
                squash(t, ("M", MC - 1))
                normalise(t, "W", 2, recurrence_out(t)[0], zw_row, rstd_w, shift_w)
                high_hidden(t, ("M", MC - 2))
                high_parts(t, "W", "z3T", recurrence_out(t)[1], zm_h_set)
                high_hidden(t, ("M", MC - 1))
                route(t)

            def last(t):
                for c in range(MC):
                    squash(t, ("M", c))
                    if c == 1:
                        combine_T(t)
                    if c >= 1:
                        high_hidden(t, ("M", c - 1))
                high_hidden(t, ("M", MC - 1))

            turns(act, turn, second, closing, last)

        @block.gpsimd
        def _(pool):
            nc.gpsimd.memset(raw2[:, HC - 1], 0.0).then_inc(pads_set, 1)
            tail = w13[:, 0, :, (HC - 1) * P:].rearrange("p k (a e) -> p k a e", a=2)
            nc.gpsimd.memset(tail[:, :, :, HR:].bitcast(F32), 0.0).then_inc(pads_set, 1)
            nc.gpsimd.memset(ones[:], 1.0)
            nc.gpsimd.memset(minus_half[:], -0.5)
            nc.gpsimd.memset(minus_one[:], -1.0)
            nc.gpsimd.memset(eps_row[:], EPS)
            nc.gpsimd.memset(ident[:], 0.0).then_inc(ident_zero, 1)
            nc.gpsimd.memset(before[:], 1.0).then_inc(ident_zero, 1)
            pool.wait_ge(ident_zero, 2)
            nc.gpsimd.affine_select(out=before[:], in_=before[:], compare_op=ALU.is_gt, fill=0.0, base=0,
                                    pattern=[[1, E], [-1, E]], channel_multiplier=0).then_inc(consts_set, 1)
            nc.gpsimd.affine_select(out=ident[:], in_=ident[:], compare_op=ALU.not_equal, fill=1.0, base=0,
                                    pattern=[[-1, P]], channel_multiplier=1).then_inc(consts_set, 1)

            def row_factors(t, stage, n, stats, nmean, var, rstd, shift):
                pool.wait_ge(mv_done[stage], t.count(stage, 2, n))
                nc.gpsimd.tensor_tensor(var[:], stats[:, :, 1], eps_row[:], ALU.add).then_inc(var_done[stage], 1)
                nc.gpsimd.tensor_tensor(nmean[:], stats[:, :, 0], minus_one[:], ALU.mult)
                pool.wait_ge(var_done[stage], t.count(stage, 2, n))
                nc.gpsimd.tensor_tensor(rstd[:], var[:], minus_half[:], ALU.pow).then_inc(rstd_done[stage], 1)
                pool.wait_ge(rstd_done[stage], t.count(stage, 2, n))
                nc.gpsimd.tensor_tensor(shift[:], nmean[:], rstd[:], ALU.mult).then_inc(shift_done[stage], 1)

            def inputs(t, h):
                pool.wait_ge(omax_set, t.count("W", KH, h + 1))
                nc.gpsimd.tensor_tensor(seqs(h, E2, 1), kw[:, h, :, 1:S1], seqs(h, OMAX, 1), ALU.subtract).then_inc(e2arg_set, 1)

            def weigh_inputs(t, h):
                pool.wait_ge(e2_set, t.count("W", KH, h + 1))
                pool.wait_ge(vw_set, t.count("W", 1, 1))
                nc.gpsimd.tensor_tensor(seqs(h, EV, 1), seqs(h, E2, 1), vw[:, h].rearrange("p (b s) -> p b s", b=NS),
                                        ALU.mult).then_inc(ev_set, 1)

            def weigh_now(t, h):
                pool.wait_ge(ee_set, t.count("W", KH, h + 1))
                pool.wait_ge(scans_done, t.count("W", 2 * KH, 2 * h + 2))
                nc.gpsimd.tensor_tensor(seqs(h, A2, 1), flat(h, EE)[:, 0:TOK].rearrange("p (b s) -> p b s", b=NS),
                                        vw[:, h].rearrange("p (b s) -> p b s", b=NS), ALU.mult).then_inc(eev_set, 1)

            def low_hidden(t, chunk):
                pos = CHUNKS.index(chunk) % 2
                pool.wait_ge(hid_h_set, chunk_no(t, chunk))
                n = hidden_rows(chunk)
                nc.gpsimd.tensor_tensor(hid_l[0:n, pos], act_sb[0:n, pos], hid_h[0:n, pos].bitcast(F32), ALU.subtract).then_inc(hid_l_set, 1)

            def weigh_chunk(t, chunk):
                c = chunk[1]
                pos = CHUNKS.index(chunk) % 2
                if c >= SC:
                    pool.wait_ge(gated, chunk_no(t, chunk))
                    pool.wait_ge(comb_in[c % 2], t.count("M", 8 * E, 16 * ((c - SC) // 2 + 1)))
                    nc.gpsimd.tensor_tensor(act_sb[:, pos], act_sb[:, pos], comb_sb[:, pos], ALU.mult).then_inc(weighted, 1)

            def turn(t):
                w, m = t.on["W"], t.on["M"]

                def m_low(c):
                    if m:
                        low_hidden(t, ("M", c))

                def m_weigh(c):
                    if m:
                        weigh_chunk(t, ("M", c))
                if w:
                    row_factors(t, "W", 1, mv_w, nmean_w, var_w, rstd_w, shift_w)
                m_low(0)
                row_factors(t, "A", 1, mv_a, nmean_a, var_a, rstd_a, shift_a)
                m_low(1)
                m_weigh(2)
                if w:
                    for h in range(KH):
                        inputs(t, h)
                m_low(2)
                m_weigh(3)
                m_low(3)
                m_weigh(4)
                if w:
                    for h in range(KH):
                        weigh_inputs(t, h)
                m_low(4)
                m_weigh(5)
                if w:
                    weigh_now(t, 0)
                m_low(5)
                m_weigh(6)
                if w:
                    weigh_now(t, 1)
                m_low(6)
                row_factors(t, "A", 2, mv_a, nmean_a, var_a, rstd_a, shift_a)
                m_weigh(7)
                m_low(7)
                m_weigh(8)
                m_low(8)
                m_weigh(9)
                m_low(9)
                for c in range(HC):
                    if w and c == 2:
                        row_factors(t, "W", 2, mv_w, nmean_w, var_w, rstd_w, shift_w)
                    if t.fixed and t.i == 0 and c == 3:
                        row_factors(Turn(1, NB, True), "A", 1, mv_a, nmean_a, var_a, rstd_a, shift_a)
                    low_hidden(t, ("A", c))

            def second(t):
                row_factors(t, "W", 1, mv_w, nmean_w, var_w, rstd_w, shift_w)
                for step in (inputs, weigh_inputs, weigh_now):
                    for h in range(KH):
                        step(t, h)
                row_factors(t, "A", 2, mv_a, nmean_a, var_a, rstd_a, shift_a)
                for c in range(3):
                    low_hidden(t, ("A", c))
                row_factors(t, "W", 2, mv_w, nmean_w, var_w, rstd_w, shift_w)
                for c in range(3, HC):
                    low_hidden(t, ("A", c))

            def closing(t):
                def m_low(c):
                    low_hidden(t, ("M", c))

                def m_weigh(c):
                    weigh_chunk(t, ("M", c))
                row_factors(t, "W", 1, mv_w, nmean_w, var_w, rstd_w, shift_w)
                m_low(0)
                m_low(1)
                m_weigh(2)
                for h in range(KH):
                    inputs(t, h)
                m_low(2)
                m_weigh(3)
                weigh_inputs(t, 0)
                m_low(3)
                weigh_inputs(t, 1)
                m_weigh(4)
                m_low(4)
                weigh_now(t, 0)
                m_weigh(5)
                m_low(5)
                weigh_now(t, 1)
                for c in range(6, MC - 2):
                    m_weigh(c)
                    m_low(c)
                row_factors(t, "W", 2, mv_w, nmean_w, var_w, rstd_w, shift_w)
                m_weigh(MC - 2)
                m_low(MC - 2)
                m_weigh(MC - 1)
                m_low(MC - 1)

            def last(t):
                for c in range(MC):
                    if c >= 1:
                        low_hidden(t, ("M", c - 1))
                    weigh_chunk(t, ("M", c))
                low_hidden(t, ("M", MC - 1))

            turns(pool, turn, second, closing, last)

        @block.vector
        def _(dve):
            def low(name):
                raw, high_part, low_part = parts[name]
                dve.wait_ge(high_set, SPLITS[name])
                nc.vector.tensor_tensor(low_part, raw, high_part.bitcast(F32), ALU.subtract).then_inc(low_set, 1)

            def decay_rows():
                nc.vector.memset(decay_row[:], 0.0).then_inc(scan_zero, 1)
                dve.wait_ge(consts_in, 64)
                dve.wait_ge(scan_zero, 1)
                for h in range(KH):
                    nc.vector.tensor_scalar(decay_row[:, h, :, 1:S1], decay_row[:, h, :, 1:S1], decay_sb[:, h:h + 1], None, ALU.add)
                nc.vector.memset(decay_row[:, :, :, 0:1], NEG)
                nc.vector.memset(kw[:, :, :, 0:1], NEG)

            def scan_slots():
                dve.wait_ge(low_set, SPLITS["up"])
                for h in range(KH):
                    for c in (A2, E2, EV):
                        last = nc.vector.memset(flat(h, c).rearrange("p (b s) -> p b s", b=NS)[:, :, 0:1], 0.0)
                last.then_inc(scan_set, 1)

            def ternary_scales():
                dve.wait_ge(gains_set, 1)
                nc.vector.tensor_scalar(gain_m[:], gains[:, 3:4], 0.5, None, ALU.mult)
                dve.wait_ge(abs_all, 1)
                abs_tot = gate_ps[0][:, 0:3]
                nc.vector.tensor_scalar(scales[:], abs_tot, 1.0 / (HID * D), None, ALU.mult)
                nc.vector.tensor_scalar(half_s[:], abs_tot, 0.5 / (HID * D), None, ALU.mult)
                nc.vector.tensor_scalar(neg_half_s[:], abs_tot, -0.5 / (HID * D), None, ALU.mult).then_inc(tern_chain, 1)
                dve.wait_ge(tern_chain, 1)
                nc.vector.tensor_scalar(s_prod[:, 0:1], scales[:, 0:1], scales[:, 1:2], scales[:, 2:3], ALU.mult, ALU.mult).then_inc(tern_chain, 1)
                dve.wait_ge(tern_chain, 2)
                nc.vector.tensor_scalar(gain_f[:], s_prod[:, 0:1], gains[:, 2:3], 0.5, ALU.mult, ALU.mult)

            LAST = (HC - 1) * P
            TERNARY = [
                ([(w13[:, 0, :, 0:HID], slice(0, HID))], raw13[:, 0], spare13),
                ([(w13[:, 1, :, 0:LAST], slice(0, LAST)), (w13[:, 0, :, LAST + HALF:LAST + HALF + HR], slice(LAST, HID))],
                 raw13[:, 1], spare13),
                ([(w2[:], slice(0, D))], raw2, spare2),
            ]

            def absolute_sums():
                dve.wait_ge(tern_in, 64)
                for w, (_, raw, spare) in enumerate(TERNARY[:2]):
                    if w:
                        dve.wait_ge(abs_set, 2 * w)
                    nc.vector.scalar_tensor_tensor(spare, raw, -1.0, raw, ALU.mult, ALU.max).then_inc(abs_set, 1)
                    dve.wait_ge(abs_set, 2 * w + 1)
                    nc.vector.tensor_reduce(abs_sum[:, w:w + 1], spare, AX.XY, ALU.add).then_inc(abs_set, 1)

            def ternary_weights():
                dve.wait_ge(abs_set, 4)
                dve.wait_ge(abs_w2_set, 1)
                for w, (places, raw, below) in enumerate(TERNARY):
                    if w:
                        dve.wait_ge(tern_set, w)
                    nc.vector.tensor_scalar(below, raw, neg_half_s[:, w:w + 1], None, ALU.is_lt).then_inc(tern_chain, 1)
                    dve.wait_ge(tern_chain, 3 + w)
                    for place, part in places:
                        last = nc.vector.scalar_tensor_tensor(place, raw[:, :, part], half_s[:, w:w + 1], below[:, :, part],
                                                              ALU.is_gt, ALU.subtract)
                    last.then_inc(tern_set, 1)

            def statistics(t, stage, n, rows_in, bn, mv):
                if not t.fixed or t.count(stage, 2, n) > 1:
                    dve.wait_ge(z_done[stage], t.count(stage, 2, n - 1))
                for r in range(NT):
                    last = nc.vector.bn_stats(bn[:, r], rows_in[:, r])
                last.then_inc(bn_done[stage], 1)
                dve.wait_ge(bn_done[stage], t.count(stage, 2, n))
                dve.sem_inc(bn_seen, 1)
                for r in range(NT):
                    last = nc.vector.bn_aggr(mv[:, r], bn[:, r])
                last.then_inc(mv_done[stage], 1)

            def low_parts(t, stage, which, high_part, low_part, done_high, n, per):
                for h in range(KH):
                    bank = wait_full(dve, t, stage, f"{which}{h}")
                    dve.wait_ge(done_high, t.count(stage, per, n + h + 1))
                    nc.vector.tensor_tensor(low_part[:, h], bank[:], high_part[:, h].bitcast(F32),
                                            ALU.subtract).then_inc(free_of(stage, f"{which}{h}"), 1)

            def row_max(t):
                bank = wait_full(dve, t, "A", "scores")
                nc.vector.tensor_reduce(smax[:], bank[:].rearrange("p (r k) -> p r k", r=NT), AX.X, ALU.max).then_inc(smax_set, 1)
                dve.wait_ge(smax_set, t.count("A", 1, 1))
                nc.vector.tensor_scalar(nsmax[:], smax[:], -SCALE, None, ALU.mult).then_inc(nsmax_set, 1)

            def row_scale(t):
                wait_taken(dve, t, "A", "scores")
                nc.vector.reciprocal(rinv[:], psum_row[:]).then_inc(rinv_set, 1)
                dve.wait_ge(rinv_set, t.count("A", 1, 1))
                nc.vector.tensor_scalar(rgain[:], rinv[:], gains[:, 0:1], None, ALU.mult).then_inc(rgain_set, 1)

            def add_attention(t):
                xa = attention_rows(t)
                dve.wait_ge(rgain_set, t.count("A", 1, 1))
                for pair in range(2):
                    bank = wait_full(dve, t, "A", f"wo{pair}")
                    for r in range(2):
                        row = 2 * pair + r
                        last = nc.vector.scalar_tensor_tensor(xa[:, row], bank[:, r * D:(r + 1) * D], rgain[:, row:row + 1],
                                                              xa[:, row], ALU.mult, ALU.add)
                    last.then_inc(free_of("A", f"wo{pair}"), 1)

            def add_sums(t, stage, gain, rows_in, rows_out):
                dve.wait_ge(down_done, chunk_no(t, (stage, (MC if stage == "M" else HC) - 1)))
                if stage == "A" and t.on["W"]:
                    dve.wait_ge(rows_kept, t.count("W", 1, 1))
                if stage == "M" and (not t.fixed or t.count("M", 1, 0) > 0):
                    dve.wait_ge(out_done, t.count("M", 16, 0))
                for pair in range(2):
                    two = slice(2 * pair, 2 * pair + 2)
                    last = nc.vector.scalar_tensor_tensor(rows_out[:, two].rearrange("p r d -> p (r d)"), sums[pair][:], gain,
                                                          rows_in[:, two].rearrange("p r d -> p (r d)"), ALU.mult, ALU.add)
                last.then_inc(sums_free, 1)

            def gate(t, chunk):
                pos = CHUNKS.index(chunk) % 2
                n = chunk_no(t, chunk)
                dve.wait_ge(tanh_done, n)
                mine = act_sb[0:hidden_rows(chunk), pos]
                ups = gate_ps[pos][HALF:P] if is_tail(chunk) else up_ps[pos][:]
                nc.vector.scalar_tensor_tensor(mine, mine, 1.0, gate_ps[pos][0:hidden_rows(chunk)], ALU.add, ALU.mult).then_inc(gated_one, 1)
                dve.wait_ge(gated_one, n)
                nc.vector.tensor_tensor(mine, mine, ups, ALU.mult).then_inc(gated, 1)

            def running_max(t, h):
                wait_taken(dve, t, "W", f"z2T{h}")
                if h == 0 and t.on["M"]:
                    dve.wait_ge(combT_out, t.count("M", 16, 16))
                nc.vector.tensor_tensor_scan(flat(h, OMAX), decay_row[:, h].rearrange("p b s -> p (b s)"),
                                             kw[:, h].rearrange("p b s -> p (b s)"), NEG, ALU.add, ALU.max).then_inc(omax_set, 1)

            def exponents(t, h):
                dve.wait_ge(omax_set, t.count("W", KH, h + 1))
                nc.vector.scalar_tensor_tensor(seqs(h, A2, 1), seqs(h, OMAX, 0), decay_sb[:, h:h + 1], seqs(h, OMAX, 1),
                                               ALU.add, ALU.subtract).then_inc(a2arg_set, 1)
                nc.vector.scalar_tensor_tensor(flat(h, DELTA)[:, 0:TOK].rearrange("p (b s) -> p b s", b=NS), kw[:, h, :, 1:S1],
                                               bonus_sb[:, h:h + 1], seqs(h, OMAX, 0), ALU.add, ALU.subtract).then_inc(delta_set, 1)

            def clamps(t, h):
                dve.wait_ge(delta_set, t.count("W", KH, h + 1))
                nc.vector.tensor_scalar(flat(h, EA)[:, 0:TOK], flat(h, DELTA)[:, 0:TOK], 0.0, None, ALU.max).then_inc(clamp_set, 1)
                nc.vector.tensor_scalar(flat(h, EE)[:, 0:TOK], flat(h, DELTA)[:, 0:TOK], 0.0, None, ALU.min).then_inc(clamp_set, 1)

            def scans(t, h):
                dve.wait_ge(a2_set, t.count("W", KH, h + 1))
                dve.wait_ge(ev_set, t.count("W", KH, h + 1))
                nc.vector.tensor_tensor_scan(flat(h, EV), flat(h, A2), flat(h, EV), 0.0, ALU.mult, ALU.add).then_inc(scans_done, 1)
                nc.vector.tensor_tensor_scan(flat(h, E2), flat(h, A2), flat(h, E2), 0.0, ALU.mult, ALU.add).then_inc(scans_done, 1)

            def in_seqs(part):
                return part[:, 0:TOK].rearrange("p (b s) -> p b s", b=NS)

            def read_states(t, h):
                dve.wait_ge(ea_set, t.count("W", KH, h + 1))
                dve.wait_ge(scans_done, t.count("W", 2 * KH, 2 * h + 2))
                nc.vector.tensor_tensor(in_seqs(flat(h, DELTA)), in_seqs(flat(h, EA)), seqs(h, EV, 0), ALU.mult).then_inc(ap_set, 1)
                nc.vector.tensor_tensor(in_seqs(flat(h, EA)), in_seqs(flat(h, EA)), seqs(h, E2, 0), ALU.mult).then_inc(aq_set, 1)

            def add_now(t, h):
                dve.wait_ge(eev_set, t.count("W", KH, h + 1))
                dve.wait_ge(ap_set, t.count("W", KH, h + 1))
                nc.vector.tensor_tensor(in_seqs(flat(h, DELTA)), in_seqs(flat(h, DELTA)), seqs(h, A2, 1), ALU.add).then_inc(num_set, 1)
                dve.wait_ge(aq_set, t.count("W", KH, h + 1))
                nc.vector.tensor_tensor(flat(h, EE)[:, 0:TOK], flat(h, EA)[:, 0:TOK], flat(h, EE)[:, 0:TOK], ALU.add).then_inc(den_set, 1)

            def divide(t, h, piece):
                part = flat(h, EE)[:, piece * TOK // 2:(piece + 1) * TOK // 2]
                dve.wait_ge(den_set, t.count("W", KH, h + 1))
                nc.vector.reciprocal(part, part).then_inc(dinv_set, 1)

            def quotient(t, h):
                dve.wait_ge(dinv_set, t.count("W", 2 * KH, 2 * h + 2))
                dve.wait_ge(num_set, t.count("W", KH, h + 1))
                nc.vector.tensor_tensor(vw[:, h], flat(h, DELTA)[:, 0:TOK], flat(h, EE)[:, 0:TOK], ALU.mult).then_inc(yw_set, 1)

            def add_recurrence(t):
                rows_out = recurrence_out(t)[0]
                for pair in range(2):
                    bank = wait_full(dve, t, "W", f"yT{pair}")
                    two = slice(2 * pair, 2 * pair + 2)
                    last = nc.vector.scalar_tensor_tensor(rows_out[:, two].rearrange("p r d -> p (r d)"), bank[:], gains[:, 1:2],
                                                          x2[:, two].rearrange("p r d -> p (r d)"), ALU.mult, ALU.add)
                    last.then_inc(free_of("W", f"yT{pair}"), 1)

            def route(t):
                bank = wait_full(dve, t, "W", "route")
                both = bank[:, 0:2 * NT * E].rearrange("p (r a e) -> p r a e", r=NT, a=2)
                step = [0]

                def chained(ins):
                    step[0] += 1
                    ins.then_inc(route_chain, 1)
                    dve.wait_ge(route_chain, t.count("W", 9, step[0]))

                chained(nc.vector.tensor_copy(logits[:], both[:, :, 1]))
                chained(nc.vector.tensor_tensor(logits[:], logits[:], both[:, :, 0], ALU.add))
                chained(nc.vector.tensor_reduce(lmax[:], logits[:], AX.X, ALU.max))
                nc.vector.tensor_tensor(pexp[:], logits[:], lmax[:].unsqueeze(2).broadcast_to([P, NT, E]), ALU.subtract).then_inc(free_of("W", "route"), 1)
                dve.wait_ge(pexp_set, t.count("W", 1, 1))
                mine = pexp[:].unsqueeze(3).broadcast_to([P, NT, E, E])
                other = pexp[:].unsqueeze(2).broadcast_to([P, NT, E, E])
                nc.vector.tensor_reduce(psum_e[:], pexp[:], AX.X, ALU.add)
                nc.vector.tensor_tensor(beats[:], other, mine, ALU.is_gt)
                chained(nc.vector.tensor_tensor(ties[:], other, mine, ALU.is_equal))
                chained(nc.vector.tensor_tensor(ties[:], ties[:], before[:].unsqueeze(1).broadcast_to([P, NT, E, E]), ALU.mult))
                chained(nc.vector.tensor_tensor(beats[:], beats[:], ties[:], ALU.add))
                nc.vector.reciprocal(pinv[:], psum_e[:])
                chained(nc.vector.tensor_reduce(ranks[:], beats[:], AX.X, ALU.add))
                chained(nc.vector.tensor_scalar(ranks[:], ranks[:], 1.5, None, ALU.is_lt))
                chained(nc.vector.tensor_tensor(ranks[:], ranks[:], pexp[:], ALU.mult))
                if t.on["M"]:
                    wait_taken(dve, t, "M", "combT")
                nc.vector.tensor_tensor(combine[:], ranks[:], pinv[:].unsqueeze(2).broadcast_to([P, NT, E]), ALU.mult).then_inc(combine_set, 1)

            def turn(t):
                first, t1 = t.fixed and t.i == 0, Turn(1, NB, True)
                w, m = t.on["W"], t.on["M"]

                def m_gate(c):
                    if m:
                        gate(t, ("M", c))
                if w:
                    dve.wait_ge(sums_free, t.before(SUMS))
                    statistics(t, "W", 1, x2, bn_w, mv_w)
                m_gate(0)
                dve.wait_ge(x_in, t.count("A", 16, 16))
                statistics(t, "A", 1, xa, bn_a, mv_a)
                if first:
                    for name in ("wq", "wk", "wv"):
                        low(name)
                m_gate(1)
                m_gate(2)
                if w:
                    for h in range(KH):
                        running_max(t, h)
                    for h in range(KH):
                        exponents(t, h)
                m_gate(3)
                low_parts(t, "A", "z0T", za_h, za_l, za_h_set, 0, 2 * KH)
                if first:
                    absolute_sums()
                    decay_rows()
                if w:
                    for h in range(KH):
                        clamps(t, h)
                m_gate(4)
                if w:
                    scans(t, 0)
                    scans(t, 1)
                row_max(t)
                m_gate(5)
                row_scale(t)
                if first:
                    ternary_scales()
                    ternary_weights()
                if w:
                    read_states(t, 0)
                    add_now(t, 0)
                    divide(t, 0, 0)
                    divide(t, 0, 1)
                m_gate(6)
                if w:
                    quotient(t, 0)
                add_attention(t)
                wait_taken(dve, t, "A", "wo0", "wo1")
                statistics(t, "A", 2, xa, bn_a, mv_a)
                if first:
                    low("route")
                    low("down")
                m_gate(7)
                if w:
                    read_states(t, 1)
                    add_now(t, 1)
                m_gate(8)
                low_parts(t, "A", "z1T", za_h, za_l, za_h_set, KH, 2 * KH)
                if w:
                    divide(t, 1, 0)
                m_gate(9)
                if w:
                    divide(t, 1, 1)
                    quotient(t, 1)
                gate(t, ("A", 0))
                if w:
                    add_recurrence(t)
                if m:
                    add_sums(t, "M", gain_m[:, 0:1], x3, out_row)
                gate(t, ("A", 1))
                if first:
                    low("gate")
                    gate(t, ("A", 2))
                    dve.wait_ge(x_in, t1.count("A", 16, 16))
                    statistics(t1, "A", 1, attention_rows(t1), bn_a, mv_a)
                if w:
                    wait_taken(dve, t, "W", "yT0", "yT1")
                    statistics(t, "W", 2, x2, bn_w, mv_w)
                for c in range(3 if first else 2, HC - 1):
                    gate(t, ("A", c))
                if w:
                    low_parts(t, "W", "z3T", zm_h, zm_l, zm_h_set, 0, KH)
                gate(t, ("A", HC - 1))
                if first:
                    low_parts(t1, "A", "z0T", za_h, za_l, za_h_set, 0, 2 * KH)
                if w:
                    route(t)
                add_sums(t, "A", gain_f[:, 0:1], xa, x2)

            def second(t):
                rows = attention_rows(t)
                dve.wait_ge(sums_free, t.before(SUMS))
                statistics(t, "W", 1, x2, bn_w, mv_w)
                low("up")
                scan_slots()
                dve.wait_ge(scan_set, 1)
                for h in range(KH):
                    running_max(t, h)
                exponents(t, 0)
                row_max(t)
                exponents(t, 1)
                for h in range(KH):
                    clamps(t, h)
                row_scale(t)
                for h in range(KH):
                    scans(t, h)
                read_states(t, 0)
                add_now(t, 0)
                add_attention(t)
                wait_taken(dve, t, "A", "wo0", "wo1")
                statistics(t, "A", 2, rows, bn_a, mv_a)
                divide(t, 0, 0)
                divide(t, 0, 1)
                read_states(t, 1)
                low_parts(t, "A", "z1T", za_h, za_l, za_h_set, KH, 2 * KH)
                quotient(t, 0)
                add_now(t, 1)
                divide(t, 1, 0)
                gate(t, ("A", 0))
                divide(t, 1, 1)
                quotient(t, 1)
                gate(t, ("A", 1))
                gate(t, ("A", 2))
                add_recurrence(t)
                wait_taken(dve, t, "W", "yT0", "yT1")
                statistics(t, "W", 2, x2, bn_w, mv_w)
                for c in range(3, HC - 1):
                    gate(t, ("A", c))
                low_parts(t, "W", "z3T", zm_h, zm_l, zm_h_set, 0, KH)
                gate(t, ("A", HC - 1))
                route(t)
                add_sums(t, "A", gain_f[:, 0:1], rows, x2)

            def closing(t):
                def m_gate(c):
                    gate(t, ("M", c))
                rows, z_h, z_l = recurrence_out(t)
                dve.wait_ge(sums_free, t.before(SUMS))
                statistics(t, "W", 1, x2, bn_w, mv_w)
                m_gate(0)
                m_gate(1)
                m_gate(2)
                for h in range(KH):
                    running_max(t, h)
                for h in range(KH):
                    exponents(t, h)
                m_gate(3)
                for h in range(KH):
                    clamps(t, h)
                m_gate(4)
                for h in range(KH):
                    scans(t, h)
                for h in range(KH):
                    read_states(t, h)
                m_gate(5)
                add_now(t, 0)
                divide(t, 0, 0)
                divide(t, 0, 1)
                m_gate(6)
                quotient(t, 0)
                add_now(t, 1)
                divide(t, 1, 0)
                divide(t, 1, 1)
                quotient(t, 1)
                m_gate(7)
                add_recurrence(t)
                wait_taken(dve, t, "W", "yT0", "yT1")
                statistics(t, "W", 2, rows, bn_w, mv_w)
                m_gate(8)
                m_gate(9)
                low_parts(t, "W", "z3T", z_h, z_l, zm_h_set, 0, KH)
                route(t)
                add_sums(t, "M", gain_m[:, 0:1], x3, out_row)

            def last(t):
                for c in range(MC):
                    gate(t, ("M", c))
                add_sums(t, "M", gain_m[:, 0:1], experts_in(t)[0], out_row)

            turns(dve, turn, second, closing, last)


def kernel(**inputs):
    import numpy as _np
    import concourse.bacc as _bacc
    from concourse import mybir as _mybir
    from concourse.bass_utils import run_bass_kernel_spmd as _run

    nc = _bacc.Bacc("TRN2", target_bir_lowering=False, num_devices=1)
    names = ["x", "ctx_2048", "g_xattn", "g_ffn", "L0_xattn_wq", "L0_xattn_wk", "L0_xattn_wv", "L0_xattn_wo", "L0_ffn_w1",
             "L0_ffn_w3", "L0_ffn_w2", "L1_xattn_w", "L1_xattn_u", "L1_ffn_router_w", "L1_ffn_shared_gate",
             "L1_ffn_shared_up", "L1_ffn_shared_down", "L1_ffn_w_gate", "L1_ffn_w_up", "L1_ffn_w_down"]
    turned = {"L0_xattn_wq", "L0_xattn_wk", "L0_xattn_wv", "L0_xattn_wo", "L0_ffn_w1", "L0_ffn_w3", "L0_ffn_w2"}
    arrays, args = {}, []
    for name in names:
        a = _np.asarray(inputs[name])
        a = _np.ascontiguousarray(a.T if name in turned else a)
        arrays[f"in_{name}"] = a
        args.append(nc.dram_tensor(f"in_{name}", a.shape, _mybir.dt.from_np(a.dtype), kind="ExternalInput").ap())
    shape = tuple(inputs["x"].shape)
    args.append(nc.dram_tensor("out_x", shape, _mybir.dt.float32, kind="ExternalOutput").ap())
    args.append(nc.dram_tensor("combine_rows", (8, 512), _mybir.dt.float32, kind="Internal").ap())
    build(nc, *args)
    return _run(nc, [arrays], core_ids=[0]).results[0]["out_x"]
```
